# Optimizing a Trainium2 kernel written in Bass

```python
import numpy as np
import jax
import jax.numpy as jnp

def _softmax(x, axis=-1):
    return jax.nn.softmax(x, axis=axis)

def _gelu(x):
    return jax.nn.gelu(x, approximate=True)

def _silu(x):
    return jax.nn.silu(x)

def _sigmoid(x):
    return jax.nn.sigmoid(x)

def _layernorm(x, axis=-1, eps=1e-05):
    m = jnp.mean(x, axis=axis, keepdims=True)
    v = jnp.var(x, axis=axis, keepdims=True)
    return (x - m) / jnp.sqrt(v + eps)

def _scatter_add(tgt, idx, src, axis=0):
    return tgt.at[idx].add(src)

def _segment_sum(src, seg, n):
    return jax.ops.segment_sum(src, seg, n)
kernel_name = 'mk_decoder_preln_d1_seqx_r2_9a0aab'

def setup_inputs(seed: int=0):
    np.random.seed(seed)
    _w = jnp.asarray

    def _rec_inputs():
        import jax
        import jax.numpy as jnp
        _rk = jax.random.key(seed)
        x = -0.0002928 + 1 * jax.random.normal(jax.random.fold_in(_rk, 1), (8, 512, 512), jnp.float32)
        _lenS = 512 - jax.random.randint(jax.random.fold_in(_rk, 7), (8,), 0, max(1, 512 // 4) + 1, jnp.int32)
        _lenS2 = 77 - jax.random.randint(jax.random.fold_in(_rk, 8), (8,), 0, max(1, 77 // 4) + 1, jnp.int32)
        _ctx_1024P = jax.random.normal(jax.random.fold_in(_rk, 11), (8, 16, 512), jnp.float32)
        _ctx_1024c = jax.random.dirichlet(jax.random.fold_in(_rk, 511), 0.3 * jnp.ones((16,), jnp.float32), (8, 77))
        _ctx_1024t = jnp.einsum('bsk,bkd->bsd', _ctx_1024c, _ctx_1024P)
        _ctx_1024t = _ctx_1024t * jax.lax.rsqrt(jnp.mean(jnp.square(_ctx_1024t)) + 1e-12) * 0.953939
        ctx_1024 = -1.39393e-06 + 0.999914 * (_ctx_1024t + 0.3 * jax.random.normal(jax.random.fold_in(_rk, 611), (8, 77, 512), jnp.float32))
        return (x, ctx_1024)
    x, ctx_1024 = _rec_inputs()

    def _L0_attn_setup():
        import jax, jax.numpy as jnp
        import numpy as np
        import math
        N_HEAD = 16
        LATENT_RANK = 64
        key = jax.random.key(seed)
        ks = jax.random.split(key, 8)
        B, T, C, H, R = (4, 1024, 512, N_HEAD, LATENT_RANK)
        std = 0.02
        return {'hidden_states': jax.random.normal(ks[0], (B, T, C), jnp.float32), 'basis_w': jax.random.normal(ks[1], (R, C), jnp.float32) * std, 'core': jax.random.normal(ks[2], (R, R), jnp.float32) * std, 'head_residual': jax.random.normal(ks[3], (H, R, R), jnp.float32) * (std / 10.0), 'v_w': jax.random.normal(ks[4], (C, C), jnp.float32) * std, 'v_b': jnp.zeros((C,), jnp.float32), 'o_w': jax.random.normal(ks[5], (C, C), jnp.float32) * std, 'o_b': jnp.zeros((C,), jnp.float32)}
    _L0_attn_all = _L0_attn_setup()
    _L0_attn_in = {k: v for k, v in _L0_attn_all.items() if k in ('basis_w', 'core', 'head_residual', 'v_w', 'v_b', 'o_w', 'o_b')}
    del _L0_attn_all

    def _L0_xattn_setup():
        import jax, jax.numpy as jnp
        import numpy as np
        B, T, C = (2, 1024, 512)
        H = 16
        D = C // H

        def _split(x):
            b, t, c = x.shape
            return x.reshape(b, t, H, D).transpose(0, 2, 1, 3)
        key = jax.random.key(seed)
        ks = jax.random.split(key, 11)
        s = 0.02
        return {'q': jax.random.normal(ks[0], (B, T, C), jnp.float32), 'k': jax.random.normal(ks[1], (B, T, C), jnp.float32), 'v': jax.random.normal(ks[2], (B, T, C), jnp.float32), 'Wq': jax.random.normal(ks[3], (C, C), jnp.float32) * s, 'bq': jnp.zeros((C,), jnp.float32), 'Wk': jax.random.normal(ks[4], (C, C), jnp.float32) * s, 'bk': jnp.zeros((C,), jnp.float32), 'Wv': jax.random.normal(ks[5], (C, C), jnp.float32) * s, 'bv': jnp.zeros((C,), jnp.float32), 'Wo': jax.random.normal(ks[6], (C, C), jnp.float32) * s, 'bo': jnp.zeros((C,), jnp.float32)}
    _L0_xattn_all = _L0_xattn_setup()
    _L0_xattn_in = {k: v for k, v in _L0_xattn_all.items() if k in ('Wq', 'bq', 'Wk', 'bk', 'Wv', 'bv', 'Wo', 'bo')}
    del _L0_xattn_all

    def _L0_ffn_setup():
        import jax, jax.numpy as jnp
        import numpy as np
        D_MODEL = 512
        H_SHARED = 1024
        H_ROUTED = 512
        N_EXPERTS = 8
        TOP_K = 2
        key = jax.random.key(seed)
        ks = jax.random.split(key, 8)
        B, T = (2, 1024)
        sc_d = 1.0 / np.sqrt(D_MODEL)
        sc_hs = 1.0 / np.sqrt(H_SHARED)
        sc_hr = 1.0 / np.sqrt(H_ROUTED)
        return {'x': jax.random.normal(ks[0], (B, T, D_MODEL), dtype=jnp.float32), 'router_w': jax.random.normal(ks[1], (N_EXPERTS, D_MODEL), dtype=jnp.float32) * sc_d, 'router_bias': jnp.zeros((N_EXPERTS,), dtype=jnp.float32), 'sw1': jax.random.normal(ks[2], (D_MODEL, H_SHARED), dtype=jnp.float32) * sc_d, 'sw3': jax.random.normal(ks[3], (D_MODEL, H_SHARED), dtype=jnp.float32) * sc_d, 'sw2': jax.random.normal(ks[4], (H_SHARED, D_MODEL), dtype=jnp.float32) * sc_hs, 'ew1': jax.random.normal(ks[5], (N_EXPERTS, D_MODEL, H_ROUTED), dtype=jnp.float32) * sc_d, 'ew2': jax.random.normal(ks[6], (N_EXPERTS, H_ROUTED, D_MODEL), dtype=jnp.float32) * sc_hr}
    _L0_ffn_all = _L0_ffn_setup()
    _L0_ffn_in = {k: v for k, v in _L0_ffn_all.items() if k in ('router_w', 'router_bias', 'sw1', 'sw3', 'sw2', 'ew1', 'ew2')}
    del _L0_ffn_all
    return {'x': x, 'ctx_1024': ctx_1024, 'L0_attn_basis_w': _L0_attn_in['basis_w'], 'L0_attn_core': _L0_attn_in['core'], 'L0_attn_head_residual': _L0_attn_in['head_residual'], 'L0_attn_v_w': _L0_attn_in['v_w'], 'L0_attn_v_b': _L0_attn_in['v_b'], 'L0_attn_o_w': _L0_attn_in['o_w'], 'L0_attn_o_b': _L0_attn_in['o_b'], 'L0_xattn_Wq': _L0_xattn_in['Wq'], 'L0_xattn_bq': _L0_xattn_in['bq'], 'L0_xattn_Wk': _L0_xattn_in['Wk'], 'L0_xattn_bk': _L0_xattn_in['bk'], 'L0_xattn_Wv': _L0_xattn_in['Wv'], 'L0_xattn_bv': _L0_xattn_in['bv'], 'L0_xattn_Wo': _L0_xattn_in['Wo'], 'L0_xattn_bo': _L0_xattn_in['bo'], 'L0_ffn_router_w': _L0_ffn_in['router_w'], 'L0_ffn_router_bias': _L0_ffn_in['router_bias'], 'L0_ffn_sw1': _L0_ffn_in['sw1'], 'L0_ffn_sw3': _L0_ffn_in['sw3'], 'L0_ffn_sw2': _L0_ffn_in['sw2'], 'L0_ffn_ew1': _L0_ffn_in['ew1'], 'L0_ffn_ew2': _L0_ffn_in['ew2']}

def reference(x, ctx_1024, L0_attn_basis_w, L0_attn_core, L0_attn_head_residual, L0_attn_v_w, L0_attn_v_b, L0_attn_o_w, L0_attn_o_b, L0_xattn_Wq, L0_xattn_bq, L0_xattn_Wk, L0_xattn_bk, L0_xattn_Wv, L0_xattn_bv, L0_xattn_Wo, L0_xattn_bo, L0_ffn_router_w, L0_ffn_router_bias, L0_ffn_sw1, L0_ffn_sw3, L0_ffn_sw2, L0_ffn_ew1, L0_ffn_ew2):
    import jax
    import jax.numpy as jnp

    def _L0_attn_ref(hidden_states, basis_w, core, head_residual, v_w, v_b, o_w, o_b):
        import jax, jax.numpy as jnp
        import numpy as np
        import math
        N_HEAD = 16
        LATENT_RANK = 64
        B, T, C = hidden_states.shape
        H = N_HEAD
        R = LATENT_RANK
        head_dim = C // H
        latent = jnp.einsum('btc,rc->btr', hidden_states, basis_w)
        core_sym = 0.5 * (core + core.T)
        centered = head_residual - head_residual.mean(axis=0, keepdims=True)
        head_mats = core_sym[None] / float(H) + centered
        lt = jnp.einsum('btr,hrs->bhts', latent, head_mats)
        att = jnp.einsum('bhts,bus->bhtu', lt, latent) * (1.0 / math.sqrt(R))
        causal = jnp.tril(jnp.ones((T, T), jnp.bool_))
        att = jnp.where(causal[None, None], att, jnp.float32(-jnp.inf))
        att = jax.nn.softmax(att, axis=-1)
        v = (hidden_states @ v_w.T + v_b).reshape(B, T, H, head_dim).transpose(0, 2, 1, 3)
        y = att @ v
        y = y.transpose(0, 2, 1, 3).reshape(B, T, C)
        y = y @ o_w.T + o_b
        return y

    def _L0_xattn_ref(q, k, v, Wq, bq, Wk, bk, Wv, bv, Wo, bo):
        import jax, jax.numpy as jnp
        import numpy as np
        B, T, C = (2, 1024, 512)
        H = 16
        D = C // H

        def _split(x):
            b, t, c = x.shape
            return x.reshape(b, t, H, D).transpose(0, 2, 1, 3)
        scale = D ** (-0.5)
        Q = _split(q @ Wq.T + bq)
        K = _split(k @ Wk.T + bk)
        V = _split(v @ Wv.T + bv)
        scores = jnp.einsum('bhqd,bhkd->bhqk', Q, K) * scale
        attn = jax.nn.softmax(scores, axis=-1)
        out = jnp.einsum('bhqk,bhkd->bhqd', attn, V)
        out = out.transpose(0, 2, 1, 3).reshape(q.shape[0], q.shape[1], H * D)
        return out @ Wo.T + bo

    def _L0_ffn_ref(x, router_w, router_bias, sw1, sw3, sw2, ew1, ew2):
        import jax, jax.numpy as jnp
        import numpy as np
        D_MODEL = 512
        H_SHARED = 1024
        H_ROUTED = 512
        N_EXPERTS = 8
        TOP_K = 2
        B, T, C = x.shape
        xf = x.reshape(-1, C)
        shared_out = jax.nn.silu(xf @ sw1) * (xf @ sw3) @ sw2
        s = jax.nn.sigmoid((xf @ router_w.T).astype(jnp.float32))
        sel_scores = s + router_bias.astype(jnp.float32)
        _, topk_idx = jax.lax.top_k(sel_scores, TOP_K)
        s_sel = jnp.take_along_axis(s, topk_idx, axis=1)
        denom = s_sel.sum(axis=1, keepdims=True)
        gates = jnp.where(denom > 1e-09, s_sel / (denom + 1e-09), 1.0 / TOP_K).astype(x.dtype)
        one_hot = jax.nn.one_hot(topk_idx, N_EXPERTS, dtype=x.dtype)
        comb = jnp.einsum('nke,nk->ne', one_hot, gates)
        h = jax.nn.gelu(jnp.einsum('nd,edh->neh', xf, ew1), approximate=False)
        y = jnp.einsum('neh,ehd->ned', h, ew2)
        routed_out = jnp.einsum('ned,ne->nd', y, comb)
        return (shared_out + routed_out).reshape(B, T, C)
    x = x + _L0_attn_ref(_layernorm(x, axis=-1), L0_attn_basis_w, L0_attn_core, L0_attn_head_residual, L0_attn_v_w, L0_attn_v_b, L0_attn_o_w, L0_attn_o_b)
    x = x + _L0_xattn_ref(_layernorm(x, axis=-1), ctx_1024, ctx_1024, L0_xattn_Wq, L0_xattn_bq, L0_xattn_Wk, L0_xattn_bk, L0_xattn_Wv, L0_xattn_bv, L0_xattn_Wo, L0_xattn_bo)
    x = x + _L0_ffn_ref(_layernorm(x, axis=-1), L0_ffn_router_w, L0_ffn_router_bias, L0_ffn_sw1, L0_ffn_sw3, L0_ffn_sw2, L0_ffn_ew1, L0_ffn_ew2)
    return x

_drawn_inputs = setup_inputs


def setup_inputs(seed=0):
    import zlib

    import numpy as np

    out = dict(_drawn_inputs(seed))
    spreads = {'L0_attn_v_b': (0.0, 0.1),
     'L0_attn_o_b': (0.0, 0.1),
     'L0_xattn_bq': (0.0, 0.466),
     'L0_xattn_bk': (0.0, 0.8),
     'L0_xattn_bv': (0.0, 0.1),
     'L0_xattn_bo': (0.0, 0.1),
     'L0_ffn_router_bias': (0.0, 0.1)}
    factors = {'L0_attn_basis_w': 8.0, 'L0_attn_core': 8.0, 'L0_attn_head_residual': 8.0}
    for name, (base, spread) in spreads.items():
        noise = np.random.default_rng([zlib.crc32(name.encode()), seed]).standard_normal(out[name].shape)
        drawn = base * np.exp(spread * noise) if base else spread * noise
        out[name] = jnp.asarray(drawn.astype(out[name].dtype))
    for name, factor in factors.items():
        out[name] = (out[name] * factor).astype(out[name].dtype)
    return out
```

```python
from contextlib import ExitStack

import concourse.bass as bass
from concourse import mybir

ALU = mybir.AluOpType
ACT = mybir.ActivationFunctionType
F32 = mybir.dt.float32
F16 = mybir.dt.float16
AX_X = mybir.AxisListType.X

P = 128
B, T, C = 8, 512, 512
TT = T // P
KT = C // P
H, R, HD = 16, 64, 32
S = 77
HG = P // HD
NG = H // HG
VW = HD + 1
WSCALE = 32.0
MSCALE = 64.0
BIG = 60000.0
EPS = 1e-5
XSCALE = float(HD) ** -0.5 / (WSCALE * WSCALE)
PAIRS = H // 2
STEPS = 2 * TT


def wait_apart(eng, s, value, passed):
    eng.wait_ge(s, value)
    eng.sem_inc(passed, 1)


def build_attention(nc, sem, x, ctx_in, weights, x2_dram):
    basisT, core, coreT, head_res, wvT, bv, woT, bo, xwqT, xbq, xwkT, xbk, xwvT, xbv, xwoT, xbo = weights
    with ExitStack() as keep:
        def sb(name, shape, dt):
            return keep.enter_context(nc.sbuf_tensor(name, shape, dt))

        w_names = ["wv", "wo", "xwq", "xwk", "xwv", "xwo"]
        W = {n: sb(n, [P, 2, KT, C], F16) for n in w_names}
        w_basis = sb("w_basis", [P, 2, KT, P], F16)
        head_mat = sb("head_mat", [P, H, P], F16)
        ident = sb("ident", [P, P], F32)
        big_ident = sb("big_ident", [P, P], F16)
        causal = sb("causal", [P, P], F16)
        vb_row = sb("vb_row", [P, C], F32)
        ob_row = sb("ob_row", [P, C], F32)
        xvb_row = sb("xvb_row", [P, C], F32)
        xob_row = sb("xob_row", [P, C], F32)
        q_bias = sb("q_bias", [P, NG], F32)
        k_bias = sb("k_bias", [P, NG], F32)
        neg_half = sb("neg_half", [P, TT], F32)

        with ExitStack() as prep:
            def tmp(name, shape, dt):
                return prep.enter_context(nc.sbuf_tensor(name, shape, dt))

            raw = {n: tmp("raw_" + n, [P, KT, C], F32) for n in w_names}
            raw_basis = tmp("raw_basis", [P, KT, R], F32)
            raw_heads = tmp("raw_heads", [P, H, R], F32)
            raw_core = tmp("raw_core", [P, 2, R], F32)
            head_sum = tmp("head_sum", [P, R], F32)
            core_sum = tmp("core_sum", [P, R], F32)
            shared = tmp("shared", [P, R], F32)
            w_loaded = {n: sem("loaded_" + n) for n in w_names}
            small_loaded, bias_loaded = sem("small_loaded"), sem("bias_loaded")
            w_high, w_low = sem("w_high"), sem("w_low")
            pool_made, head_step, head_high = sem("pool_made"), sem("head_step"), sem("head_high")
            bias_scaled = sem("bias_scaled")
            with nc.Block() as block:
                @block.sync
                def _(sp):
                    for half in (0, R):
                        sp.dma_start(raw_heads[half:half + R], head_res.rearrange("h r s -> r h s")).then_inc(small_loaded, 16)
                        sp.dma_start(raw_core[half:half + R, 0, :], core).then_inc(small_loaded, 16)
                        sp.dma_start(raw_core[half:half + R, 1, :], coreT).then_inc(small_loaded, 16)
                    sp.dma_start(raw_basis[:], basisT.rearrange("(a p) n -> p a n", p=P)).then_inc(small_loaded, 16)
                    for n, src in zip(w_names, (wvT, woT, xwqT, xwkT, xwvT, xwoT)):
                        sp.dma_start(raw[n][:], src.rearrange("(a p) n -> p a n", p=P)).then_inc(w_loaded[n], 16)
                    for dst, src in ((vb_row, bv), (ob_row, bo), (xvb_row, xbv), (xob_row, xbo)):
                        sp.dma_start(dst[:], src.rearrange("(a n) -> a n", a=1).broadcast_to([P, C])).then_inc(bias_loaded, 16)
                    for dst, src in ((q_bias, xbq), (k_bias, xbk)):
                        sp.dma_start(dst[:], src).then_inc(bias_loaded, 16)

                @block.gpsimd
                def _(pool):
                    nc.gpsimd.memset(neg_half[:], -0.5).then_inc(pool_made, 1)
                    nc.gpsimd.memset(ident[:], 0.0).then_inc(pool_made, 1)
                    nc.gpsimd.memset(big_ident[:], 0.0).then_inc(pool_made, 1)
                    nc.gpsimd.memset(causal[:], 0.0).then_inc(pool_made, 1)
                    pool.wait_ge(pool_made, 4)
                    for t, value in ((ident, 1.0), (big_ident, BIG)):
                        nc.gpsimd.affine_select(out=t[:], in_=t[:], compare_op=ALU.not_equal, fill=value, base=0,
                                                pattern=[[-1, P]], channel_multiplier=1).then_inc(pool_made, 1)
                    nc.gpsimd.affine_select(out=causal[:], in_=causal[:], compare_op=ALU.is_ge, fill=-BIG, base=0,
                                            pattern=[[-1, P]], channel_multiplier=1).then_inc(pool_made, 1)
                    pool.wait_ge(bias_loaded, 16 * 6)
                    for t in (q_bias, k_bias):
                        nc.gpsimd.tensor_scalar(t[:], t[:], WSCALE, None, ALU.mult).then_inc(bias_scaled, 1)

                @block.scalar
                def _(act):
                    act.wait_ge(small_loaded, 16 * 7)
                    for half in range(2):
                        nc.scalar.activation(w_basis[:, 0, :, half * R:half * R + R], raw_basis[:], ACT.Copy,
                                             scale=WSCALE).then_inc(w_high, 1)
                    act.wait_ge(head_step, 6)
                    nc.scalar.activation(head_mat[:, :, 0:R], raw_heads[:], ACT.Copy, scale=MSCALE).then_inc(head_high, 1)
                    for n in w_names:
                        act.wait_ge(w_loaded[n], 16)
                        nc.scalar.activation(W[n][:, 0], raw[n][:], ACT.Copy, scale=WSCALE).then_inc(w_high, 1)

                @block.vector
                def _(dve):
                    dve.wait_ge(small_loaded, 16 * 7)
                    nc.vector.tensor_reduce(head_sum[:], raw_heads[:].rearrange("p h s -> p s h"), AX_X,
                                            ALU.add).then_inc(head_step, 1)
                    nc.vector.tensor_tensor(core_sum[:], raw_core[:, 0], raw_core[:, 1], ALU.add).then_inc(head_step, 1)
                    dve.wait_ge(head_step, 2)
                    nc.vector.tensor_scalar(core_sum[:], core_sum[:], 0.5 / H, None, ALU.mult).then_inc(head_step, 1)
                    nc.vector.tensor_scalar(head_sum[:], head_sum[:], 1.0 / H, None, ALU.mult).then_inc(head_step, 1)
                    dve.wait_ge(head_step, 4)
                    nc.vector.tensor_tensor(shared[:], core_sum[:], head_sum[:], ALU.subtract).then_inc(head_step, 1)
                    dve.wait_ge(head_step, 5)
                    nc.vector.tensor_tensor(raw_heads[:], raw_heads[:],
                                            shared[:].unsqueeze(1).broadcast_to([P, H, R]), ALU.add).then_inc(head_step, 1)
                    for half in range(2):
                        dve.wait_ge(w_high, half + 1)
                        cols = slice(half * R, half * R + R)
                        nc.vector.scalar_tensor_tensor(w_basis[:, 1, :, cols], raw_basis[:], WSCALE,
                                                       w_basis[:, 0, :, cols], ALU.mult, ALU.subtract).then_inc(w_low, 1)
                    dve.wait_ge(head_step, 6)
                    dve.wait_ge(head_high, 1)
                    nc.vector.scalar_tensor_tensor(head_mat[R:P, :, 0:R], raw_heads[R:P], MSCALE,
                                                   head_mat[R:P, :, 0:R], ALU.mult, ALU.subtract).then_inc(head_step, 1)
                    dve.wait_ge(head_step, 7)
                    nc.vector.tensor_copy(head_mat[:, :, R:P], head_mat[:, :, 0:R]).then_inc(head_step, 1)
                    for k, n in enumerate(w_names):
                        dve.wait_ge(w_high, 3 + k)
                        nc.vector.scalar_tensor_tensor(W[n][:, 1], raw[n][:], WSCALE, W[n][:, 0],
                                                       ALU.mult, ALU.subtract).then_inc(w_low, 1)

        x_in = sb("x_in", [P, TT, C], F32)
        x_res = sb("x_res", [P, TT, C], F32)
        xn = sb("xn", [P, TT, C], F32)
        ctx_sb = sb("ctx_sb", [S, C], F32)
        stats = sb("stats", [P, TT, 6], F32)
        moments = sb("moments", [P, TT, 2], F32)
        rstd = sb("rstd", [P, TT], F32)
        shift = sb("shift", [P, TT], F32)
        xT = sb("xT", [P, 2, KT, T], F16)
        latent = sb("latent", [P, 2, T], F16)
        values = sb("values", [P, 2, TT, H, VW], F16)
        left = sb("left", [P, 2, T], F16)
        neg_max = sb("neg_max", [P, STEPS], F32)
        probs = sb("probs", [P, TT, T], F32)
        probsT = sb("probsT", [P, 4, 2, T], F16)
        sums = sb("sums", [P, 2, TT], F32)
        y = sb("y", [P, TT, C], F32)
        yT = sb("yT", [P, 2, KT, T], F16)
        qT = sb("qT", [P, 2, NG, T], F16)
        ctxT = sb("ctxT", [P, 2, KT, S], F16)
        k_sum = sb("k_sum", [P, NG, S], F32)
        k_diag = sb("k_diag", [P, 2, NG, HG * S], F16)
        c_values = sb("c_values", [S, 2, H, VW], F16)
        c_max = sb("c_max", [P, 2, H], F32)
        c_probs = sb("c_probs", [P, 2, H, S], F32)
        c_probsT = sb("c_probsT", [S, 2, 2, HG * P], F16)
        c_sums = sb("c_sums", [P, 2, H], F32)
        x2_out = sb("x2_out", [P, TT, C], F32)
        bank = [keep.enter_context(nc.psum_tensor(f"bank{i}", [P, 512], F32)) for i in range(8)]

        x_loaded, ctx_loaded, x_taken = sem("x_loaded"), sem("ctx_loaded"), sem("x_taken")
        ln_stats, ln_mom, ln_rstd, ln_xn = sem("ln_stats"), sem("ln_mom"), sem("ln_rstd"), sem("ln_xn")
        ln_pool = sem("ln_pool")
        dve_waits, pool_waits = sem("dve_waits"), sem("pool_waits")
        ones_set = sem("ones_set")

        def split_sems(name):
            return sem(name + "_ready"), sem(name + "_high"), sem(name + "_low")

        xT_ready, xT_high, xT_low = split_sems("xT")
        lat_ready, lat_high, lat_low = split_sems("lat")
        v_ready, v_high, v_low = split_sems("v")
        left_ready, left_high, left_low = split_sems("left")
        pT_ready, pT_high, pT_low = split_sems("pT")
        yT_ready, yT_high, yT_low = split_sems("yT")
        ctxT_ready, ctxT_high, ctxT_low = split_sems("ctxT")
        k_ready, k_high, k_low = split_sems("k")
        cv_ready, cv_high, cv_low = split_sems("cv")
        q_ready, q_high, q_low = split_sems("q")
        cpT_ready, cpT_high, cpT_low = split_sems("cpT")
        scores_ready, max_done, exp_done = sem("scores_ready"), sem("max_done"), sem("exp_done")
        y_ready, sums_done, y_normed, y_biased = sem("y_ready"), sem("sums_done"), sem("y_normed"), sem("y_biased")
        o_ready, x1_done, xb_done = sem("o_ready"), sem("x1_done"), sem("xb_done")
        k_added = sem("k_added")
        cs_ready, c_max_done, c_sub_done, c_exp_done = sem("cs_ready"), sem("c_max_done"), sem("c_sub_done"), sem("c_exp_done")
        cy_ready, c_sums_done, cy_normed, cy_biased = sem("cy_ready"), sem("c_sums_done"), sem("cy_normed"), sem("cy_biased")
        xo_ready, x2_done, x2_stored = sem("xo_ready"), sem("x2_done"), sem("x2_stored")

        x_v = x.rearrange("b (a p) c -> b p a c", p=P)
        x2_v = x2_dram.rearrange("(b a p) c -> b p a c", p=P, a=TT)

        def copy_high(out, in_, scale=1.0):
            return nc.scalar.activation(out, in_, ACT.Copy, scale=scale)

        def low(out, in_, scale, high):
            return nc.vector.scalar_tensor_tensor(out, in_, scale, high, ALU.mult, ALU.subtract)

        with nc.Block() as block:
            @block.sync
            def _(sp):
                sp.sem_inc(x2_stored, 16)
                sp.dma_start(x_in[:], x_v[0]).then_inc(x_loaded, 16)
                sp.dma_start(ctx_sb[:], ctx_in[0]).then_inc(ctx_loaded, 16)

                def store(b):
                    sp.wait_ge(x2_done, b * TT + TT + 1)
                    sp.dma_start(x2_v[b] if isinstance(b, int) else x2_v[bass.ds(b, 1)].rearrange("o p a c -> (o p) a c"),
                                 x2_out[:]).then_inc(x2_stored, 16)

                with sp.Fori(1, B) as b:
                    sp.wait_ge(x_taken, b * TT)
                    sp.wait_ge(ln_xn, b * 2 * TT - TT)
                    sp.dma_start(x_in[:], x_v[bass.ds(b, 1)].rearrange("o p a c -> (o p) a c")).then_inc(x_loaded, 16)
                    sp.wait_ge(ctxT_ready, b)
                    sp.dma_start(ctx_sb[:], ctx_in[bass.ds(b, 1)].rearrange("o s c -> (o s) c")).then_inc(ctx_loaded, 16)
                    store(b - 1)
                store(B - 1)
                sp.wait_ge(x2_stored, 16 * B + 16)

            @block.gpsimd
            def _(pool):
                for t, value in ((values, WSCALE), (c_values, WSCALE)):
                    nc.gpsimd.memset(t[:], 0.0).then_inc(ones_set, 1)
                nc.gpsimd.memset(k_diag[:], 0.0).then_inc(ones_set, 1)
                pool.wait_ge(ones_set, 3)
                nc.gpsimd.memset(values[:, 0, :, :, HD:VW], WSCALE).then_inc(ones_set, 1)
                nc.gpsimd.memset(c_values[:, 0, :, HD:VW], WSCALE).then_inc(ones_set, 1)

                def layer_norm_scale(n):
                    wait_apart(pool, ln_mom, n * TT + TT, pool_waits)
                    nc.gpsimd.tensor_scalar(rstd[:], moments[:, :, 1], 1.0, EPS, ALU.mult, ALU.add).then_inc(ln_pool, 1)
                    pool.wait_ge(ln_pool, n * 3 + 1)
                    nc.gpsimd.tensor_tensor(rstd[:], rstd[:], neg_half[:], ALU.pow).then_inc(ln_pool, 1)
                    pool.wait_ge(ln_pool, n * 3 + 2)
                    nc.gpsimd.tensor_tensor(shift[:], moments[:, :, 0], rstd[:], ALU.mult).then_inc(ln_pool, 1)
                    wait_apart(pool, ln_pool, n * 3 + 3, pool_waits)
                    nc.gpsimd.tensor_scalar(shift[:], shift[:], -1.0, 0.0, ALU.mult, ALU.add).then_inc(ln_rstd, 1)

                with pool.Fori(0, B) as b:
                    layer_norm_scale(b * 2)
                    pool.wait_ge(x2_done, b * TT + 1)
                    for t in range(TT):
                        nc.gpsimd.tensor_tensor(x_res[:, t], x_in[:, t], ob_row[:], ALU.add).then_inc(x_taken, 1)
                    pool.wait_ge(y_normed, b * H + H)
                    for t in range(TT):
                        nc.gpsimd.tensor_tensor(y[:, t], y[:, t], vb_row[:], ALU.add).then_inc(y_biased, 1)
                    layer_norm_scale(b * 2 + 1)
                    pool.wait_ge(ln_xn, b * 2 * TT + 2 * TT)
                    for t in range(TT):
                        nc.gpsimd.tensor_tensor(x_res[:, t], x_res[:, t], xob_row[:], ALU.add).then_inc(xb_done, 1)
                    for t in range(TT):
                        pool.wait_ge(cy_normed, b * 2 * TT + 2 * t + 2)
                        nc.gpsimd.tensor_tensor(y[:, t], y[:, t], xvb_row[:], ALU.add).then_inc(cy_biased, 1)

            @block.scalar
            def _(act):
                def exp_tile(g, k):
                    n = (k % TT + 1) * P
                    act.wait_ge(max_done, g + k + 1)
                    nc.scalar.activation(probs[:, k % TT, 0:n], bank[k % 4][:, 0:n], ACT.Exp,
                                         bias=neg_max[:, k:k + 1], scale=1.0).then_inc(exp_done, 1)

                def left_high_part(i, k):
                    act.wait_ge(left_ready, i + 1)
                    copy_high(left[:, k % 2], bank[4][:], 0.5 / 16).then_inc(left_high, 1)

                def probs_high(g, k, first):
                    j = k - 2
                    n = (j % TT + 1) * P
                    act.wait_ge(pT_ready, g + j + 1)
                    if not (first and j < 4):
                        act.wait_ge(y_ready, g + j - 3)
                    copy_high(probsT[:, j % 4, 0, 0:n], bank[5 + j % 2][:, 0:n]).then_inc(pT_high, 1)

                def turn(b, p, first=False):
                    g = b * (H * TT) + p * STEPS
                    for k in range(STEPS):
                        if k % TT == 1:
                            h = 1 + k // TT
                            if not (isinstance(p, int) and p * 2 + h == H):
                                left_high_part(b * H + p * 2 + h, h)
                        if not (first and k < 2):
                            probs_high(g, k, first)
                        exp_tile(g, k)

                act.wait_ge(ones_set, 5)
                with act.Fori(0, B) as b:
                    for c in range(KT):
                        act.wait_ge(xT_ready, b * 2 * KT + c + 1)
                        copy_high(xT[:, 0, c], bank[c][:]).then_inc(xT_high, 1)
                    act.wait_ge(lat_ready, b + 1)
                    copy_high(latent[:, 0], bank[4][:], 0.25 / WSCALE).then_inc(lat_high, 1)
                    for t in range(TT):
                        act.wait_ge(v_ready, b * TT + t + 1)
                        copy_high(values[:, 0, t, :, 0:HD], bank[5 + t % 3][:].rearrange("p (h d) -> p h d", h=H)
                                  ).then_inc(v_high, 1)
                        if t == 0:
                            left_high_part(b * H, 0)
                    turn(b, 0, first=True)
                    with act.Fori(1, PAIRS - 1) as p:
                        turn(b, p)
                    turn(b, PAIRS - 1)
                    g = b * (H * TT) + H * TT
                    for k in (0, 1):
                        probs_high(g, k, False)
                    act.wait_ge(ctxT_ready, b + 1)
                    copy_high(ctxT[:, 0], bank[4][:, 0:KT * S].rearrange("p (c s) -> p c s", c=KT)).then_inc(ctxT_high, 1)
                    act.wait_ge(k_added, b + 1)
                    for j in range(HG):
                        rows = slice(j * HD, j * HD + HD)
                        copy_high(k_diag[rows, 0, :, j * S:j * S + S], k_sum[rows]).then_inc(k_high, 1)
                    act.wait_ge(cv_ready, b + 1)
                    copy_high(c_values[:, 0, :, 0:HD], bank[6][0:S].rearrange("p (h d) -> p h d", h=H)).then_inc(cv_high, 1)
                    for c in range(KT):
                        act.wait_ge(yT_ready, b * 2 * KT + c + 1)
                        copy_high(yT[:, 0, c], bank[c][:]).then_inc(yT_high, 1)
                    for c in range(KT):
                        act.wait_ge(xT_ready, b * 2 * KT + KT + c + 1)
                        copy_high(xT[:, 0, c], bank[c][:]).then_inc(xT_high, 1)
                    for m in range(NG):
                        act.wait_ge(q_ready, b * NG + m + 1)
                        nc.scalar.activation(qT[:, 0, m], bank[4 + m][:], ACT.Identity, bias=q_bias[:, m:m + 1],
                                             scale=1.0).then_inc(q_high, 1)

                    def c_exp(t):
                        act.wait_ge(c_sub_done, (b * TT + t) * NG + NG)
                        nc.scalar.activation(c_probs[:, t % 2], c_probs[:, t % 2], ACT.Exp, scale=XSCALE).then_inc(c_exp_done, 1)

                    c_exp(0)
                    for t in range(TT):
                        for m in range(NG):
                            act.wait_ge(cpT_ready, (b * TT + t) * NG + m + 1)
                            if t * NG + m >= 2:
                                act.wait_ge(cy_ready, (b * TT + t) * NG + m - 1)
                            copy_high(c_probsT[:, m % 2, 0], bank[4 + m % 2][0:S]).then_inc(cpT_high, 1)
                        if t + 1 < TT:
                            c_exp(t + 1)
                    for c in range(KT):
                        act.wait_ge(yT_ready, b * 2 * KT + KT + c + 1)
                        copy_high(yT[:, 0, c], bank[c][:]).then_inc(yT_high, 1)

            @block.vector
            def _(dve):
                def layer_norm(n, src, loaded, count):
                    for t in range(TT):
                        dve.wait_ge(loaded, count(t))
                        nc.vector.bn_stats(stats[:, t], src[:, t]).then_inc(ln_stats, 1)
                    for t in range(TT):
                        wait_apart(dve, ln_stats, n * TT + t + 1, dve_waits)
                        nc.vector.bn_aggr(moments[:, t], stats[:, t]).then_inc(ln_mom, 1)
                    dve.wait_ge(ln_rstd, n + 1)
                    for t in range(TT):
                        nc.vector.tensor_scalar(xn[:, t], src[:, t], rstd[:, t:t + 1], shift[:, t:t + 1],
                                                ALU.mult, ALU.add).then_inc(ln_xn, 1)

                def max_tile(g, k):
                    n = (k % TT + 1) * P
                    dve.wait_ge(scores_ready, g + k + 1)
                    nc.vector.tensor_reduce(neg_max[:, k:k + 1], bank[k % 4][:, 0:n], AX_X, ALU.max,
                                            negate=True).then_inc(max_done, 1)

                def left_low_part(i, k):
                    dve.wait_ge(left_high, i + 1)
                    low(left[R:P, k % 2], bank[4][R:P], 0.5 / 16, left[R:P, k % 2]).then_inc(left_low, 1)

                def probs_low(g, k):
                    j = k - 2
                    n = (j % TT + 1) * P
                    dve.wait_ge(pT_high, g + j + 1)
                    nc.vector.tensor_tensor(probsT[:, j % 4, 1, 0:n], bank[5 + j % 2][:, 0:n], probsT[:, j % 4, 0, 0:n],
                                            ALU.subtract).then_inc(pT_low, 1)

                def normalise(i, h, col):
                    dve.wait_ge(y_ready, (i + 1) * TT)
                    src = bank[7][:, 0:TT * VW].rearrange("p (t d) -> p t d", t=TT)
                    nc.vector.reciprocal(sums[:, col], src[:, :, HD]).then_inc(sums_done, 1)
                    dve.wait_ge(sums_done, i + 1)
                    dst = y[:, :, h * HD:h * HD + HD] if isinstance(h, int) else y[:, :, bass.ds(h * HD, HD)]
                    nc.vector.tensor_tensor(dst, src[:, :, 0:HD], sums[:, col].unsqueeze(2).broadcast_to([P, TT, HD]),
                                            ALU.mult).then_inc(y_normed, 1)

                def turn(b, p, first=False):
                    g = b * (H * TT) + p * STEPS
                    for k in range(STEPS):
                        max_tile(g, k)
                        if k % TT == 1:
                            h = 1 + k // TT
                            if not (isinstance(p, int) and p * 2 + h == H):
                                left_low_part(b * H + p * 2 + h, h)
                        if not (first and k < 2):
                            probs_low(g, k)
                        if k == 3 and not first:
                            normalise(b * H + p * 2 - 1, p * 2 - 1, 1)
                        if k == 7:
                            normalise(b * H + p * 2, p * 2, 0)

                dve.sem_inc(x2_done, 1)
                with dve.Fori(0, B) as b:
                    layer_norm(b * 2, x_in, x_loaded, lambda t: (b + 1) * 16)
                    for c in range(KT):
                        dve.wait_ge(xT_high, b * 2 * KT + c + 1)
                        low(xT[:, 1, c], bank[c][:], 1.0, xT[:, 0, c]).then_inc(xT_low, 1)
                    dve.wait_ge(lat_high, b + 1)
                    low(latent[:, 1], bank[4][:], 0.25 / WSCALE, latent[:, 0]).then_inc(lat_low, 1)
                    for t in range(TT):
                        dve.wait_ge(v_high, b * TT + t + 1)
                        low(values[:, 1, t, :, 0:HD], bank[5 + t % 3][:].rearrange("p (h d) -> p h d", h=H), 1.0,
                            values[:, 0, t, :, 0:HD]).then_inc(v_low, 1)
                        if t == 0:
                            left_low_part(b * H, 0)
                    turn(b, 0, first=True)
                    with dve.Fori(1, PAIRS - 1) as p:
                        turn(b, p)
                    turn(b, PAIRS - 1)
                    g = b * (H * TT) + H * TT
                    for k in (0, 1):
                        probs_low(g, k)
                    normalise(b * H + H - 1, H - 1, 1)
                    dve.wait_ge(ctxT_high, b + 1)
                    low(ctxT[:, 1], bank[4][:, 0:KT * S].rearrange("p (c s) -> p c s", c=KT), 1.0,
                        ctxT[:, 0]).then_inc(ctxT_low, 1)
                    dve.wait_ge(k_ready, b + 1)
                    nc.vector.tensor_tensor(k_sum[:], bank[5][:, 0:NG * S].rearrange("p (c s) -> p c s", c=NG),
                                            k_bias[:].unsqueeze(2).broadcast_to([P, NG, S]), ALU.add).then_inc(k_added, 1)
                    for j in range(HG):
                        dve.wait_ge(k_high, b * HG + j + 1)
                        rows = slice(j * HD, j * HD + HD)
                        nc.vector.tensor_tensor(k_diag[rows, 1, :, j * S:j * S + S], k_sum[rows],
                                                k_diag[rows, 0, :, j * S:j * S + S], ALU.subtract).then_inc(k_low, 1)
                    dve.wait_ge(cv_high, b + 1)
                    low(c_values[:, 1, :, 0:HD], bank[6][0:S].rearrange("p (h d) -> p h d", h=H), 1.0,
                        c_values[:, 0, :, 0:HD]).then_inc(cv_low, 1)
                    for c in range(KT):
                        dve.wait_ge(yT_high, b * 2 * KT + c + 1)
                        low(yT[:, 1, c], bank[c][:], 1.0, yT[:, 0, c]).then_inc(yT_low, 1)
                    dve.wait_ge(x_taken, b * TT + TT)
                    for t in range(TT):
                        dve.wait_ge(o_ready, b * TT + t + 1)
                        nc.vector.scalar_tensor_tensor(x_res[:, t], bank[4 + t][:], 1.0 / WSCALE, x_res[:, t],
                                                       ALU.mult, ALU.add).then_inc(x1_done, 1)
                    layer_norm(b * 2 + 1, x_res, x1_done, lambda t: b * TT + t + 1)
                    for c in range(KT):
                        dve.wait_ge(xT_high, b * 2 * KT + KT + c + 1)
                        low(xT[:, 1, c], bank[c][:], 1.0, xT[:, 0, c]).then_inc(xT_low, 1)
                    for m in range(NG):
                        dve.wait_ge(q_high, b * NG + m + 1)
                        nc.vector.scalar_tensor_tensor(qT[:, 1, m], bank[4 + m][:], q_bias[:, m:m + 1], qT[:, 0, m],
                                                       ALU.add, ALU.subtract).then_inc(q_low, 1)

                    def c_center(t, m):
                        i = (b * TT + t) * NG + m
                        dve.wait_ge(cs_ready, i + 1)
                        src = bank[m][:, 0:HG * S].rearrange("p (h s) -> p h s", h=HG)
                        top = c_max[:, t % 2, m * HG:m * HG + HG]
                        nc.vector.tensor_reduce(top, src, AX_X, ALU.max).then_inc(c_max_done, 1)
                        dve.wait_ge(c_max_done, i + 1)
                        nc.vector.tensor_tensor(c_probs[:, t % 2, m * HG:m * HG + HG], src,
                                                top.unsqueeze(2).broadcast_to([P, HG, S]), ALU.subtract).then_inc(c_sub_done, 1)

                    for m in range(NG):
                        c_center(0, m)
                    for t in range(TT):
                        for m in range(NG):
                            if t + 1 < TT:
                                c_center(t + 1, m)
                            dve.wait_ge(cpT_high, (b * TT + t) * NG + m + 1)
                            nc.vector.tensor_tensor(c_probsT[:, m % 2, 1], bank[4 + m % 2][0:S], c_probsT[:, m % 2, 0],
                                                    ALU.subtract).then_inc(cpT_low, 1)
                        for half in range(2):
                            dve.wait_ge(cy_ready, (b * TT + t) * NG + 2 * half + 2)
                            src = bank[6 + half][:, 0:8 * VW].rearrange("p (h d) -> p h d", h=8)
                            s = c_sums[:, t % 2, half * 8:half * 8 + 8]
                            nc.vector.reciprocal(s, src[:, :, HD]).then_inc(c_sums_done, 1)
                            dve.wait_ge(c_sums_done, (b * TT + t) * 2 + half + 1)
                            nc.vector.tensor_tensor(
                                y[:, t, half * 256:half * 256 + 256].rearrange("p (h d) -> p h d", h=8), src[:, :, 0:HD],
                                s.unsqueeze(2).broadcast_to([P, 8, HD]), ALU.mult).then_inc(cy_normed, 1)
                    for c in range(KT):
                        dve.wait_ge(yT_high, b * 2 * KT + KT + c + 1)
                        low(yT[:, 1, c], bank[c][:], 1.0, yT[:, 0, c]).then_inc(yT_low, 1)
                    dve.wait_ge(xb_done, b * TT + TT)
                    dve.wait_ge(x2_stored, b * 16 + 16)
                    for t in range(TT):
                        dve.wait_ge(xo_ready, b * TT + t + 1)
                        nc.vector.scalar_tensor_tensor(x2_out[:, t], bank[4 + t][:], 1.0 / WSCALE, x_res[:, t],
                                                       ALU.mult, ALU.add).then_inc(x2_done, 1)

            @block.tensor
            def _(pe):
                def product(out, left_high, left_low, right_high, right_low, n=KT):
                    for c in range(n):
                        nc.tensor.matmul(out, left_high(c), right_high(c), start=(c == 0), stop=False)
                        nc.tensor.matmul(out, left_high(c), right_low(c), start=False, stop=False)
                        last = nc.tensor.matmul(out, left_low(c), right_high(c), start=False, stop=(c == n - 1))
                    return last

                def head_columns(buf, h, *lead):
                    return None

                def left_product(i, h, k):
                    if i is not None:
                        pe.wait_ge(left_low, i)
                    mat = head_mat[:, h, :] if isinstance(h, int) else head_mat[:, bass.ds(h, 1), :].rearrange("p o s -> p (o s)")
                    nc.tensor.matmul(bank[4][:], mat, latent[:, 0], start=True, stop=False)
                    nc.tensor.matmul(bank[4][:], mat, latent[:, 1], start=False, stop=True).then_inc(left_ready, 1)

                def score_tile(g, i, k, first):
                    t = k % TT
                    n = (t + 1) * P
                    if k % TT == 0:
                        pe.wait_ge(left_low, i + 1)
                    if not (first and k < 4):
                        pe.wait_ge(exp_done, g + k - 3)
                    lhs = left[:, (k // TT) % 2, t * P:t * P + P]
                    nc.tensor.matmul(bank[k % 4][:, 0:n], lhs, latent[:, 0, 0:n], start=True, stop=False)
                    nc.tensor.matmul(bank[k % 4][:, 0:n], lhs, latent[:, 1, 0:n], start=False, stop=False)
                    nc.tensor.matmul(bank[k % 4][:, n - P:n], big_ident[:], causal[:], start=False, stop=True
                                     ).then_inc(scores_ready, 1)

                def transpose_tile(g, k, first):
                    j = k - 2
                    t = j % TT
                    pe.wait_ge(exp_done, g + j + 1)
                    if not (first and j < 2):
                        pe.wait_ge(pT_low, g + j - 1)
                    for u in range(t + 1):
                        last = nc.tensor.transpose(bank[5 + j % 2][:, u * P:u * P + P], probs[:, t, u * P:u * P + P], ident[:])
                    last.then_inc(pT_ready, 1)

                def values_tile(g, i, h, k, first):
                    j = k - 4
                    t = j % TT
                    pe.wait_ge(pT_low, g + j + 1)
                    if t == 0 and not (first and j < 4):
                        pe.wait_ge(y_normed, i)
                    out = bank[7][:, t * VW:(t + 1) * VW]
                    for u in range(t + 1):
                        def v(part, width):
                            if isinstance(h, int):
                                return values[:, part, u, h, 0:width]
                            return values[:, part, u, bass.ds(h, 1), 0:width].rearrange("p o d -> p (o d)")
                        ph = probsT[:, j % 4, 0, u * P:u * P + P]
                        pl = probsT[:, j % 4, 1, u * P:u * P + P]
                        nc.tensor.matmul(out, ph, v(0, VW), start=(u == 0), stop=False)
                        nc.tensor.matmul(out[:, 0:HD], ph, v(1, HD), start=False, stop=False)
                        last = nc.tensor.matmul(out, pl, v(0, VW), start=False, stop=(u == t))
                    last.then_inc(y_ready, 1)

                def turn(b, p, first=False):
                    g = b * (H * TT) + p * STEPS
                    i = b * H + p * 2
                    for k in range(STEPS):
                        score_tile(g, i + k // TT, k, first)
                        if k % TT == 1:
                            h = 1 + k // TT
                            if not (isinstance(p, int) and p * 2 + h == H):
                                left_product(i + h, p * 2 + h, k)
                        if not (first and k < 2):
                            transpose_tile(g, k, first)
                        if not (first and k < 4):
                            d = 0 if k >= 4 else -1
                            values_tile(g, i + d, p * 2 + d, k, first)

                pe.wait_ge(ones_set, 5)
                with pe.Fori(0, B) as b:
                    def transposes(n, src, ready, count, out_ready):
                        pe.wait_ge(ready, count)
                        for c in range(KT):
                            for t in range(TT):
                                last = nc.tensor.transpose(bank[c][:, t * P:t * P + P], src[:, t, c * P:c * P + P], ident[:])
                            last.then_inc(out_ready, 1)

                    pe.wait_ge(x2_done, b * TT + 1)
                    transposes(0, xn, ln_xn, b * 2 * TT + TT, xT_ready)
                    pe.wait_ge(xT_low, b * 2 * KT + KT)
                    product(bank[4][:], lambda c: w_basis[:, 0, c], lambda c: w_basis[:, 1, c],
                            lambda c: xT[:, 0, c], lambda c: xT[:, 1, c]).then_inc(lat_ready, 1)
                    for t in range(TT):
                        if t == TT - 1:
                            pe.wait_ge(v_low, b * TT + 1)
                        ts = slice(t * P, t * P + P)
                        product(bank[5 + t % 3][:], lambda c: xT[:, 0, c, ts], lambda c: xT[:, 1, c, ts],
                                lambda c: W["wv"][:, 0, c], lambda c: W["wv"][:, 1, c]).then_inc(v_ready, 1)
                        if t == 0:
                            pe.wait_ge(lat_low, b + 1)
                            left_product(None, 0, 0)
                    pe.wait_ge(v_low, b * TT + TT)
                    turn(b, 0, first=True)
                    with pe.Fori(1, PAIRS - 1) as p:
                        turn(b, p)
                    turn(b, PAIRS - 1)
                    g = b * (H * TT) + H * TT
                    for k in range(4):
                        if k < 2:
                            transpose_tile(g, k, False)
                        values_tile(g, b * H + H - 1, H - 1, k, False)

                    pe.wait_ge(ctx_loaded, b * 16 + 16)
                    for c in range(KT):
                        last = nc.tensor.transpose(bank[4][:, c * S:c * S + S], ctx_sb[:, c * P:c * P + P], ident[0:S, 0:S])
                    last.then_inc(ctxT_ready, 1)
                    pe.wait_ge(ctxT_low, b + 1)
                    for m in range(NG):
                        ms = slice(m * P, m * P + P)
                        last = product(bank[5][:, m * S:m * S + S], lambda c: W["xwk"][:, 0, c, ms],
                                       lambda c: W["xwk"][:, 1, c, ms], lambda c: ctxT[:, 0, c], lambda c: ctxT[:, 1, c])
                    last.then_inc(k_ready, 1)
                    product(bank[6][0:S], lambda c: ctxT[:, 0, c], lambda c: ctxT[:, 1, c],
                            lambda c: W["xwv"][:, 0, c], lambda c: W["xwv"][:, 1, c]).then_inc(cv_ready, 1)

                    transposes(1, y, y_biased, b * TT + TT, yT_ready)
                    pe.wait_ge(yT_low, b * 2 * KT + KT)
                    pe.wait_ge(cv_low, b + 1)
                    for t in range(TT):
                        ts = slice(t * P, t * P + P)
                        product(bank[4 + t][:], lambda c: yT[:, 0, c, ts], lambda c: yT[:, 1, c, ts],
                                lambda c: W["wo"][:, 0, c], lambda c: W["wo"][:, 1, c]).then_inc(o_ready, 1)
                    transposes(2, xn, ln_xn, b * 2 * TT + 2 * TT, xT_ready)
                    pe.wait_ge(xT_low, b * 2 * KT + 2 * KT)
                    for m in range(NG):
                        ms = slice(m * P, m * P + P)
                        product(bank[4 + m][:], lambda c: W["xwq"][:, 0, c, ms], lambda c: W["xwq"][:, 1, c, ms],
                                lambda c: xT[:, 0, c], lambda c: xT[:, 1, c]).then_inc(q_ready, 1)
                    pe.wait_ge(q_low, b * NG + NG)
                    pe.wait_ge(k_low, b * HG + HG)

                    def c_scores(t):
                        ts = slice(t * P, t * P + P)
                        for m in range(NG):
                            if t > 0:
                                pe.wait_ge(c_sub_done, (b * TT + t - 1) * NG + m + 1)
                            product(bank[m][:, 0:HG * S], lambda c: qT[:, 0, m, ts], lambda c: qT[:, 1, m, ts],
                                    lambda c: k_diag[:, 0, m], lambda c: k_diag[:, 1, m], n=1).then_inc(cs_ready, 1)

                    def c_transposes(t, m):
                        if m == 0:
                            pe.wait_ge(c_exp_done, b * TT + t + 1)
                        if t * NG + m >= 2:
                            pe.wait_ge(cpT_low, (b * TT + t) * NG + m - 1)
                        for h in range(HG):
                            last = nc.tensor.transpose(bank[4 + m % 2][0:S, h * P:h * P + P],
                                                       c_probs[:, t % 2, m * HG + h], ident[:])
                        last.then_inc(cpT_ready, 1)

                    def c_values_product(t, m):
                        pe.wait_ge(cpT_low, (b * TT + t) * NG + m + 1)
                        if t > 0 and m % 2 == 0:
                            pe.wait_ge(cy_normed, (b * TT + t - 1) * 2 + m // 2 + 1)
                        for h in range(HG):
                            out = bank[6 + m // 2][:, ((m % 2) * HG + h) * VW:((m % 2) * HG + h + 1) * VW]
                            ph = c_probsT[:, m % 2, 0, h * P:h * P + P]
                            pl = c_probsT[:, m % 2, 1, h * P:h * P + P]
                            hh = m * HG + h
                            nc.tensor.matmul(out, ph, c_values[:, 0, hh, :], start=True, stop=False)
                            nc.tensor.matmul(out[:, 0:HD], ph, c_values[:, 1, hh, 0:HD], start=False, stop=False)
                            last = nc.tensor.matmul(out, pl, c_values[:, 0, hh, :], start=False, stop=True)
                        last.then_inc(cy_ready, 1)

                    c_scores(0)
                    for t in range(TT):
                        if t + 1 < TT:
                            c_scores(t + 1)
                        for m in range(NG):
                            c_transposes(t, m)
                            if m > 0:
                                c_values_product(t, m - 1)
                        c_values_product(t, NG - 1)

                    transposes(3, y, cy_biased, b * TT + TT, yT_ready)
                    pe.wait_ge(yT_low, b * 2 * KT + 2 * KT)
                    for t in range(TT):
                        ts = slice(t * P, t * P + P)
                        product(bank[4 + t][:], lambda c: yT[:, 0, c, ts], lambda c: yT[:, 1, c, ts],
                                lambda c: W["xwo"][:, 0, c], lambda c: W["xwo"][:, 1, c]).then_inc(xo_ready, 1)


NE, TOPK = 8, 2
F = 1024
FT = F // P
N = B * T
TILES = N // P
SLOT_TILES = -(-(TOPK * N // P + NE - 1) // 2) * 2
NM = 2 * NE
FREE_MATS = 6
X_SLOT, RAW_SLOT = 6, 7
XT_SLOT = 8


def wait(eng, s, value):
    if not isinstance(value, int) or value > 0:
        eng.wait_ge(s, value)


def build_ffn(nc, sem, x2_dram, out, rwT, r_bias, sw1, sw3, sw2, ew1, ew2, constants, xn_dram, slot_dram):
    with ExitStack() as keep:
        def sb(name, shape, dt):
            return keep.enter_context(nc.sbuf_tensor(name, shape, dt))

        experts = sb("experts", [P, NM, 2, KT, C], F16)
        slots = sb("slots", [P, TOPK, TILES, 1], mybir.dt.uint32)
        slot_rows = sb("slot_rows", [P, TOPK, TILES, 2], F32)
        tile_expert = sb("tile_expert", [P, SLOT_TILES], mybir.dt.int32)
        w1, w3 = sb("w1", [P, 2, KT, F], F16), sb("w3", [P, 2, KT, F], F16)
        w2 = sb("w2", [P, 2, FT, C], F16)

        def bytes_of(k):
            return experts[:, k].rearrange("p a b c -> p (a b c)").bitcast(F32)

        x_tiles = bytes_of(X_SLOT).rearrange("p (a c) -> p a c", a=TT)
        raw_tile = bytes_of(RAW_SLOT).rearrange("p (a c) -> p a c", a=KT)

        def matrix(e):
            return ew1[e // 2] if e % 2 == 0 else ew2[e // 2]

        bank = [keep.enter_context(nc.psum_tensor(f"ffn_bank{i}", [P, 512], F32)) for i in range(8)]
        x2_v = x2_dram.rearrange("(g a p) c -> g p a c", p=P, a=TT)
        out_v = out[0:N].rearrange("(g a p) c -> g p a c", p=P, a=TT)
        xn_v = xn_dram[0:N].rearrange("(g a p) c -> g p a c", p=P, a=TT)

        def group_of(v, g):
            return v[g] if isinstance(g, int) else v[bass.ds(g, 1)].rearrange("o p a c -> (o p) a c")

        with ExitStack() as scope:
            def tmp(name, shape, dt):
                return scope.enter_context(nc.sbuf_tensor(name, shape, dt))

            logits = tmp("logits", [P, TILES, NE], F32)
            router = tmp("router", [P, 2, KT, NE], F16)
            raw_router = tmp("raw_router", [P, KT, NE], F32)
            ident = tmp("f_ident", [P, P], F32)
            neg_half = tmp("f_neg_half", [P, TT], F32)
            zeros = tmp("zeros", [P, C], F32)
            consts = tmp("consts", [P, constants.shape[1]], F32)
            bias_row = tmp("bias_row", [P, NE], F32)
            with ExitStack() as inner:
                def tmp2(name, shape, dt):
                    return inner.enter_context(nc.sbuf_tensor(name, shape, dt))
                x_in = [bytes_of(k).rearrange("p (a c) -> p a c", a=TT) for k in (0, 1)]
                xn = [bytes_of(k).rearrange("p (a c) -> p a c", a=TT) for k in (2, 3)]
                raw1 = bytes_of(4), bytes_of(5)
                stats, moments = tmp2("f_stats", [P, TT, 6], F32), tmp2("f_moments", [P, TT, 2], F32)
                rstd, shift = tmp2("f_rstd", [P, TT], F32), tmp2("f_shift", [P, TT], F32)
                x_loaded = [sem("f_x_loaded0"), sem("f_x_loaded1")]
                router_loaded, const_loaded = sem("router_loaded"), sem("const_loaded")
                made, router_high, router_low = sem("f_made"), sem("router_high"), sem("router_low")
                st, mo, pl, rs, xn_done = sem("f_stats"), sem("f_moments"), sem("f_pool"), sem("f_rstd"), sem("f_xn")
                xn_stored, pads_stored = [sem("xn_stored0"), sem("xn_stored1")], sem("pads_stored")
                t_ready, t_high, t_low = sem("f_t_ready"), sem("f_t_high"), sem("f_t_low")
                lg_ready, lg_done = sem("lg_ready"), sem("lg_done")
                dve_waits, pool_waits = sem("f_dve_waits"), sem("f_pool_waits")
                sw_loaded, sw_high, sw_low = [sem("sw_loaded0"), sem("sw_loaded1")], sem("sw_high"), sem("sw_low")
                G = B

                with nc.Block() as block:
                    @block.sync
                    def _(sp):
                        sp.dma_start(raw_router[:], rwT.rearrange("(a p) n -> p a n", p=P)).then_inc(router_loaded, 16)
                        sp.dma_start(consts[:], constants.broadcast_to([P, constants.shape[1]])).then_inc(const_loaded, 16)
                        sp.dma_start(bias_row[:], r_bias.rearrange("(a n) -> a n", a=1).broadcast_to([P, NE])).then_inc(const_loaded, 16)

                        def load(g, s):
                            wait(sp, xn_done, g * TT - TT)
                            sp.dma_start(x_in[s], group_of(x2_v, g)).then_inc(x_loaded[s], 16)

                        def store(g, s):
                            sp.wait_ge(xn_done, g * TT + TT)
                            sp.dma_start(group_of(xn_v, g), xn[s]).then_inc(xn_stored[s], 16)

                        load(0, 0)
                        load(1, 1)
                        sp.wait_ge(made, 3)
                        sp.dma_start(xn_dram[N:N + P], zeros[:]).then_inc(pads_stored, 16)
                        with sp.Fori(1, G // 2) as i:
                            for s in range(2):
                                store(i * 2 + (s - 2), s)
                                load(i * 2 + s, s)
                        store(G - 2, 0)
                        store(G - 1, 1)
                        for s in range(2):
                            sp.wait_ge(xn_stored[s], 16 * (G // 2))
                        sp.wait_ge(pads_stored, 16)

                    @block.gpsimd
                    def _(pool):
                        nc.gpsimd.memset(ident[:], 0.0).then_inc(made, 1)
                        nc.gpsimd.memset(neg_half[:], -0.5).then_inc(made, 1)
                        nc.gpsimd.memset(zeros[:], 0.0).then_inc(made, 1)
                        pool.wait_ge(made, 3)
                        nc.gpsimd.affine_select(out=ident[:], in_=ident[:], compare_op=ALU.not_equal, fill=1.0, base=0,
                                                pattern=[[-1, P]], channel_multiplier=1).then_inc(made, 1)
                        with pool.Fori(0, G) as g:
                            wait_apart(pool, mo, g * TT + TT, pool_waits)
                            nc.gpsimd.tensor_scalar(rstd[:], moments[:, :, 1], 1.0, EPS, ALU.mult, ALU.add).then_inc(pl, 1)
                            pool.wait_ge(pl, g * 3 + 1)
                            nc.gpsimd.tensor_tensor(rstd[:], rstd[:], neg_half[:], ALU.pow).then_inc(pl, 1)
                            pool.wait_ge(pl, g * 3 + 2)
                            nc.gpsimd.tensor_tensor(shift[:], moments[:, :, 0], rstd[:], ALU.mult).then_inc(pl, 1)
                            wait_apart(pool, pl, g * 3 + 3, pool_waits)
                            nc.gpsimd.tensor_scalar(shift[:], shift[:], -1.0, 0.0, ALU.mult, ALU.add).then_inc(rs, 1)

                    @block.scalar
                    def _(act):
                        act.wait_ge(router_loaded, 16)
                        nc.scalar.activation(router[:, 0], raw_router[:], ACT.Copy, scale=WSCALE).then_inc(router_high, 1)

                        def high(g, s):
                            for c in range(KT):
                                act.wait_ge(t_ready, g * KT + c + 1)
                                k = g + XT_SLOT
                                dst = experts[:, k, 0, c] if isinstance(g, int) else \
                                    experts[:, bass.ds(k, 1), 0, c].rearrange("p o n -> p (o n)")
                                nc.scalar.activation(dst, bank[c][:], ACT.Copy).then_inc(t_high, 1)

                        def logit(g):
                            act.wait_ge(lg_ready, g + 1)
                            nc.scalar.activation(logits[:, bass.ds(g * TT, TT)], bank[4][:, 0:TT * NE].rearrange(
                                "p (t e) -> p t e", t=TT), ACT.Copy, scale=1.0 / WSCALE).then_inc(lg_done, 1)

                        high(0, 0)
                        with act.Fori(1, G) as g:
                            logit(g - 1)
                            high(g, 0)
                        logit(G - 1)

                    @block.vector
                    def _(dve):
                        dve.wait_ge(router_high, 1)
                        nc.vector.scalar_tensor_tensor(router[:, 1], raw_router[:], WSCALE, router[:, 0],
                                                       ALU.mult, ALU.subtract).then_inc(router_low, 1)

                        def moments_of(i, g, s):
                            dve.wait_ge(x_loaded[s], i * 16 + 16)
                            for t in range(TT):
                                nc.vector.bn_stats(stats[:, t], x_in[s][:, t]).then_inc(st, 1)
                            for t in range(TT):
                                wait_apart(dve, st, g * TT + t + 1, dve_waits)
                                nc.vector.bn_aggr(moments[:, t], stats[:, t]).then_inc(mo, 1)

                        def low(g, s):
                            for c in range(KT):
                                dve.wait_ge(t_high, g * KT + c + 1)
                                k = g + XT_SLOT
                                hi, lo = (experts[:, k, h, c] if isinstance(g, int) else
                                          experts[:, bass.ds(k, 1), h, c].rearrange("p o n -> p (o n)") for h in range(2))
                                nc.vector.tensor_tensor(lo, bank[c][:], hi, ALU.subtract).then_inc(t_low, 1)

                        def normalise(i, g, s):
                            dve.wait_ge(rs, g + 1)
                            wait(dve, xn_stored[s], i * 16)
                            wait(dve, t_ready, g * KT - KT)
                            for t in range(TT):
                                nc.vector.tensor_scalar(xn[s][:, t], x_in[s][:, t], rstd[:, t:t + 1], shift[:, t:t + 1],
                                                        ALU.mult, ALU.add).then_inc(xn_done, 1)

                        def step(i, s):
                            g = i * 2 + s
                            moments_of(i, g, s)
                            if not (isinstance(g, int) and g == 0):
                                low(g - 1, 1 - s)
                            normalise(i, g, s)

                        step(0, 0)
                        step(0, 1)
                        with dve.Fori(1, G // 2) as i:
                            for s in range(2):
                                step(i, s)
                        low(G - 1, 1)

                    @block.tensor
                    def _(pe):
                        pe.wait_ge(made, 4)
                        pe.wait_ge(router_low, 1)

                        def transposes(g, s):
                            pe.wait_ge(xn_done, g * TT + TT)
                            for c in range(KT):
                                for t in range(TT):
                                    last = nc.tensor.transpose(bank[c][:, t * P:t * P + P], xn[s][:, t, c * P:c * P + P], ident[:])
                                last.then_inc(t_ready, 1)

                        def logit(g):
                            pe.wait_ge(t_low, g * KT + KT)
                            wait(pe, lg_done, g)
                            for t in range(TT):
                                for c in range(KT):
                                    def xt(h):
                                        k = g + XT_SLOT
                                        ts = slice(t * P, t * P + P)
                                        return experts[:, k, h, c, ts] if isinstance(g, int) else \
                                            experts[:, bass.ds(k, 1), h, c, ts].rearrange("p o n -> p (o n)")
                                    o = bank[4][:, t * NE:t * NE + NE]
                                    nc.tensor.matmul(o, xt(0), router[:, 0, c], start=(c == 0), stop=False)
                                    nc.tensor.matmul(o, xt(0), router[:, 1, c], start=False, stop=False)
                                    last = nc.tensor.matmul(o, xt(1), router[:, 0, c], start=False, stop=(c == KT - 1))
                            last.then_inc(lg_ready, 1)

                        transposes(0, 0)
                        logit(0)
                        transposes(1, 1)
                        with pe.Fori(1, G // 2) as i:
                            for s in range(2):
                                logit(i * 2 + (s - 1))
                                transposes(i * 2 + s, s)
                        logit(G - 1)

            with ExitStack() as inner:
                views = iter(range(4 * 8))
                W_ = TILES * NE

                def grid():
                    k = next(views)
                    return bytes_of(k // 8)[:, (k % 8) * W_:(k % 8 + 1) * W_].rearrange("p (t e) -> p t e", e=NE)

                def col(name, n=TILES, dt=F32):
                    return inner.enter_context(nc.sbuf_tensor(name, [P, n], dt))

                raw_sw = [bytes_of(4), bytes_of(5)]
                score, biased, first, second, rest, both = grid(), grid(), grid(), grid(), grid(), grid()
                cand, within, total, upto, slot, work = grid(), grid(), grid(), grid(), grid(), grid()
                m1, m2, i1, i2 = col("m1"), col("m2"), col("i1"), col("i2")
                s1, s2, den, safe, fine = col("s1"), col("s2"), col("den"), col("safe"), col("fine")
                g1, g2, sf = col("g1"), col("g2"), col("sf", TOPK * TILES)
                count, tiles_of, tiles_upto, base = col("count", NE), col("tiles_of", NE), col("tiles_upto", NE), col("base", NE)
                ones_col = col("ones_col", TILES)
                both16 = col("both16", W_, F16)
                below = inner.enter_context(nc.sbuf_tensor("below", [P, P], F16))
                all_ones = inner.enter_context(nc.sbuf_tensor("all_ones", [P, P], F16))
                many = bytes_of(3)[:, 0:SLOT_TILES * NE].rearrange("p (q e) -> p q e", e=NE)
                ef = col("ef", SLOT_TILES)
                token = col("token", TILES, mybir.dt.int32)
                pad_rows = inner.enter_context(nc.sbuf_tensor("pad_rows", [P, SLOT_TILES, 2], mybir.dt.int32))
                e_row = consts[:, 0:NE]
                steps_row = consts[:, NE:NE + TILES]
                q_row = consts[:, NE + TILES:NE + TILES + SLOT_TILES]
                sig, chain, made2, pos_ready = sem("sig"), sem("chain"), sem("made2"), sem("pos_ready")
                pads_done, both_done = sem("pads_done"), sem("both_done")

                def over_tiles(row):
                    return row.unsqueeze(1).broadcast_to([P, TILES, NE])

                def over_experts(c):
                    return c.unsqueeze(2).broadcast_to([P, TILES, NE])

                with nc.Block() as block:
                    @block.scalar
                    def _(act):
                        nc.scalar.activation(score, logits[:], ACT.Sigmoid).then_inc(sig, 1)
                        pieces = [(w, a) for w in range(3) for a in range(2)]
                        for n, (w, a) in enumerate(pieces):
                            act.wait_ge(sw_loaded[n % 2], 16 * (n // 2) + 16)
                            dst = (w1[:, 0, 2 * a:2 * a + 2], w3[:, 0, 2 * a:2 * a + 2], w2[:, 0, 4 * a:4 * a + 4])[w]
                            nc.scalar.activation(dst, raw_sw[n % 2].rearrange("p (a c) -> p a c", c=dst.shape[2]), ACT.Copy,
                                                 scale=WSCALE).then_inc(sw_high, 1)

                    @block.sync
                    def _(sp):
                        pieces = [(w, a) for w in range(3) for a in range(2)]
                        for n, (w, a) in enumerate(pieces):
                            if n >= 2:
                                sp.wait_ge(sw_low, n - 1)
                            src = (sw1, sw3, sw2)[w].rearrange("(h a p) n -> h p a n", p=P, h=2)[a]
                            sp.dma_start(raw_sw[n % 2].rearrange("p (a c) -> p a c", c=src.shape[2]), src).then_inc(sw_loaded[n % 2], 16)
                            if n == 1:
                                sp.wait_ge(made2, 5)
                                sp.dma_start(slot_dram.rearrange("(q p) c -> p q c", p=P), pad_rows[:]).then_inc(pads_done, 16)
                        sp.wait_ge(pads_done, 16)

                    @block.gpsimd
                    def _(pool):
                        nc.gpsimd.memset(below[:], 1.0).then_inc(made2, 1)
                        nc.gpsimd.memset(all_ones[:], 1.0).then_inc(made2, 1)
                        nc.gpsimd.memset(pad_rows[:, :, 1], 0).then_inc(made2, 1)
                        nc.gpsimd.iota(pad_rows[:, :, 0], pattern=[[0, SLOT_TILES]], base=N, channel_multiplier=1).then_inc(made2, 1)
                        nc.gpsimd.iota(token[:], pattern=[[P, TILES]], base=0, channel_multiplier=1).then_inc(made2, 1)
                        pool.wait_ge(made2, 5)
                        nc.gpsimd.affine_select(out=below[:], in_=below[:], compare_op=ALU.is_gt, fill=0.0, base=0,
                                                pattern=[[1, P]], channel_multiplier=-1).then_inc(made2, 1)

                    @block.tensor
                    def _(pe):
                        pe.wait_ge(both_done, 1)
                        pe.wait_ge(made2, 6)
                        nc.tensor.matmul(bank[0][:, 0:W_], below[:], both16[:], start=True, stop=True).then_inc(pos_ready, 1)
                        nc.tensor.matmul(bank[1][:, 0:W_], all_ones[:], both16[:], start=True, stop=True).then_inc(pos_ready, 1)

                    @block.vector
                    def _(dve):
                        steps = [0]

                        def then(ins):
                            steps[0] += 1
                            ins.then_inc(chain, 1)
                            dve.wait_ge(chain, steps[0])

                        def split_shared(n):
                            w, a = n // 2, n % 2
                            dve.wait_ge(sw_high, n + 1)
                            hi, lo = ((w1[:, h, 2 * a:2 * a + 2], w3[:, h, 2 * a:2 * a + 2], w2[:, h, 4 * a:4 * a + 4])[w] for h in range(2))
                            nc.vector.scalar_tensor_tensor(lo, raw_sw[n % 2].rearrange("p (a c) -> p a c", c=hi.shape[2]), WSCALE, hi,
                                                           ALU.mult, ALU.subtract).then_inc(sw_low, 1)

                        V = nc.vector
                        dve.wait_ge(sig, 1)
                        then(V.tensor_tensor(biased, score, over_tiles(bias_row[:]), ALU.add))

                        def best(src, top, index, mask):
                            then(V.tensor_reduce(top, src, AX_X, ALU.max))
                            then(V.tensor_tensor(cand, src, over_experts(top), ALU.is_lt))
                            then(V.scalar_tensor_tensor(cand, cand, float(NE), over_tiles(e_row), ALU.mult, ALU.add))
                            then(V.tensor_reduce(index, cand, AX_X, ALU.min))
                            then(V.tensor_tensor(mask, over_tiles(e_row), over_experts(index), ALU.is_equal))

                        best(biased, m1[:], i1[:], first)
                        then(V.scalar_tensor_tensor(rest, first, -1e30, biased, ALU.mult, ALU.add))
                        best(rest, m2[:], i2[:], second)
                        then(V.tensor_tensor(both, first, second, ALU.add))
                        steps[0] += 0
                        V.tensor_copy(both16[:], both.rearrange("p t e -> p (t e)")).then_inc(both_done, 1)
                        for mask, s in ((first, s1), (second, s2)):
                            then(V.tensor_tensor(work, mask, score, ALU.mult))
                            then(V.tensor_reduce(s[:], work, AX_X, ALU.add))
                        then(V.tensor_tensor(den[:], s1[:], s2[:], ALU.add))
                        then(V.tensor_scalar(safe[:], den[:], 1e-9, None, ALU.add))
                        then(V.reciprocal(safe[:], safe[:]))
                        then(V.tensor_scalar(fine[:], den[:], 1e-9, None, ALU.is_gt))
                        dve.wait_ge(made2, 5)
                        for s, g, k in ((s1, g1, 0), (s2, g2, 1)):
                            then(V.tensor_tensor(g[:], s[:], safe[:], ALU.mult))
                            then(V.tensor_tensor(g[:], g[:], fine[:], ALU.mult))
                            then(V.tensor_scalar(s[:], fine[:], -0.5, 0.5, ALU.mult, ALU.add))
                            then(V.tensor_tensor(slot_rows[:, k, :, 1], g[:], s[:], ALU.add))
                            then(V.tensor_copy(slot_rows[:, k, :, 0].bitcast(mybir.dt.int32), token[:]))
                        split_shared(0)
                        split_shared(1)
                        dve.wait_ge(pos_ready, 2)
                        then(V.tensor_copy(total, bank[1][:, 0:W_].rearrange("p (t e) -> p t e", e=NE)))
                        then(V.memset(ones_col[:], 1.0))
                        for e in range(NE):
                            then(V.tensor_tensor_scan(upto[:, :, e], ones_col[:], total[:, :, e], 0.0, ALU.mult, ALU.add))
                        then(V.tensor_copy(count[:], upto[:, TILES - 1]))
                        cmp = work.rearrange("p t e -> p (t e)").rearrange("p (e k) -> p e k", e=NE)
                        then(V.tensor_tensor(cmp, count[:].unsqueeze(2).broadcast_to([P, NE, TILES]),
                                             steps_row.unsqueeze(1).broadcast_to([P, NE, TILES]), ALU.is_gt))
                        then(V.tensor_reduce(tiles_of[:], cmp, AX_X, ALU.add))
                        then(V.tensor_tensor_scan(tiles_upto[:], ones_col[:, 0:NE], tiles_of[:], 0.0, ALU.mult, ALU.add))
                        then(V.tensor_tensor(base[:], tiles_upto[:], tiles_of[:], ALU.subtract))
                        then(V.tensor_scalar(base[:], base[:], float(P), None, ALU.mult))
                        then(V.tensor_tensor(slot, upto, total, ALU.subtract))
                        then(V.tensor_tensor(slot, slot, over_tiles(base[:]), ALU.add))
                        then(V.tensor_tensor(slot, slot, bank[0][:, 0:W_].rearrange("p (t e) -> p t e", e=NE), ALU.add))
                        for k, mask in enumerate((first, second)):
                            then(V.tensor_tensor(work, mask, slot, ALU.mult))
                            then(V.tensor_reduce(sf[:, k * TILES:(k + 1) * TILES], work, AX_X, ALU.add))
                        then(V.tensor_copy(slots[:, :, :, 0], sf[:].rearrange("p (k t) -> p k t", k=TOPK)))
                        then(V.tensor_tensor(many, tiles_upto[:].unsqueeze(1).broadcast_to([P, SLOT_TILES, NE]),
                                             q_row.unsqueeze(2).broadcast_to([P, SLOT_TILES, NE]), ALU.is_le))
                        then(V.tensor_reduce(ef[:], many, AX_X, ALU.add))
                        then(V.tensor_scalar(ef[:], ef[:], float(NE - 1), None, ALU.min))
                        then(V.tensor_copy(tile_expert[:], ef[:]))
                        for n in range(2, 6):
                            split_shared(n)

        gT = sb("gT", [P, 2, FT, T], F16)
        with ExitStack() as scope:
            gate = scope.enter_context(nc.sbuf_tensor("gate", [P, 2, T], F32))
            x_loaded, x_stored = sem("s_x_loaded"), sem("s_x_stored")
            h_ready, silu_done, g_done, g_high, g_low = sem("h_ready"), sem("silu_done"), sem("g_done"), sem("g_high"), sem("g_low")
            o_ready, o_done = sem("s_o_ready"), sem("s_o_done")
            rows_placed = sem("rows_placed")
            mat_loaded, mat_step, mat_done = sem("mat_loaded"), sem("mat_step"), sem("mat_done")
            early = list(range(FREE_MATS)) + list(range(XT_SLOT, NM - 1))

            with nc.Block() as block:
                @block.sync
                def _(sp):
                    sp.dma_start(x_tiles, x2_v[0]).then_inc(x_loaded, 16)

                    for g in range(B):
                        sp.wait_ge(o_done, g * TT + TT)
                        sp.dma_start(out_v[g], x_tiles).then_inc(x_stored, 16)
                        if g + 1 < B:
                            sp.wait_ge(x_stored, g * 16 + 16)
                            sp.dma_start(x_tiles, x2_v[g + 1]).then_inc(x_loaded, 16)
                    sp.wait_ge(x_stored, 16 * B)

                @block.gpsimd
                def _(pool):
                    for k in range(TOPK):
                        for t in range(TILES):
                            nc.gpsimd.indirect_dma_start(
                                slot_dram, bass.IndirectOffsetOnAxis(ap=slots[:, k, t], axis=0),
                                slot_rows[:, k, t].bitcast(mybir.dt.int32), None).then_inc(rows_placed, 16)
                    for n, m in enumerate(early):
                        if m >= XT_SLOT:
                            pool.wait_ge(o_ready, (m - XT_SLOT) * TT + TT)
                        if n > 0:
                            pool.wait_ge(mat_done, n)
                        pool.dma_start(raw_tile, matrix(m).rearrange("(a p) c -> p a c", p=P)).then_inc(mat_loaded, 16)
                        pool.wait_ge(mat_loaded, 16 * n + 16)
                        nc.gpsimd.tensor_scalar(raw_tile, raw_tile, WSCALE, 0.0, ALU.mult, ALU.add).then_inc(mat_step, 1)
                        pool.wait_ge(mat_step, 2 * n + 1)
                        nc.gpsimd.tensor_copy(experts[:, m, 0], raw_tile).then_inc(mat_step, 1)
                        pool.wait_ge(mat_step, 2 * n + 2)
                        nc.gpsimd.tensor_tensor(experts[:, m, 1], raw_tile, experts[:, m, 0], ALU.subtract).then_inc(mat_done, 1)
                    pool.wait_ge(rows_placed, 16 * TOPK * TILES)

                @block.scalar
                def _(act):
                    def high(i, f):
                        act.wait_ge(g_done, i + 1)
                        nc.scalar.activation(gT[:, 0, f], gate[:, f % 2], ACT.Copy).then_inc(g_high, 1)

                    def group(g):
                        for f in range(FT):
                            i = g * FT + f
                            act.wait_ge(h_ready, i * 2 + 1)
                            wait(act, g_low, i - 1)
                            nc.scalar.activation(gate[:, f % 2], bank[f % 2][:], ACT.Silu, scale=1.0 / WSCALE).then_inc(silu_done, 1)
                            if f == 0:
                                wait(act, o_ready, g * TT)
                            else:
                                high(i - 1, f - 1)
                        high(g * FT + FT - 1, FT - 1)

                    group(0)
                    with act.Fori(1, B) as g:
                        group(g)

                @block.vector
                def _(dve):
                    def low(i, f):
                        dve.wait_ge(g_high, i + 1)
                        nc.vector.tensor_tensor(gT[:, 1, f], gate[:, f % 2], gT[:, 0, f], ALU.subtract).then_inc(g_low, 1)

                    def group(g):
                        for f in range(FT):
                            i = g * FT + f
                            dve.wait_ge(silu_done, i + 1)
                            dve.wait_ge(h_ready, i * 2 + 2)
                            nc.vector.scalar_tensor_tensor(gate[:, f % 2], bank[2 + f % 2][:], 1.0 / WSCALE, gate[:, f % 2],
                                                           ALU.mult, ALU.mult).then_inc(g_done, 1)
                            if f > 0:
                                low(i - 1, f - 1)
                        low(g * FT + FT - 1, FT - 1)
                        dve.wait_ge(x_loaded, g * 16 + 16)
                        for t in range(TT):
                            dve.wait_ge(o_ready, g * TT + t + 1)
                            nc.vector.scalar_tensor_tensor(x_tiles[:, t], bank[4 + t][:], 1.0 / WSCALE, x_tiles[:, t],
                                                           ALU.mult, ALU.add).then_inc(o_done, 1)

                    group(0)
                    with dve.Fori(1, B) as g:
                        group(g)

                @block.tensor
                def _(pe):
                    def group(g):
                        def xt(h, c):
                            k = g + XT_SLOT
                            return experts[:, k, h, c] if isinstance(g, int) else \
                                experts[:, bass.ds(k, 1), h, c].rearrange("p o n -> p (o n)")

                        def hidden(out_bank, w, f):
                            fs = slice(f * P, f * P + P)
                            for c in range(KT):
                                nc.tensor.matmul(out_bank, w[:, 0, c, fs], xt(0, c), start=(c == 0), stop=False)
                                nc.tensor.matmul(out_bank, w[:, 0, c, fs], xt(1, c), start=False, stop=False)
                                last = nc.tensor.matmul(out_bank, w[:, 1, c, fs], xt(0, c), start=False, stop=(c == KT - 1))
                            last.then_inc(h_ready, 1)

                        for f in range(FT):
                            i = g * FT + f
                            wait(pe, silu_done, i - 1)
                            hidden(bank[f % 2][:], w1, f)
                            wait(pe, g_done, i - 1)
                            hidden(bank[2 + f % 2][:], w3, f)
                        wait(pe, o_done, g * TT)
                        for f in range(FT):
                            pe.wait_ge(g_low, g * FT + f + 1)
                            for t in range(TT):
                                ts = slice(t * P, t * P + P)
                                nc.tensor.matmul(bank[4 + t][:], gT[:, 0, f, ts], w2[:, 0, f], start=(f == 0), stop=False)
                                nc.tensor.matmul(bank[4 + t][:], gT[:, 0, f, ts], w2[:, 1, f], start=False, stop=False)
                                last = nc.tensor.matmul(bank[4 + t][:], gT[:, 1, f, ts], w2[:, 0, f], start=False, stop=(f == FT - 1))
                                if f == FT - 1:
                                    last.then_inc(o_ready, 1)

                    group(0)
                    with pe.Fori(1, B) as g:
                        group(g)

        build_routed(nc, sem, keep, experts, tile_expert, bank, matrix, out, xn_dram, slot_dram, w1, w3, w2, gT)


AHEAD = 4


def build_routed(nc, sem, keep, experts, tile_expert, bank, matrix, out, xn_dram, slot_dram, w1, w3, w2, gT):
    with ExitStack() as scope:
        def view(t, lead, dt, *shape):
            flat = t[:].rearrange("p a b c -> p (a b c)").bitcast(dt)
            return flat

        f1, f3, f2, fg = (view(t, None, F32) for t in (w1, w3, w2, gT))
        raw = [f1[:, 0:2048], f1[:, 2048:4096], f3[:, 0:2048]]
        xg = [f3[:, 2048 + k * C:2048 + k * C + C] for k in range(AHEAD)]
        h_sb = [f2[:, k * C:k * C + C] for k in range(2)]
        y_sb = [f2[:, (2 + k) * C:(3 + k) * C] for k in range(2)]
        h16 = w2[:].rearrange("p a b c -> p (a b c)")
        xT = [h16[:, 4096 + k * 1024:4096 + k * 1024 + 1024].rearrange("p (h c t) -> p h c t", h=2, c=KT) for k in range(2)]
        hT = [h16[:, 6144 + k * 1024:6144 + k * 1024 + 1024].rearrange("p (h c t) -> p h c t", h=2, c=KT) for k in range(2)]
        ident = scope.enter_context(nc.sbuf_tensor("r_ident", [P, P], F32))
        rows = scope.enter_context(nc.sbuf_tensor("rows", [P, 2 * AHEAD, 2], mybir.dt.int32))
        made, raw_high, raw_low = sem("r_made"), sem("raw_high"), sem("raw_low")
        raw_loaded = [sem(f"raw_loaded{n}") for n in range(3)]
        rows_loaded = [sem(f"rows_loaded{k}") for k in range(8)]
        gathered, added = [sem(f"gathered{k}") for k in range(AHEAD)], sem("added")
        xT_ready, xT_high, xT_low = sem("r_xT_ready"), sem("r_xT_high"), sem("r_xT_low")
        h_ready, gelu_done = sem("r_h_ready"), sem("gelu_done")
        hT_ready, hT_high, hT_low = sem("hT_ready"), sem("hT_high"), sem("hT_low")
        y_ready, y_done = sem("r_y_ready"), sem("r_y_done")
        pe_waits, pool_waits = sem("r_pe_waits"), sem("r_pool_waits")
        late = [X_SLOT, RAW_SLOT, NM - 1]
        Q = SLOT_TILES
        I32 = mybir.dt.int32
        slot_v = slot_dram.rearrange("(q p) c -> q p c", p=P)

        def turns_all(eng, body):
            for k in range(8):
                body(0, k)
            with eng.Fori(1, Q // 8 - 1) as i:
                for k in range(8):
                    body(i, k)
            for k in range(8):
                body(Q // 8 - 1, k)

        with nc.Block() as block:
            @block.sync
            def _(sp):
                for n, m in enumerate(late):
                    sp.dma_start(raw[n].rearrange("p (a c) -> p a c", a=KT), matrix(m).rearrange("(a p) c -> p a c", p=P)
                                 ).then_inc(raw_loaded[n], 16)

                def body(i, k):
                    q = i * 8 + k
                    wait(sp, added, q * 16 - 7 * 16)
                    src = slot_v[q] if isinstance(q, int) else slot_v[bass.ds(q, 1)].rearrange("o p c -> (o p) c")
                    sp.dma_start(rows[:, k], src).then_inc(rows_loaded[k], 16)
                turns_all(sp, body)

            @block.gpsimd
            def _(pool):
                nc.gpsimd.memset(ident[:], 0.0).then_inc(made, 1)
                pool.wait_ge(made, 1)
                nc.gpsimd.affine_select(out=ident[:], in_=ident[:], compare_op=ALU.not_equal, fill=1.0, base=0,
                                        pattern=[[-1, P]], channel_multiplier=1).then_inc(made, 1)

                def gather(i, k):
                    i, k = i + k // 8, k % 8
                    q = i * 8 + k
                    wait(pool, xT_ready, q - AHEAD + 1)
                    wait_apart(pool, rows_loaded[k], i * 16 + 16, pool_waits)
                    nc.gpsimd.indirect_dma_start(xg[k % AHEAD], None, xn_dram,
                                                 bass.IndirectOffsetOnAxis(ap=rows[:, k, 0:1].bitcast(mybir.dt.uint32), axis=0)
                                                 ).then_inc(gathered[k % AHEAD], 16)

                def add(i, k):
                    q = i * 8 + k
                    wait(pool, added, q * 16)
                    wait_apart(pool, y_done, q + 1, pool_waits)
                    nc.gpsimd.indirect_dma_start(out, bass.IndirectOffsetOnAxis(ap=rows[:, k, 0:1].bitcast(mybir.dt.uint32), axis=0),
                                                 y_sb[k % 2], None, compute_op=ALU.add).then_inc(added, 16)

                for k in range(AHEAD - 1):
                    gather(0, k)

                def body(i, k):
                    if not (isinstance(i, int) and i * 8 + k + AHEAD - 1 >= Q):
                        gather(i, k + AHEAD - 1)
                    add(i, k)
                turns_all(pool, body)
                pool.wait_ge(added, 16 * Q)

            @block.scalar
            def _(act):
                for n, m in enumerate(late):
                    act.wait_ge(raw_loaded[n], 16)
                    nc.scalar.activation(experts[:, m, 0], raw[n].rearrange("p (a c) -> p a c", a=KT), ACT.Copy,
                                         scale=WSCALE).then_inc(raw_high, 1)

                def x_high(i, k):
                    i, k = i + k // 8, k % 8
                    q = i * 8 + k
                    act.wait_ge(xT_ready, q + 1)
                    wait(act, h_ready, q - 1)
                    nc.scalar.activation(xT[k % 2][:, 0], bank[k % 2][:].rearrange("p (c t) -> p c t", c=KT), ACT.Copy).then_inc(xT_high, 1)

                def h_high(i, k):
                    i, k = i + k // 8, k % 8
                    q = i * 8 + k
                    act.wait_ge(hT_ready, q + 1)
                    wait(act, y_ready, q - 1)
                    nc.scalar.activation(hT[k % 2][:, 0], bank[4 + k % 2][:].rearrange("p (c t) -> p c t", c=KT), ACT.Copy).then_inc(hT_high, 1)

                def gelu(i, k):
                    i, k = i + k // 8, k % 8
                    q = i * 8 + k
                    act.wait_ge(h_ready, q + 1)
                    wait(act, hT_ready, q - 1)
                    nc.scalar.activation(h_sb[k % 2], bank[2 + k % 2][:], ACT.Gelu, scale=1.0 / WSCALE).then_inc(gelu_done, 1)

                x_high(0, 0)

                def ordered(i, k):
                    if not (isinstance(i, int) and i * 8 + k == 0):
                        h_high(i, k - 1)
                    if not (isinstance(i, int) and i * 8 + k == Q - 1):
                        x_high(i, k + 1)
                    gelu(i, k)
                turns_all(act, ordered)
                h_high(0, Q - 1)

            @block.vector
            def _(dve):
                for n, m in enumerate(late):
                    dve.wait_ge(raw_high, n + 1)
                    nc.vector.scalar_tensor_tensor(experts[:, m, 1], raw[n].rearrange("p (a c) -> p a c", a=KT), WSCALE,
                                                   experts[:, m, 0], ALU.mult, ALU.subtract).then_inc(raw_low, 1)

                def x_low(i, k):
                    i, k = i + k // 8, k % 8
                    q = i * 8 + k
                    dve.wait_ge(xT_high, q + 1)
                    nc.vector.tensor_tensor(xT[k % 2][:, 1], bank[k % 2][:].rearrange("p (c t) -> p c t", c=KT), xT[k % 2][:, 0],
                                            ALU.subtract).then_inc(xT_low, 1)

                def h_low(i, k):
                    i, k = i + k // 8, k % 8
                    q = i * 8 + k
                    dve.wait_ge(hT_high, q + 1)
                    nc.vector.tensor_tensor(hT[k % 2][:, 1], bank[4 + k % 2][:].rearrange("p (c t) -> p c t", c=KT), hT[k % 2][:, 0],
                                            ALU.subtract).then_inc(hT_low, 1)

                def y_out(i, k):
                    i, k = i + k // 8, k % 8
                    q = i * 8 + k
                    dve.wait_ge(y_ready, q + 1)
                    wait(dve, added, q * 16 - 16)
                    nc.vector.tensor_scalar(y_sb[k % 2], bank[6 + k % 2][:], rows[:, k, 1:2].bitcast(F32), 1.0 / WSCALE,
                                            ALU.mult, ALU.mult).then_inc(y_done, 1)

                x_low(0, 0)

                def ordered(i, k):
                    if not (isinstance(i, int) and i * 8 + k == 0):
                        h_low(i, k - 1)
                    if not (isinstance(i, int) and i * 8 + k == Q - 1):
                        x_low(i, k + 1)
                    if not (isinstance(i, int) and i * 8 + k < 2):
                        y_out(i, k - 2)
                turns_all(dve, ordered)
                y_out(0, Q - 2)
                h_low(0, Q - 1)
                y_out(0, Q - 1)

            @block.tensor
            def _(pe):
                def x_transposes(i, k):
                    i, k = i + k // 8, k % 8
                    q = i * 8 + k
                    pe.wait_ge(gathered[k % AHEAD], i * (16 * 8 // AHEAD) + (k // AHEAD) * 16 + 16)
                    wait(pe, xT_low, q - 1)
                    for c in range(KT):
                        last = nc.tensor.transpose(bank[k % 2][:, c * P:c * P + P], xg[k % AHEAD][:, c * P:c * P + P], ident[:])
                    last.then_inc(xT_ready, 1)

                def h_transposes(i, k):
                    i, k = i + k // 8, k % 8
                    q = i * 8 + k
                    pe.wait_ge(gelu_done, q + 1)
                    wait(pe, hT_low, q - 1)
                    for c in range(KT):
                        last = nc.tensor.transpose(bank[4 + k % 2][:, c * P:c * P + P], h_sb[k % 2][:, c * P:c * P + P], ident[:])
                    last.then_inc(hT_ready, 1)

                def expert_product(q, bank_, lhs, second):
                    e = pe.value_load(tile_expert[0:1, bass.ds(q, 1)], min_val=0, max_val=NE - 1)

                    def w(h, c):
                        return experts[:, bass.ds(e * 2 + second, 1), h, c].rearrange("p o n -> p (o n)")
                    for c in range(KT):
                        nc.tensor.matmul(bank_[:], lhs[:, 0, c], w(0, c), start=(c == 0), stop=False)
                        nc.tensor.matmul(bank_[:], lhs[:, 0, c], w(1, c), start=False, stop=False)
                        last = nc.tensor.matmul(bank_[:], lhs[:, 1, c], w(0, c), start=False, stop=(c == KT - 1))
                    return last

                def hidden(i, k):
                    i, k = i + k // 8, k % 8
                    q = i * 8 + k
                    wait(pe, gelu_done, q - 1)
                    wait_apart(pe, xT_low, q + 1, pe_waits)
                    expert_product(q, bank[2 + k % 2], xT[k % 2], 0).then_inc(h_ready, 1)

                def result(i, k):
                    i, k = i + k // 8, k % 8
                    q = i * 8 + k
                    wait(pe, y_done, q - 1)
                    wait_apart(pe, hT_low, q + 1, pe_waits)
                    expert_product(q, bank[6 + k % 2], hT[k % 2], 1).then_inc(y_ready, 1)

                pe.wait_ge(made, 2)
                pe.wait_ge(raw_low, len(late))
                x_transposes(0, 0)

                def ordered(i, k):
                    hidden(i, k)
                    if not (isinstance(i, int) and i * 8 + k == 0):
                        h_transposes(i, k - 1)
                    if not (isinstance(i, int) and i * 8 + k == Q - 1):
                        x_transposes(i, k + 1)
                    if not (isinstance(i, int) and i * 8 + k < 2):
                        result(i, k - 2)
                turns_all(pe, ordered)
                result(0, Q - 2)
                h_transposes(0, Q - 1)
                result(0, Q - 1)


def shape_constants():
    import numpy as np
    return np.concatenate([np.arange(NE), P * np.arange(TILES), np.arange(SLOT_TILES)]).astype(np.float32)[None]


def build_program(nc, out, in_x, in_ctx, in_basisT, in_core, in_coreT, in_head_res, in_wvT, in_bv, in_woT, in_bo, in_xwqT,
                  in_xbq, in_xwkT, in_xbk, in_xwvT, in_xbv, in_xwoT, in_xbo, in_rwT, in_r_bias, in_sw1, in_sw3, in_sw2,
                  in_ew1, in_ew2, in_constants):
    with ExitStack() as ctx:
        def sem(name):
            return ctx.enter_context(nc.semaphore(name))

        x2 = nc.dram_tensor("x2", (N, C), F32, kind="Internal").ap()
        xn = nc.dram_tensor("xn3", (N + P, C), F32, kind="Internal").ap()
        slots = nc.dram_tensor("slot_table", (SLOT_TILES * P, 2), mybir.dt.int32, kind="Internal").ap()
        build_attention(nc, sem, in_x, in_ctx, (in_basisT, in_core, in_coreT, in_head_res, in_wvT, in_bv, in_woT, in_bo,
                                                in_xwqT, in_xbq, in_xwkT, in_xbk, in_xwvT, in_xbv, in_xwoT, in_xbo), x2)
        build_ffn(nc, sem, x2, out, in_rwT, in_r_bias, in_sw1, in_sw3, in_sw2, in_ew1, in_ew2, in_constants, xn, slots)


def kernel(**inputs):
    import numpy as _np
    import concourse.bacc as _bacc
    from concourse import mybir as _mybir
    from concourse.bass_utils import run_bass_kernel_spmd as _run

    nc = _bacc.Bacc("TRN2", target_bir_lowering=False, num_devices=1)
    i = {k: _np.asarray(v) for k, v in inputs.items()}
    columns = lambda v: v.reshape(NG, P).T
    arrays = {
        "x": i["x"], "ctx": i["ctx_1024"], "basisT": i["L0_attn_basis_w"].T, "core": i["L0_attn_core"],
        "coreT": i["L0_attn_core"].T, "head_res": i["L0_attn_head_residual"], "wvT": i["L0_attn_v_w"].T,
        "bv": i["L0_attn_v_b"], "woT": i["L0_attn_o_w"].T, "bo": i["L0_attn_o_b"], "xwqT": i["L0_xattn_Wq"].T,
        "xbq": columns(i["L0_xattn_bq"]), "xwkT": i["L0_xattn_Wk"].T, "xbk": columns(i["L0_xattn_bk"]),
        "xwvT": i["L0_xattn_Wv"].T, "xbv": i["L0_xattn_bv"], "xwoT": i["L0_xattn_Wo"].T, "xbo": i["L0_xattn_bo"],
        "rwT": i["L0_ffn_router_w"].T, "r_bias": i["L0_ffn_router_bias"], "sw1": i["L0_ffn_sw1"],
        "sw3": i["L0_ffn_sw3"], "sw2": i["L0_ffn_sw2"], "ew1": i["L0_ffn_ew1"], "ew2": i["L0_ffn_ew2"],
        "constants": shape_constants(),
    }
    arrays = {"in_" + k: _np.ascontiguousarray(v) for k, v in arrays.items()}
    args = {k: nc.dram_tensor(k, v.shape, _mybir.dt.from_np(v.dtype), kind="ExternalInput").ap() for k, v in arrays.items()}
    out = nc.dram_tensor("out_0", (N + P, C), F32, kind="ExternalOutput").ap()
    build_program(nc, out, **args)
    r = _run(nc, [arrays], core_ids=[0])
    return r.results[0]["out_0"][:N].reshape(B, T, C)
```

```python
from contextlib import ExitStack

import concourse.bass as bass
from concourse import mybir

ALU = mybir.AluOpType
ACT = mybir.ActivationFunctionType
F32 = mybir.dt.float32
F16 = mybir.dt.float16
AX_X = mybir.AxisListType.X

P = 128
B, T, C = 8, 512, 512
TT = T // P
KT = C // P
H, R, HD = 16, 64, 32
S = 77
HG = P // HD
NG = H // HG
VW = HD + 1
WSCALE = 32.0
MSCALE = 64.0
BIG = 60000.0
EPS = 1e-5
XSCALE = float(HD) ** -0.5 / (WSCALE * WSCALE)
NE = 8
STEPS = 2 * TT


def wait(eng, s, value):
    if not isinstance(value, int) or value > 0:
        eng.wait_ge(s, value)


def wait_apart(eng, s, value, passed):
    eng.wait_ge(s, value)
    eng.sem_inc(passed, 1)


UNSPLIT = ("k", "o", "cs", "cy", "xo", "logits")


def rest_jobs():
    jobs = [(2, ("yT", 0)), (2, ("yT", 1)), (3, ("yT", 2)), (3, ("yT", 3)),
            (5, ("o", 0)), (6, ("o", 1)), (7, ("o", 2)), (8, ("o", 3)),
            (9, ("ctxT", 0)), (10, ("k", 0)), (11, ("cv", 0)),
            (13, ("x2T", 0)), (14, ("x2T", 1)), (14, ("x2T", 2)), (15, ("x2T", 3)),
            (16, ("q", 0)), (17, ("q", 1)), (18, ("q", 2)), (19, ("q", 3)),
            (20, ("cs", 0)), (20, ("cs", 1)), (21, ("cs", 2)), (22, ("cs", 3))]
    for t in range(TT):
        s = 24 + 6 * t
        places = [(0, ("cpT", 4 * t)), (0, ("cpT", 4 * t + 1)), (2, ("cy", 2 * t)), (2, ("cpT", 4 * t + 2)),
                  (3, ("cpT", 4 * t + 3)), (5, ("cy", 2 * t + 1))]
        if t + 1 < TT:
            places += [(1, ("cs", 4 * t + 4)), (1, ("cs", 4 * t + 5)), (3, ("cs", 4 * t + 6)), (4, ("cs", 4 * t + 7))]
        jobs += [(s + k, j) for k, j in places]
    jobs += [(49, ("y2T", 0)), (50, ("y2T", 1)), (50, ("y2T", 2)), (51, ("y2T", 3)),
             (52, ("xo", 0)), (53, ("xo", 1)), (54, ("xo", 2)), (55, ("xo", 3)),
             (59, ("x3T", 0)), (59, ("x3T", 1)), (60, ("x3T", 2)), (60, ("x3T", 3)), (62, ("logits", 0))]
    return sorted(jobs, key=lambda j: j[0])


REST = rest_jobs()
AHEAD_JOBS = [(56, ("x1T", 0)), (56, ("x1T", 1)), (58, ("x1T", 2)), (58, ("x1T", 3))]
K_LOW_STEP, XN2_STEP, XN3_STEP = 14, 12, 58
LN1_STEPS, XN1_STEP = (45, 46, 47, 48), 51


def build_attention(nc, sem, x, ctx_in, weights, rwT, logits, x2_dram, xn_dram, xT_dram):
    basisT, core, coreT, head_res, wvT, bv, woT, bo, xwqT, xbq, xwkT, xbk, xwvT, xbv, xwoT, xbo = weights
    with ExitStack() as keep:
        def sb(name, shape, dt):
            return keep.enter_context(nc.sbuf_tensor(name, shape, dt))

        w_names = ["wv", "wo", "xwq", "xwk", "xwv", "xwo"]
        W = {n: sb(n, [P, 2, KT, C], F16) for n in w_names}
        w_basis = sb("w_basis", [P, 2, KT, P], F16)
        head_mat = sb("head_mat", [P, H, P], F16)
        ident = sb("ident", [P, P], F32)
        big_ident = sb("big_ident", [P, P], F16)
        causal = sb("causal", [P, P], F16)
        vb_row = sb("vb_row", [P, C], F32)
        ob_row = sb("ob_row", [P, C], F32)
        xvb_row = sb("xvb_row", [P, C], F32)
        xob_row = sb("xob_row", [P, C], F32)
        q_bias = sb("q_bias", [P, NG], F32)
        k_bias = sb("k_bias", [P, NG], F32)
        neg_half = sb("neg_half", [P, TT], F32)
        router = sb("router", [P, 2, KT, NE], F16)

        with ExitStack() as prep:
            def tmp(name, shape, dt):
                return prep.enter_context(nc.sbuf_tensor(name, shape, dt))

            raw = {n: tmp("raw_" + n, [P, KT, C], F32) for n in w_names}
            raw_basis = tmp("raw_basis", [P, KT, R], F32)
            raw_router = tmp("raw_router", [P, KT, NE], F32)
            raw_heads = tmp("raw_heads", [P, H, R], F32)
            raw_core = tmp("raw_core", [P, 2, R], F32)
            head_sum = tmp("head_sum", [P, R], F32)
            core_sum = tmp("core_sum", [P, R], F32)
            shared = tmp("shared", [P, R], F32)
            w_loaded = {n: sem("loaded_" + n) for n in w_names}
            small_loaded, bias_loaded = sem("small_loaded"), sem("bias_loaded")
            w_high, w_low = sem("w_high"), sem("w_low")
            pool_made, head_step, head_high = sem("pool_made"), sem("head_step"), sem("head_high")
            bias_scaled = sem("bias_scaled")
            with nc.Block() as block:
                @block.sync
                def _(sp):
                    for half in (0, R):
                        sp.dma_start(raw_heads[half:half + R], head_res.rearrange("h r s -> r h s")).then_inc(small_loaded, 16)
                        sp.dma_start(raw_core[half:half + R, 0, :], core).then_inc(small_loaded, 16)
                        sp.dma_start(raw_core[half:half + R, 1, :], coreT).then_inc(small_loaded, 16)
                    sp.dma_start(raw_basis[:], basisT.rearrange("(a p) n -> p a n", p=P)).then_inc(small_loaded, 16)
                    sp.dma_start(raw_router[:], rwT.rearrange("(a p) n -> p a n", p=P)).then_inc(small_loaded, 16)
                    for n, src in zip(w_names, (wvT, woT, xwqT, xwkT, xwvT, xwoT)):
                        sp.dma_start(raw[n][:], src.rearrange("(a p) n -> p a n", p=P)).then_inc(w_loaded[n], 16)
                    for dst, src in ((vb_row, bv), (ob_row, bo), (xvb_row, xbv), (xob_row, xbo)):
                        sp.dma_start(dst[:], src.rearrange("(a n) -> a n", a=1).broadcast_to([P, C])).then_inc(bias_loaded, 16)
                    for dst, src in ((q_bias, xbq), (k_bias, xbk)):
                        sp.dma_start(dst[:], src).then_inc(bias_loaded, 16)

                @block.gpsimd
                def _(pool):
                    nc.gpsimd.memset(neg_half[:], -0.5).then_inc(pool_made, 1)
                    nc.gpsimd.memset(ident[:], 0.0).then_inc(pool_made, 1)
                    nc.gpsimd.memset(big_ident[:], 0.0).then_inc(pool_made, 1)
                    nc.gpsimd.memset(causal[:], 0.0).then_inc(pool_made, 1)
                    pool.wait_ge(pool_made, 4)
                    for t, value in ((ident, 1.0), (big_ident, BIG)):
                        nc.gpsimd.affine_select(out=t[:], in_=t[:], compare_op=ALU.not_equal, fill=value, base=0,
                                                pattern=[[-1, P]], channel_multiplier=1).then_inc(pool_made, 1)
                    nc.gpsimd.affine_select(out=causal[:], in_=causal[:], compare_op=ALU.is_ge, fill=-BIG, base=0,
                                            pattern=[[-1, P]], channel_multiplier=1).then_inc(pool_made, 1)
                    pool.wait_ge(bias_loaded, 16 * 6)
                    for t in (q_bias, k_bias):
                        nc.gpsimd.tensor_scalar(t[:], t[:], WSCALE, None, ALU.mult).then_inc(bias_scaled, 1)

                @block.scalar
                def _(act):
                    act.wait_ge(small_loaded, 16 * 8)
                    for half in range(2):
                        nc.scalar.activation(w_basis[:, 0, :, half * R:half * R + R], raw_basis[:], ACT.Copy,
                                             scale=WSCALE).then_inc(w_high, 1)
                    nc.scalar.activation(router[:, 0], raw_router[:], ACT.Copy, scale=WSCALE).then_inc(w_high, 1)
                    act.wait_ge(head_step, 6)
                    nc.scalar.activation(head_mat[:, :, 0:R], raw_heads[:], ACT.Copy, scale=MSCALE).then_inc(head_high, 1)
                    for n in w_names:
                        act.wait_ge(w_loaded[n], 16)
                        nc.scalar.activation(W[n][:, 0], raw[n][:], ACT.Copy, scale=WSCALE).then_inc(w_high, 1)

                @block.vector
                def _(dve):
                    dve.wait_ge(small_loaded, 16 * 8)
                    nc.vector.tensor_reduce(head_sum[:], raw_heads[:].rearrange("p h s -> p s h"), AX_X,
                                            ALU.add).then_inc(head_step, 1)
                    nc.vector.tensor_tensor(core_sum[:], raw_core[:, 0], raw_core[:, 1], ALU.add).then_inc(head_step, 1)
                    dve.wait_ge(head_step, 2)
                    nc.vector.tensor_scalar(core_sum[:], core_sum[:], 0.5 / H, None, ALU.mult).then_inc(head_step, 1)
                    nc.vector.tensor_scalar(head_sum[:], head_sum[:], 1.0 / H, None, ALU.mult).then_inc(head_step, 1)
                    dve.wait_ge(head_step, 4)
                    nc.vector.tensor_tensor(shared[:], core_sum[:], head_sum[:], ALU.subtract).then_inc(head_step, 1)
                    dve.wait_ge(head_step, 5)
                    nc.vector.tensor_tensor(raw_heads[:], raw_heads[:],
                                            shared[:].unsqueeze(1).broadcast_to([P, H, R]), ALU.add).then_inc(head_step, 1)
                    for half in range(2):
                        dve.wait_ge(w_high, half + 1)
                        cols = slice(half * R, half * R + R)
                        nc.vector.scalar_tensor_tensor(w_basis[:, 1, :, cols], raw_basis[:], WSCALE,
                                                       w_basis[:, 0, :, cols], ALU.mult, ALU.subtract).then_inc(w_low, 1)
                    dve.wait_ge(w_high, 3)
                    nc.vector.scalar_tensor_tensor(router[:, 1], raw_router[:], WSCALE, router[:, 0],
                                                   ALU.mult, ALU.subtract).then_inc(w_low, 1)
                    dve.wait_ge(head_step, 6)
                    dve.wait_ge(head_high, 1)
                    nc.vector.scalar_tensor_tensor(head_mat[R:P, :, 0:R], raw_heads[R:P], MSCALE,
                                                   head_mat[R:P, :, 0:R], ALU.mult, ALU.subtract).then_inc(head_step, 1)
                    dve.wait_ge(head_step, 7)
                    nc.vector.tensor_copy(head_mat[:, :, R:P], head_mat[:, :, 0:R]).then_inc(head_step, 1)
                    for k, n in enumerate(w_names):
                        dve.wait_ge(w_high, 4 + k)
                        nc.vector.scalar_tensor_tensor(W[n][:, 1], raw[n][:], WSCALE, W[n][:, 0],
                                                       ALU.mult, ALU.subtract).then_inc(w_low, 1)

        x_in = sb("x_in", [P, TT, C], F32)
        x_res = sb("x_res", [P, TT, C], F32)
        xn = sb("xn", [P, TT, C], F32)
        ctx_sb = sb("ctx_sb", [S, C], F32)
        stats = sb("stats", [P, 3, TT, 6], F32)
        moments = sb("moments", [P, 3, TT, 2], F32)
        rstd = sb("rstd", [P, 3, TT], F32)
        shift = sb("shift", [P, 3, TT], F32)
        x1T = sb("x1T", [P, 2, KT, T], F16)
        xT = sb("xT", [P, 2, KT, T], F16)
        latent = sb("latent", [P, 2, T], F16)
        values = sb("values", [P, 2, TT, H, VW], F16)
        left = sb("left", [P, 2, T], F16)
        neg_max = sb("neg_max", [P, STEPS], F32)
        probs = sb("probs", [P, TT, T], F32)
        probsT = sb("probsT", [P, 4, 2, T], F16)
        sums = sb("sums", [P, 2, TT], F32)
        y = sb("y", [P, TT, C], F32)
        yT = sb("yT", [P, 2, KT, T], F16)
        qT = sb("qT", [P, 2, NG, T], F16)
        ctxT = sb("ctxT", [P, 2, KT, S], F16)
        k_sum = sb("k_sum", [P, NG, S], F32)
        k_diag = sb("k_diag", [P, 2, NG, HG * S], F16)
        c_values = sb("c_values", [S, 2, H, VW], F16)
        c_max = sb("c_max", [P, 2, H], F32)
        c_probs = sb("c_probs", [P, 2, H, S], F32)
        c_probsT = sb("c_probsT", [S, NG, 2, HG * P], F16)
        c_sums = sb("c_sums", [P, 2, H], F32)
        score_bank = [keep.enter_context(nc.psum_tensor(f"score_bank{i}", [P, 512], F32)) for i in range(2)]
        probsT_bank = [keep.enter_context(nc.psum_tensor(f"probsT_bank{i}", [P, 512], F32)) for i in range(2)]
        y_bank = keep.enter_context(nc.psum_tensor("y_bank", [P, 512], F32))
        job_bank = [keep.enter_context(nc.psum_tensor(f"job_bank{i}", [P, 512], F32)) for i in range(3)]

        x_loaded, res_loaded, ctx_loaded = sem("x_loaded"), sem("res_loaded"), sem("ctx_loaded")
        x2_stored, xn_stored, xT_stored = sem("x2_stored"), sem("xn_stored"), sem("xT_stored")
        ln_stats, ln_moments, ln_pool, ln_scale, ln_done = (
            [sem(f"{name}{n + 1}") for n in range(3)] for name in ("ln_stats", "ln_moments", "ln_pool", "ln_scale", "ln_done"))
        stores_passed = sem("stores_passed")
        ones_set = sem("ones_set")
        dve_waits, pool_waits = sem("dve_waits"), sem("pool_waits")
        scores_ready, max_done, exp_done = sem("scores_ready"), sem("max_done"), sem("exp_done")
        pT_ready, pT_high, pT_low = sem("pT_ready"), sem("pT_high"), sem("pT_low")
        y_ready, sums_done, y_normed, y_biased = sem("y_ready"), sem("sums_done"), sem("y_normed"), sem("y_biased")
        job_ready, job_high, job_done = sem("job_ready"), sem("job_high"), sem("job_done")
        res_biased, x1_biased = sem("res_biased"), sem("x1_biased")
        k_high, k_low = sem("k_high"), sem("k_low")
        c_max_done, c_exp_done, c_sums_done, cy_biased = sem("c_max_done"), sem("c_exp_done"), sem("c_sums_done"), sem("cy_biased")

        x_v = x.rearrange("b (a p) c -> b p a c", p=P)
        x2_v = x2_dram.rearrange("(b a p) c -> b p a c", p=P, a=TT)
        xn_v = xn_dram[0:B * T].rearrange("(b a p) c -> b p a c", p=P, a=TT)

        def of_batch(v, b, names):
            return v[b] if isinstance(b, int) else v[bass.ds(b, 1)].rearrange(f"o {names} -> (o {names.split()[0]}) " + " ".join(names.split()[1:]))

        def low(out, in_, scale, high):
            return nc.vector.scalar_tensor_tensor(out, in_, scale, high, ALU.mult, ALU.subtract)

        def jobs_of(heads, rest, ahead):
            before = [("latent", 0), ("v", 0), ("left", 0), ("v", 1), ("v", 2), ("v", 3)] if heads else []
            steps = {k: [] for k in range(H * TT)}
            if rest:
                for k, job in REST:
                    steps[k].append(job)
            if ahead:
                for k, job in AHEAD_JOBS:
                    steps[k].append(job)
            if heads:
                for h in range(1, H):
                    k = min((TT * h - 3, TT * h - 4, TT * h - 5, TT * h - 2), key=lambda k: len(steps[k]) // 2 if k >= 0 else 9)
                    steps[k].append(("left", h))
            assert all(len(v) <= 2 for v in steps.values()), {k: v for k, v in steps.items() if len(v) > 2}
            return before, steps

        class Turn:
            def __init__(self, b, heads, rest, ahead, jobs_before, high_before):
                self.b, self.heads, self.rest, self.ahead = b, heads, rest, ahead
                self.before, self.steps = jobs_of(heads, rest, ahead)
                self.order = self.before + [j for k in sorted(self.steps) for j in self.steps[k]]
                self.high_order = [j for j in self.order if j[0] not in UNSPLIT]
                self.jobs, self.highs = jobs_before, high_before
                self.g = b * (H * TT)

            def number(self, job):
                return self.order.index(job)

            def done(self, job):
                return self.jobs + self.number(job) + 1

            def high(self, job):
                return self.highs + self.high_order.index(job) + 1

            def bank(self, job):
                return job_bank[self.number(job) % 3]

            def bank_free(self, job):
                n = self.number(job)
                return self.jobs + (n - 2 if n >= 3 else 0)

        def turns(eng, body):
            n_first, h_first = count_jobs(jobs_of(True, False, True))
            n_full, h_full = count_jobs(jobs_of(True, True, True))
            n_last, h_last = count_jobs(jobs_of(True, True, False))
            body(Turn(0, True, False, True, KT, KT))
            with eng.Fori(1, B - 1) as b:
                body(Turn(b, True, True, True, (b - 1) * n_full + (KT + n_first), (b - 1) * h_full + (KT + h_first)))
            n, h = KT + n_first + (B - 2) * n_full, KT + h_first + (B - 2) * h_full
            body(Turn(B - 1, True, True, False, n, h))
            body(Turn(B, False, True, False, n + n_last, h + h_last))

        def count_jobs(jobs):
            order = jobs[0] + [j for v in jobs[1].values() for j in v]
            return len(order), sum(j[0] not in UNSPLIT for j in order)

        class Start:
            order = high_order = [("x1T", c) for c in range(KT)]
            jobs = highs = 0
            b = -1
            number, done, high, bank, bank_free = Turn.number, Turn.done, Turn.high, Turn.bank, Turn.bank_free

        start = Start()

        with nc.Block() as block:
            @block.sync
            def _(sp):
                def load_x(b, names="p a c"):
                    sp.dma_start(x_in[:], of_batch(x_v, b, "p a c")).then_inc(x_loaded, 16)

                load_x(0)
                sp.sem_inc(stores_passed, 1)

                def body(t):
                    b = t.b
                    if t.ahead:
                        prev = start.done(("x1T", KT - 1)) if isinstance(b, int) else None
                        sp.wait_ge(job_ready, prev if prev is not None else t.jobs)
                        load_x(b + 1)
                    if t.rest:
                        sp.dma_start(x_res[:], of_batch(x_v, b - 1, "p a c")).then_inc(res_loaded, 16)
                        if not (isinstance(b, int) and b == 1):
                            sp.wait_ge(job_ready, t.jobs)
                        sp.dma_start(ctx_sb[:], of_batch(ctx_in, b - 1, "s c")).then_inc(ctx_loaded, 16)
                        sp.wait_ge(job_done, t.done(("xo", TT - 1)))
                        sp.dma_start(of_batch(x2_v, b - 1, "p a c"), x_res[:]).then_inc(x2_stored, 16)
                        sp.wait_ge(ln_done[2], b * TT)
                        sp.dma_start(of_batch(xn_v, b - 1, "p a c"), xn[:]).then_inc(xn_stored, 16)
                        sp.wait_ge(job_done, t.done(("x3T", KT - 1)))
                        sp.dma_start(of_batch(xT_dram, b - 1, "p n"), xT[:].rearrange("p h c t -> p (h c t)")).then_inc(xT_stored, 16)
                        for s in (x2_stored, xn_stored, xT_stored):
                            sp.wait_ge(s, b * 16)
                        sp.sem_inc(stores_passed, 1)

                turns(sp, body)

            @block.gpsimd
            def _(pool):
                for t, value in ((values, WSCALE), (c_values, WSCALE)):
                    nc.gpsimd.memset(t[:], 0.0).then_inc(ones_set, 1)
                nc.gpsimd.memset(k_diag[:], 0.0).then_inc(ones_set, 1)
                pool.wait_ge(ones_set, 3)
                nc.gpsimd.memset(values[:, 0, :, :, HD:VW], WSCALE).then_inc(ones_set, 1)
                nc.gpsimd.memset(c_values[:, 0, :, HD:VW], WSCALE).then_inc(ones_set, 1)

                def scale_of(n, i):
                    wait_apart(pool, ln_moments[n], i * TT + TT, pool_waits)
                    nc.gpsimd.tensor_scalar(rstd[:, n], moments[:, n, :, 1], 1.0, EPS, ALU.mult, ALU.add).then_inc(ln_pool[n], 1)
                    pool.wait_ge(ln_pool[n], i * 3 + 1)
                    nc.gpsimd.tensor_tensor(rstd[:, n], rstd[:, n], neg_half[:], ALU.pow).then_inc(ln_pool[n], 1)
                    pool.wait_ge(ln_pool[n], i * 3 + 2)
                    nc.gpsimd.tensor_tensor(shift[:, n], moments[:, n, :, 0], rstd[:, n], ALU.mult).then_inc(ln_pool[n], 1)
                    wait_apart(pool, ln_pool[n], i * 3 + 3, pool_waits)
                    nc.gpsimd.tensor_scalar(shift[:, n], shift[:, n], -1.0, 0.0, ALU.mult, ALU.add).then_inc(ln_scale[n], 1)

                def add_cross_bias(t, tile):
                    pool.wait_ge(job_done, t.done(("cy", tile * 2 + 1)))
                    nc.gpsimd.tensor_tensor(xn[:, tile], xn[:, tile], xvb_row[:], ALU.add).then_inc(cy_biased, 1)

                scale_of(0, 0)

                def body(t):
                    b = t.b
                    if t.rest:
                        pool.wait_ge(y_normed, b * H)
                        for tile in range(TT):
                            nc.gpsimd.tensor_tensor(y[:, tile], y[:, tile], vb_row[:], ALU.add).then_inc(y_biased, 1)
                        pool.wait_ge(res_loaded, b * 16)
                        for tile in range(TT):
                            nc.gpsimd.tensor_tensor(x_res[:, tile], x_res[:, tile], ob_row[:], ALU.add).then_inc(res_biased, 1)
                        scale_of(1, b - 1)
                        pool.wait_ge(ln_done[1], b * TT)
                        for tile in range(TT):
                            nc.gpsimd.tensor_tensor(x_res[:, tile], x_res[:, tile], xob_row[:], ALU.add).then_inc(x1_biased, 1)
                        for tile in range(TT):
                            add_cross_bias(t, tile)
                    if t.ahead:
                        scale_of(0, b + 1)
                    if t.rest:
                        scale_of(2, b - 1)

                turns(pool, body)

            @block.scalar
            def _(act):
                def copy_high(out, in_, scale=1.0):
                    return nc.scalar.activation(out, in_, ACT.Copy, scale=scale)

                def job(t, name, i):
                    if name in UNSPLIT:
                        if name == "cs" and i % NG == NG - 1:
                            pass
                        return
                    if name == "cpT" and i % NG == 0:
                        pass
                    act.wait_ge(job_ready, t.done((name, i)))
                    src = t.bank((name, i))
                    if name == "latent":
                        ins = copy_high(latent[:, 0], src[:], 0.25 / WSCALE)
                    elif name == "v":
                        ins = copy_high(values[:, 0, i, :, 0:HD], src[:].rearrange("p (h d) -> p h d", h=H))
                    elif name == "left":
                        ins = copy_high(left[:, i % 2], src[:], 0.5 / 16)
                    elif name == "x1T":
                        ins = copy_high(x1T[:, 0, i], src[:])
                    elif name == "x2T":
                        if i == 0:
                            act.wait_ge(stores_passed, t.b)
                        ins = copy_high(xT[:, 0, i], src[:])
                    elif name == "x3T":
                        ins = copy_high(xT[:, 0, i], src[:])
                    elif name in ("yT", "y2T"):
                        ins = copy_high(yT[:, 0, i], src[:])
                    elif name == "ctxT":
                        ins = copy_high(ctxT[:, 0], src[:, 0:KT * S].rearrange("p (c s) -> p c s", c=KT))
                    elif name == "cv":
                        ins = copy_high(c_values[:, 0, :, 0:HD], src[0:S].rearrange("p (h d) -> p h d", h=H))
                    elif name == "q":
                        ins = nc.scalar.activation(qT[:, 0, i], src[:], ACT.Identity, bias=q_bias[:, i:i + 1], scale=1.0)
                    elif name == "cpT":
                        ins = copy_high(c_probsT[:, i % NG, 0], src[0:S])
                    ins.then_inc(job_high, 1)

                def after_job(t, name, i):
                    if name == "k":
                        act.wait_ge(job_done, t.done((name, i)))
                        for j in range(HG):
                            rows = slice(j * HD, j * HD + HD)
                            copy_high(k_diag[rows, 0, :, j * S:j * S + S], k_sum[rows]).then_inc(k_high, 1)
                    if name == "cs" and i % NG == NG - 1:
                        act.wait_ge(job_done, t.done((name, i)))
                        tile = i // NG
                        nc.scalar.activation(c_probs[:, tile % 2], c_probs[:, tile % 2], ACT.Exp, scale=XSCALE).then_inc(c_exp_done, 1)

                def probs_high(t, j):
                    n = (j % TT + 1) * P
                    act.wait_ge(pT_ready, t.g + j + 1)
                    if j >= 4:
                        act.wait_ge(y_ready, t.g + j - 3)
                    copy_high(probsT[:, j % 4, 0, 0:n], probsT_bank[j % 2][:, 0:n]).then_inc(pT_high, 1)

                def exp_tile(t, k):
                    n = (k % TT + 1) * P
                    act.wait_ge(max_done, t.g + k + 1)
                    nc.scalar.activation(probs[:, k % TT, 0:n], score_bank[k % 2][:, 0:n], ACT.Exp,
                                         bias=neg_max[:, k % STEPS:k % STEPS + 1], scale=1.0).then_inc(exp_done, 1)

                def body(t):
                    for j in t.before:
                        job(t, *j)
                    for k in range(H * TT + 2):
                        for j in t.steps.get(k - 2, []):
                            after_job(t, *j)
                        for j in t.steps.get(k - 1, []):
                            job(t, *j)
                        if t.heads and 1 <= k <= H * TT:
                            exp_tile(t, k - 1)
                        if t.heads and k >= 2:
                            probs_high(t, k - 2)

                act.wait_ge(ones_set, 5)
                for c in range(KT):
                    job(start, "x1T", c)
                turns(act, body)

            @block.vector
            def _(dve):
                def moments_of(n, i, tile, src):
                    nc.vector.bn_stats(stats[:, n, tile], src[:, tile]).then_inc(ln_stats[n], 1)
                    wait_apart(dve, ln_stats[n], i * TT + tile + 1, dve_waits)
                    nc.vector.bn_aggr(moments[:, n, tile], stats[:, n, tile]).then_inc(ln_moments[n], 1)

                def normalise(n, i, out, src):
                    dve.wait_ge(ln_scale[n], i + 1)
                    for tile in range(TT):
                        nc.vector.tensor_scalar(out[:, tile], src[:, tile], rstd[:, n, tile:tile + 1], shift[:, n, tile:tile + 1],
                                                ALU.mult, ALU.add).then_inc(ln_done[n], 1)

                def job(t, name, i):
                    src = t.bank((name, i))
                    if name in UNSPLIT:
                        dve.wait_ge(job_ready, t.done((name, i)))
                    else:
                        dve.wait_ge(job_high, t.high((name, i)))
                    if name == "latent":
                        ins = low(latent[:, 1], src[:], 0.25 / WSCALE, latent[:, 0])
                    elif name == "v":
                        ins = low(values[:, 1, i, :, 0:HD], src[:].rearrange("p (h d) -> p h d", h=H), 1.0, values[:, 0, i, :, 0:HD])
                    elif name == "left":
                        ins = low(left[R:P, i % 2], src[R:P], 0.5 / 16, left[R:P, i % 2])
                    elif name == "x1T":
                        ins = low(x1T[:, 1, i], src[:], 1.0, x1T[:, 0, i])
                    elif name in ("x2T", "x3T"):
                        ins = low(xT[:, 1, i], src[:], 1.0, xT[:, 0, i])
                    elif name in ("yT", "y2T"):
                        ins = low(yT[:, 1, i], src[:], 1.0, yT[:, 0, i])
                    elif name == "ctxT":
                        ins = low(ctxT[:, 1], src[:, 0:KT * S].rearrange("p (c s) -> p c s", c=KT), 1.0, ctxT[:, 0])
                    elif name == "k":
                        ins = nc.vector.tensor_tensor(k_sum[:], src[:, 0:NG * S].rearrange("p (c s) -> p c s", c=NG),
                                                      k_bias[:].unsqueeze(2).broadcast_to([P, NG, S]), ALU.add)
                    elif name == "cv":
                        ins = low(c_values[:, 1, :, 0:HD], src[0:S].rearrange("p (h d) -> p h d", h=H), 1.0, c_values[:, 0, :, 0:HD])
                    elif name == "o":
                        dve.wait_ge(res_biased, (t.b - 1) * TT + i + 1)
                        ins = nc.vector.scalar_tensor_tensor(x_res[:, i], src[:], 1.0 / WSCALE, x_res[:, i], ALU.mult, ALU.add)
                    elif name == "q":
                        ins = nc.vector.scalar_tensor_tensor(qT[:, 1, i], src[:], q_bias[:, i:i + 1], qT[:, 0, i], ALU.add, ALU.subtract)
                    elif name == "cs":
                        tile, m = i // NG, i % NG
                        scores = src[:, 0:HG * S].rearrange("p (h s) -> p h s", h=HG)
                        top = c_max[:, tile % 2, m * HG:m * HG + HG]
                        nc.vector.tensor_reduce(top, scores, AX_X, ALU.max).then_inc(c_max_done, 1)
                        dve.wait_ge(c_max_done, (t.b - 1) * (TT * NG) + i + 1)
                        ins = nc.vector.tensor_tensor(c_probs[:, tile % 2, m * HG:m * HG + HG], scores,
                                                      top.unsqueeze(2).broadcast_to([P, HG, S]), ALU.subtract)
                    elif name == "cpT":
                        ins = low(c_probsT[:, i % NG, 1], src[0:S], 1.0, c_probsT[:, i % NG, 0])
                    elif name == "cy":
                        tile, half = i // 2, i % 2
                        heads = src[:, 0:8 * VW].rearrange("p (h d) -> p h d", h=8)
                        total = c_sums[:, tile % 2, half * 8:half * 8 + 8]
                        nc.vector.reciprocal(total, heads[:, :, HD]).then_inc(c_sums_done, 1)
                        dve.wait_ge(c_sums_done, (t.b - 1) * (2 * TT) + i + 1)
                        ins = nc.vector.tensor_tensor(
                            xn[:, tile, half * 256:half * 256 + 256].rearrange("p (h d) -> p h d", h=8), heads[:, :, 0:HD],
                            total.unsqueeze(2).broadcast_to([P, 8, HD]), ALU.mult)
                    elif name == "xo":
                        dve.wait_ge(x1_biased, (t.b - 1) * TT + i + 1)
                        ins = nc.vector.scalar_tensor_tensor(x_res[:, i], src[:], 1.0 / WSCALE, x_res[:, i], ALU.mult, ALU.add)
                    elif name == "logits":
                        at = (t.b - 1) * TT
                        dst = logits[:, at:at + TT] if isinstance(t.b, int) else logits[:, bass.ds(at, TT)]
                        ins = nc.vector.tensor_scalar(dst, src[:, 0:TT * NE].rearrange("p (t e) -> p t e", t=TT), 1.0 / WSCALE, None,
                                                      ALU.mult)
                    ins.then_inc(job_done, 1)
                    if name in ("o", "xo"):
                        n = 1 if name == "o" else 2
                        wait_apart(dve, job_done, t.done((name, i)), dve_waits)
                        moments_of(n, t.b - 1, i, x_res)
                    if name == "k":
                        wait_apart(dve, job_done, t.done((name, i)), dve_waits)

                def between(t, k):
                    if t.rest and k == K_LOW_STEP:
                        for j in range(HG):
                            dve.wait_ge(k_high, (t.b - 1) * HG + j + 1)
                            rows = slice(j * HD, j * HD + HD)
                            nc.vector.tensor_tensor(k_diag[rows, 1, :, j * S:j * S + S], k_sum[rows],
                                                    k_diag[rows, 0, :, j * S:j * S + S], ALU.subtract).then_inc(k_low, 1)
                    if t.rest and k == XN2_STEP:
                        dve.wait_ge(stores_passed, t.b)
                        normalise(1, t.b - 1, xn, x_res)
                    if t.rest and k == XN3_STEP:
                        normalise(2, t.b - 1, xn, x_res)
                    if t.ahead and k in LN1_STEPS:
                        dve.wait_ge(x_loaded, (t.b + 1) * 16 + 16)
                        moments_of(0, t.b + 1, LN1_STEPS.index(k), x_in)
                    if t.ahead and k == XN1_STEP:
                        normalise(0, t.b + 1, x_in, x_in)

                def max_tile(t, k):
                    n = (k % TT + 1) * P
                    dve.wait_ge(scores_ready, t.g + k + 1)
                    nc.vector.tensor_reduce(neg_max[:, k % STEPS:k % STEPS + 1], score_bank[k % 2][:, 0:n], AX_X, ALU.max,
                                            negate=True).then_inc(max_done, 1)

                def probs_low(t, j):
                    n = (j % TT + 1) * P
                    dve.wait_ge(pT_high, t.g + j + 1)
                    nc.vector.tensor_tensor(probsT[:, j % 4, 1, 0:n], probsT_bank[j % 2][:, 0:n], probsT[:, j % 4, 0, 0:n],
                                            ALU.subtract).then_inc(pT_low, 1)

                def head_out(t, h):
                    i = t.b * H + h
                    if h == 0:
                        wait(dve, y_biased, t.b * TT)
                    dve.wait_ge(y_ready, (i + 1) * TT)
                    src = y_bank[:, 0:TT * VW].rearrange("p (t d) -> p t d", t=TT)
                    nc.vector.reciprocal(sums[:, h % 2], src[:, :, HD]).then_inc(sums_done, 1)
                    dve.wait_ge(sums_done, i + 1)
                    nc.vector.tensor_tensor(y[:, :, h * HD:h * HD + HD], src[:, :, 0:HD],
                                            sums[:, h % 2].unsqueeze(2).broadcast_to([P, TT, HD]), ALU.mult).then_inc(y_normed, 1)

                def body(t):
                    for j in t.before:
                        job(t, *j)
                    for k in range(H * TT + 5):
                        for j in t.steps.get(k - 1, []):
                            job(t, *j)
                        if t.heads and k % TT == 0 and k >= 8:
                            head_out(t, k // TT - 2)
                        if t.heads and k < H * TT:
                            max_tile(t, k)
                        if t.heads and 2 <= k < H * TT + 2:
                            probs_low(t, k - 2)
                        between(t, k)

                for tile in range(TT):
                    dve.wait_ge(x_loaded, 16)
                    moments_of(0, 0, tile, x_in)
                normalise(0, 0, x_in, x_in)
                for c in range(KT):
                    job(start, "x1T", c)
                turns(dve, body)

            @block.tensor
            def _(pe):
                def product(out, left_high, left_low, right_high, right_low, n=KT):
                    for c in range(n):
                        nc.tensor.matmul(out, left_high(c), right_high(c), start=(c == 0), stop=False)
                        nc.tensor.matmul(out, left_high(c), right_low(c), start=False, stop=False)
                        last = nc.tensor.matmul(out, left_low(c), right_high(c), start=False, stop=(c == n - 1))
                    return last

                def rows_times(out, src, tile, w):
                    ts = slice(tile * P, tile * P + P)
                    return product(out, lambda c: src[:, 0, c, ts], lambda c: src[:, 1, c, ts], lambda c: W[w][:, 0, c], lambda c: W[w][:, 1, c])

                def columns_times(out, w, m, right, n=None):
                    ms = slice(m * P, m * P + P)
                    return product(out, lambda c: W[w][:, 0, c, ms], lambda c: W[w][:, 1, c, ms], lambda c: right[:, 0, c], lambda c: right[:, 1, c])

                def transposes(out, src, c):
                    for tile in range(TT):
                        last = nc.tensor.transpose(out[:, tile * P:tile * P + P], src[:, tile, c * P:c * P + P], ident[:])
                    return last

                def job(t, name, i):
                    out = t.bank((name, i))
                    b = t.b
                    wait(pe, job_done, t.bank_free((name, i)))
                    if name == "x1T":
                        pe.wait_ge(ln_done[0], (b + 1) * TT + TT)
                        ins = transposes(out, x_in, i)
                    elif name == "latent":
                        ins = product(out[:], lambda c: w_basis[:, 0, c], lambda c: w_basis[:, 1, c],
                                      lambda c: x1T[:, 0, c], lambda c: x1T[:, 1, c])
                    elif name == "v":
                        ins = rows_times(out[:], x1T, i, "wv")
                    elif name == "left":
                        if i == 0:
                            pe.wait_ge(job_done, t.done(("latent", 0)))
                        nc.tensor.matmul(out[:], head_mat[:, i, :], latent[:, 0], start=True, stop=False)
                        ins = nc.tensor.matmul(out[:], head_mat[:, i, :], latent[:, 1], start=False, stop=True)
                    elif name == "yT":
                        pe.wait_ge(y_biased, b * TT)
                        ins = transposes(out, y, i)
                    elif name == "o":
                        pe.wait_ge(job_done, t.done(("yT", KT - 1)))
                        ins = rows_times(out[:], yT, i, "wo")
                    elif name == "ctxT":
                        pe.wait_ge(ctx_loaded, b * 16)
                        for c in range(KT):
                            ins = nc.tensor.transpose(out[:, c * S:c * S + S], ctx_sb[:, c * P:c * P + P], ident[0:S, 0:S])
                    elif name == "k":
                        pe.wait_ge(job_done, t.done(("ctxT", 0)))
                        for m in range(NG):
                            ins = columns_times(out[:, m * S:m * S + S], "xwk", m, ctxT)
                    elif name == "cv":
                        ins = product(out[0:S], lambda c: ctxT[:, 0, c], lambda c: ctxT[:, 1, c],
                                      lambda c: W["xwv"][:, 0, c], lambda c: W["xwv"][:, 1, c])
                    elif name in ("x2T", "x3T"):
                        pe.wait_ge(ln_done[1 if name == "x2T" else 2], b * TT)
                        ins = transposes(out, xn, i)
                    elif name == "q":
                        pe.wait_ge(job_done, t.done(("x2T", KT - 1)))
                        ins = columns_times(out[:], "xwq", i, xT)
                    elif name == "cs":
                        tile, m = i // NG, i % NG
                        if i == 0:
                            pe.wait_ge(job_done, t.done(("q", NG - 1)))
                            pe.wait_ge(k_low, b * HG)
                        ts = slice(tile * P, tile * P + P)
                        ins = product(out[:, 0:HG * S], lambda c: qT[:, 0, m, ts], lambda c: qT[:, 1, m, ts],
                                      lambda c: k_diag[:, 0, m], lambda c: k_diag[:, 1, m], n=1)
                    elif name == "cpT":
                        tile, m = i // NG, i % NG
                        pe.wait_ge(c_exp_done, (b - 1) * TT + tile + 1)
                        for h in range(HG):
                            ins = nc.tensor.transpose(out[0:S, h * P:h * P + P], c_probs[:, tile % 2, m * HG + h], ident[:])
                    elif name == "cy":
                        tile, half = i // 2, i % 2
                        pe.wait_ge(job_done, t.done(("cpT", tile * NG + half * 2 + 1)))
                        for n in range(8):
                            m, h = half * 2 + n // HG, n % HG
                            o = out[:, n * VW:n * VW + VW]
                            ph = c_probsT[:, m, 0, h * P:h * P + P]
                            pl = c_probsT[:, m, 1, h * P:h * P + P]
                            hh = m * HG + h
                            nc.tensor.matmul(o, ph, c_values[:, 0, hh, :], start=True, stop=False)
                            nc.tensor.matmul(o[:, 0:HD], ph, c_values[:, 1, hh, 0:HD], start=False, stop=False)
                            ins = nc.tensor.matmul(o, pl, c_values[:, 0, hh, :], start=False, stop=True)
                    elif name == "y2T":
                        pe.wait_ge(cy_biased, b * TT)
                        ins = transposes(out, xn, i)
                    elif name == "xo":
                        pe.wait_ge(job_done, t.done(("y2T", KT - 1)))
                        ins = rows_times(out[:], yT, i, "xwo")
                    elif name == "logits":
                        pe.wait_ge(job_done, t.done(("x3T", KT - 1)))
                        for tile in range(TT):
                            ts = slice(tile * P, tile * P + P)
                            ins = product(out[:, tile * NE:tile * NE + NE], lambda c: xT[:, 0, c, ts], lambda c: xT[:, 1, c, ts],
                                          lambda c: router[:, 0, c], lambda c: router[:, 1, c])
                    ins.then_inc(job_ready, 1)

                def score_tile(t, k):
                    tile, h = k % TT, k // TT
                    n = (tile + 1) * P
                    if tile == 0:
                        pe.wait_ge(job_done, t.done(("left", h)))
                    wait(pe, exp_done, t.g + (k - 1 if k >= 2 else 0))
                    lhs = left[:, h % 2, tile * P:tile * P + P]
                    out = score_bank[k % 2]
                    nc.tensor.matmul(out[:, 0:n], lhs, latent[:, 0, 0:n], start=True, stop=False)
                    nc.tensor.matmul(out[:, 0:n], lhs, latent[:, 1, 0:n], start=False, stop=False)
                    nc.tensor.matmul(out[:, n - P:n], big_ident[:], causal[:], start=False, stop=True).then_inc(scores_ready, 1)

                def transpose_tile(t, j):
                    tile = j % TT
                    pe.wait_ge(exp_done, t.g + j + 1)
                    wait(pe, pT_low, t.g + (j - 1 if j >= 2 else 0))
                    for u in range(tile + 1):
                        last = nc.tensor.transpose(probsT_bank[j % 2][:, u * P:u * P + P], probs[:, tile, u * P:u * P + P], ident[:])
                    last.then_inc(pT_ready, 1)

                def values_tile(t, j):
                    tile, h = j % TT, j // TT
                    pe.wait_ge(pT_low, t.g + j + 1)
                    if tile == 0:
                        wait(pe, y_normed, t.b * H + h)
                    if j == 0:
                        pe.wait_ge(job_done, t.done(("v", TT - 1)))
                    out = y_bank[:, tile * VW:(tile + 1) * VW]
                    for u in range(tile + 1):
                        ph = probsT[:, j % 4, 0, u * P:u * P + P]
                        pl = probsT[:, j % 4, 1, u * P:u * P + P]
                        nc.tensor.matmul(out, ph, values[:, 0, u, h, :], start=(u == 0), stop=False)
                        nc.tensor.matmul(out[:, 0:HD], ph, values[:, 1, u, h, 0:HD], start=False, stop=False)
                        last = nc.tensor.matmul(out, pl, values[:, 0, u, h, :], start=False, stop=(u == tile))
                    last.then_inc(y_ready, 1)

                def body(t):
                    if t.heads:
                        pe.wait_ge(job_done, t.jobs)
                    for j in t.before:
                        job(t, *j)
                    for k in range(H * TT + 4):
                        if t.heads and k < H * TT:
                            score_tile(t, k)
                        if t.heads and 2 <= k < H * TT + 2:
                            transpose_tile(t, k - 2)
                        for j in t.steps.get(k, []):
                            job(t, *j)
                        if t.heads and k >= 4:
                            values_tile(t, k - 4)

                pe.wait_ge(ones_set, 5)
                for c in range(KT):
                    job(start, "x1T", c)
                turns(pe, body)


NE, TOPK = 8, 2
F = 1024
FT = F // P
N = B * T
TILES = N // P
SLOT_TILES = -(-(TOPK * N // P + NE - 1) // 2) * 2
NM = 2 * NE
X_SLOT, RAW_SLOT = 12, 13
XT_SLOT = 14


def build_ffn(nc, sem, logits, x2_dram, out, r_bias, sw1, sw3, sw2, ew1, ew2, constants, xn_dram, xT_dram, slot_dram):
    with ExitStack() as keep:
        def sb(name, shape, dt):
            return keep.enter_context(nc.sbuf_tensor(name, shape, dt))

        experts = sb("experts", [P, NM, 2, KT, C], F16)
        slots = sb("slots", [P, TOPK, TILES, 1], mybir.dt.uint32)
        slot_rows = sb("slot_rows", [P, TOPK, TILES, 2], F32)
        tile_expert = sb("tile_expert", [P, SLOT_TILES], mybir.dt.int32)
        w1, w3 = sb("w1", [P, 2, KT, F], F16), sb("w3", [P, 2, KT, F], F16)
        w2 = sb("w2", [P, 2, FT, C], F16)

        def bytes_of(k):
            return experts[:, k].rearrange("p a b c -> p (a b c)").bitcast(F32)

        x_tiles = bytes_of(X_SLOT).rearrange("p (a c) -> p a c", a=TT)
        raw_tile = bytes_of(RAW_SLOT).rearrange("p (a c) -> p a c", a=KT)

        def matrix(e):
            return ew1[e // 2] if e % 2 == 0 else ew2[e // 2]

        bank = [keep.enter_context(nc.psum_tensor(f"ffn_bank{i}", [P, 512], F32)) for i in range(8)]
        x2_v = x2_dram.rearrange("(g a p) c -> g p a c", p=P, a=TT)
        out_v = out[0:N].rearrange("(g a p) c -> g p a c", p=P, a=TT)
        xT = [experts[:, XT_SLOT + k] for k in range(2)]
        xT_loaded, x_loaded = [sem("xT_loaded0"), sem("xT_loaded1")], sem("s_x_loaded")

        def load_xT(eng, g):
            eng.dma_start(xT[g % 2].rearrange("p a b c -> p (a b c)"), xT_dram[g]).then_inc(xT_loaded[g % 2], 16)

        with ExitStack() as inner:
            views = iter(range(4 * 8))
            W_ = TILES * NE

            def grid():
                k = next(views)
                return bytes_of(k // 8)[:, (k % 8) * W_:(k % 8 + 1) * W_].rearrange("p (t e) -> p t e", e=NE)

            def col(name, n=TILES, dt=F32):
                return inner.enter_context(nc.sbuf_tensor(name, [P, n], dt))

            raw_sw = [bytes_of(4 + n) for n in range(6)]
            zeros = bytes_of(10)[:, 0:C]
            sw_loaded, sw_high, sw_low = [sem(f"sw_loaded{n}") for n in range(6)], sem("sw_high"), sem("sw_low")
            sw_scaled = sem("sw_scaled")
            const_loaded, zero_set, zeros_stored = sem("const_loaded"), sem("zero_set"), sem("zeros_stored")
            consts = col("consts", constants.shape[1])
            bias_row = col("bias_row", NE)
            score, biased, first, second, rest, both = grid(), grid(), grid(), grid(), grid(), grid()
            cand, within, total, upto, slot, work = grid(), grid(), grid(), grid(), grid(), grid()
            m1, m2, i1, i2 = col("m1"), col("m2"), col("i1"), col("i2")
            s1, s2, den, safe, fine = col("s1"), col("s2"), col("den"), col("safe"), col("fine")
            g1, g2, sf = col("g1"), col("g2"), col("sf", TOPK * TILES)
            count, tiles_of, tiles_upto, base = col("count", NE), col("tiles_of", NE), col("tiles_upto", NE), col("base", NE)
            ones_col = col("ones_col", TILES)
            both16 = col("both16", W_, F16)
            below = inner.enter_context(nc.sbuf_tensor("below", [P, P], F16))
            all_ones = inner.enter_context(nc.sbuf_tensor("all_ones", [P, P], F16))
            many = bytes_of(3)[:, 0:SLOT_TILES * NE].rearrange("p (q e) -> p q e", e=NE)
            ef = col("ef", SLOT_TILES)
            token = col("token", TILES, mybir.dt.int32)
            pad_rows = inner.enter_context(nc.sbuf_tensor("pad_rows", [P, SLOT_TILES, 2], mybir.dt.int32))
            e_row = consts[:, 0:NE]
            steps_row = consts[:, NE:NE + TILES]
            q_row = consts[:, NE + TILES:NE + TILES + SLOT_TILES]
            sig, chain, made2, pos_ready = sem("sig"), sem("chain"), sem("made2"), sem("pos_ready")
            pads_done, both_done = sem("pads_done"), sem("both_done")

            def over_tiles(row):
                return row.unsqueeze(1).broadcast_to([P, TILES, NE])

            def over_experts(c):
                return c.unsqueeze(2).broadcast_to([P, TILES, NE])

            with nc.Block() as block:
                @block.scalar
                def _(act):
                    nc.scalar.activation(score, logits[:], ACT.Sigmoid).then_inc(sig, 1)
                    pieces = [(w, a) for w in range(3) for a in range(2)]
                    for n, (w, a) in enumerate(pieces):
                        act.wait_ge(sw_loaded[n], 16)
                        dst = (w1[:, 0, 2 * a:2 * a + 2], w3[:, 0, 2 * a:2 * a + 2], w2[:, 0, 4 * a:4 * a + 4])[w]
                        nc.scalar.activation(dst, raw_sw[n].rearrange("p (a c) -> p a c", c=dst.shape[2]), ACT.Copy,
                                             scale=WSCALE).then_inc(sw_high, 1)

                @block.sync
                def _(sp):
                    sp.dma_start(consts[:], constants.broadcast_to([P, constants.shape[1]])).then_inc(const_loaded, 16)
                    sp.dma_start(bias_row[:], r_bias.rearrange("(a n) -> a n", a=1).broadcast_to([P, NE])).then_inc(const_loaded, 16)
                    pieces = [(w, a) for w in range(3) for a in range(2)]
                    for n, (w, a) in enumerate(pieces):
                        src = (sw1, sw3, sw2)[w].rearrange("(h a p) n -> h p a n", p=P, h=2)[a]
                        sp.dma_start(raw_sw[n].rearrange("p (a c) -> p a c", c=src.shape[2]), src).then_inc(sw_loaded[n], 16)
                    load_xT(sp, 0)
                    sp.dma_start(x_tiles, x2_v[0]).then_inc(x_loaded, 16)
                    load_xT(sp, 1)
                    sp.wait_ge(zero_set, 1)
                    sp.dma_start(xn_dram[N:N + P], zeros).then_inc(zeros_stored, 16)
                    sp.wait_ge(made2, 5)
                    sp.dma_start(slot_dram.rearrange("(q p) c -> p q c", p=P), pad_rows[:]).then_inc(pads_done, 16)
                    sp.wait_ge(zeros_stored, 16)
                    sp.wait_ge(pads_done, 16)

                @block.gpsimd
                def _(pool):
                    nc.gpsimd.memset(zeros, 0.0).then_inc(zero_set, 1)
                    nc.gpsimd.memset(below[:], 1.0).then_inc(made2, 1)
                    nc.gpsimd.memset(all_ones[:], 1.0).then_inc(made2, 1)
                    nc.gpsimd.memset(pad_rows[:, :, 1], 0).then_inc(made2, 1)
                    nc.gpsimd.iota(pad_rows[:, :, 0], pattern=[[0, SLOT_TILES]], base=N, channel_multiplier=1).then_inc(made2, 1)
                    nc.gpsimd.iota(token[:], pattern=[[P, TILES]], base=0, channel_multiplier=1).then_inc(made2, 1)
                    pool.wait_ge(made2, 5)
                    nc.gpsimd.affine_select(out=below[:], in_=below[:], compare_op=ALU.is_gt, fill=0.0, base=0,
                                            pattern=[[1, P]], channel_multiplier=-1).then_inc(made2, 1)

                    def split_shared(n):
                        w, a = n // 2, n % 2
                        pool.wait_ge(sw_high, n + 1)
                        hi, lo = ((w1[:, h, 2 * a:2 * a + 2], w3[:, h, 2 * a:2 * a + 2], w2[:, h, 4 * a:4 * a + 4])[w] for h in range(2))
                        src = raw_sw[n].rearrange("p (a c) -> p a c", c=hi.shape[2])
                        nc.gpsimd.tensor_scalar(src, src, WSCALE, 0.0, ALU.mult, ALU.add).then_inc(sw_scaled, 1)
                        pool.wait_ge(sw_scaled, n + 1)
                        nc.gpsimd.tensor_tensor(lo, src, hi, ALU.subtract).then_inc(sw_low, 1)

                    for n in range(6):
                        split_shared(n)

                @block.tensor
                def _(pe):
                    pe.wait_ge(both_done, 1)
                    pe.wait_ge(made2, 6)
                    nc.tensor.matmul(bank[0][:, 0:W_], below[:], both16[:], start=True, stop=True).then_inc(pos_ready, 1)
                    nc.tensor.matmul(bank[1][:, 0:W_], all_ones[:], both16[:], start=True, stop=True).then_inc(pos_ready, 1)

                @block.vector
                def _(dve):
                    steps = [0]

                    def then(ins):
                        steps[0] += 1
                        ins.then_inc(chain, 1)
                        dve.wait_ge(chain, steps[0])

                    V = nc.vector
                    dve.wait_ge(const_loaded, 32)
                    dve.wait_ge(sig, 1)
                    then(V.tensor_tensor(biased, score, over_tiles(bias_row[:]), ALU.add))

                    def best(src, top, index, mask):
                        then(V.tensor_reduce(top, src, AX_X, ALU.max))
                        then(V.tensor_tensor(cand, src, over_experts(top), ALU.is_lt))
                        then(V.scalar_tensor_tensor(cand, cand, float(NE), over_tiles(e_row), ALU.mult, ALU.add))
                        then(V.tensor_reduce(index, cand, AX_X, ALU.min))
                        then(V.tensor_tensor(mask, over_tiles(e_row), over_experts(index), ALU.is_equal))

                    best(biased, m1[:], i1[:], first)
                    then(V.scalar_tensor_tensor(rest, first, -1e30, biased, ALU.mult, ALU.add))
                    best(rest, m2[:], i2[:], second)
                    then(V.tensor_tensor(both, first, second, ALU.add))
                    V.tensor_copy(both16[:], both.rearrange("p t e -> p (t e)")).then_inc(both_done, 1)
                    for mask, s in ((first, s1), (second, s2)):
                        then(V.tensor_tensor(work, mask, score, ALU.mult))
                        then(V.tensor_reduce(s[:], work, AX_X, ALU.add))
                    then(V.tensor_tensor(den[:], s1[:], s2[:], ALU.add))
                    then(V.tensor_scalar(safe[:], den[:], 1e-9, None, ALU.add))
                    then(V.reciprocal(safe[:], safe[:]))
                    then(V.tensor_scalar(fine[:], den[:], 1e-9, None, ALU.is_gt))
                    dve.wait_ge(made2, 5)
                    for s, g, k in ((s1, g1, 0), (s2, g2, 1)):
                        then(V.tensor_tensor(g[:], s[:], safe[:], ALU.mult))
                        then(V.tensor_tensor(g[:], g[:], fine[:], ALU.mult))
                        then(V.tensor_scalar(s[:], fine[:], -0.5, 0.5, ALU.mult, ALU.add))
                        then(V.tensor_tensor(slot_rows[:, k, :, 1], g[:], s[:], ALU.add))
                        then(V.tensor_copy(slot_rows[:, k, :, 0].bitcast(mybir.dt.int32), token[:]))
                    dve.wait_ge(pos_ready, 2)
                    then(V.tensor_copy(total, bank[1][:, 0:W_].rearrange("p (t e) -> p t e", e=NE)))
                    then(V.memset(ones_col[:], 1.0))
                    for e in range(NE):
                        then(V.tensor_tensor_scan(upto[:, :, e], ones_col[:], total[:, :, e], 0.0, ALU.mult, ALU.add))
                    then(V.tensor_copy(count[:], upto[:, TILES - 1]))
                    cmp = work.rearrange("p t e -> p (t e)").rearrange("p (e k) -> p e k", e=NE)
                    then(V.tensor_tensor(cmp, count[:].unsqueeze(2).broadcast_to([P, NE, TILES]),
                                         steps_row.unsqueeze(1).broadcast_to([P, NE, TILES]), ALU.is_gt))
                    then(V.tensor_reduce(tiles_of[:], cmp, AX_X, ALU.add))
                    then(V.tensor_tensor_scan(tiles_upto[:], ones_col[:, 0:NE], tiles_of[:], 0.0, ALU.mult, ALU.add))
                    then(V.tensor_tensor(base[:], tiles_upto[:], tiles_of[:], ALU.subtract))
                    then(V.tensor_scalar(base[:], base[:], float(P), None, ALU.mult))
                    then(V.tensor_tensor(slot, upto, total, ALU.subtract))
                    then(V.tensor_tensor(slot, slot, over_tiles(base[:]), ALU.add))
                    then(V.tensor_tensor(slot, slot, bank[0][:, 0:W_].rearrange("p (t e) -> p t e", e=NE), ALU.add))
                    for k, mask in enumerate((first, second)):
                        then(V.tensor_tensor(work, mask, slot, ALU.mult))
                        then(V.tensor_reduce(sf[:, k * TILES:(k + 1) * TILES], work, AX_X, ALU.add))
                    then(V.tensor_copy(slots[:, :, :, 0], sf[:].rearrange("p (k t) -> p k t", k=TOPK)))
                    then(V.tensor_tensor(many, tiles_upto[:].unsqueeze(1).broadcast_to([P, SLOT_TILES, NE]),
                                         q_row.unsqueeze(2).broadcast_to([P, SLOT_TILES, NE]), ALU.is_le))
                    then(V.tensor_reduce(ef[:], many, AX_X, ALU.add))
                    then(V.tensor_scalar(ef[:], ef[:], float(NE - 1), None, ALU.min))
                    then(V.tensor_copy(tile_expert[:], ef[:]))

        gT = sb("gT", [P, 2, FT, T], F16)
        with ExitStack() as scope:
            gate = scope.enter_context(nc.sbuf_tensor("gate", [P, 2, T], F32))
            x_stored = sem("s_x_stored")
            h_ready, silu_done, g_done, g_high, g_low = sem("h_ready"), sem("silu_done"), sem("g_done"), sem("g_high"), sem("g_low")
            o_ready, o_done = sem("s_o_ready"), sem("s_o_done")
            rows_placed = sem("rows_placed")
            mat_loaded, mat_step, mat_done = sem("mat_loaded"), sem("mat_step"), sem("mat_done")
            early = list(range(X_SLOT)) + [XT_SLOT]

            with nc.Block() as block:
                @block.sync
                def _(sp):
                    for g in range(B):
                        if g + 2 < B:
                            sp.wait_ge(h_ready, (g + 1) * 2 * FT)
                            load_xT(sp, g + 2)
                        sp.wait_ge(o_done, g * TT + TT)
                        sp.dma_start(out_v[g], x_tiles).then_inc(x_stored, 16)
                        if g + 1 < B:
                            sp.wait_ge(x_stored, g * 16 + 16)
                            sp.dma_start(x_tiles, x2_v[g + 1]).then_inc(x_loaded, 16)
                    sp.wait_ge(x_stored, 16 * B)

                @block.gpsimd
                def _(pool):
                    for k in range(TOPK):
                        for t in range(TILES):
                            nc.gpsimd.indirect_dma_start(
                                slot_dram, bass.IndirectOffsetOnAxis(ap=slots[:, k, t], axis=0),
                                slot_rows[:, k, t].bitcast(mybir.dt.int32), None).then_inc(rows_placed, 16)
                    for n, m in enumerate(early):
                        if m >= XT_SLOT:
                            pool.wait_ge(h_ready, (B - 1) * 2 * FT)
                        if n > 0:
                            pool.wait_ge(mat_done, n)
                        pool.dma_start(raw_tile, matrix(m).rearrange("(a p) c -> p a c", p=P)).then_inc(mat_loaded, 16)
                        pool.wait_ge(mat_loaded, 16 * n + 16)
                        nc.gpsimd.tensor_scalar(raw_tile, raw_tile, WSCALE, 0.0, ALU.mult, ALU.add).then_inc(mat_step, 1)
                        pool.wait_ge(mat_step, 2 * n + 1)
                        nc.gpsimd.tensor_copy(experts[:, m, 0], raw_tile).then_inc(mat_step, 1)
                        pool.wait_ge(mat_step, 2 * n + 2)
                        nc.gpsimd.tensor_tensor(experts[:, m, 1], raw_tile, experts[:, m, 0], ALU.subtract).then_inc(mat_done, 1)
                    pool.wait_ge(rows_placed, 16 * TOPK * TILES)

                @block.scalar
                def _(act):
                    def high(i, f):
                        act.wait_ge(g_done, i + 1)
                        nc.scalar.activation(gT[:, 0, f], gate[:, f % 2], ACT.Copy).then_inc(g_high, 1)

                    def group(g):
                        for f in range(FT):
                            i = g * FT + f
                            act.wait_ge(h_ready, i * 2 + 1)
                            wait(act, g_low, i - 1)
                            nc.scalar.activation(gate[:, f % 2], bank[f % 2][:], ACT.Silu, scale=1.0 / WSCALE).then_inc(silu_done, 1)
                            if f == 0:
                                wait(act, o_ready, g * TT)
                            else:
                                high(i - 1, f - 1)
                        high(g * FT + FT - 1, FT - 1)

                    group(0)
                    with act.Fori(1, B) as g:
                        group(g)

                @block.vector
                def _(dve):
                    def low(i, f):
                        dve.wait_ge(g_high, i + 1)
                        nc.vector.tensor_tensor(gT[:, 1, f], gate[:, f % 2], gT[:, 0, f], ALU.subtract).then_inc(g_low, 1)

                    def group(g):
                        for f in range(FT):
                            i = g * FT + f
                            dve.wait_ge(silu_done, i + 1)
                            dve.wait_ge(h_ready, i * 2 + 2)
                            nc.vector.scalar_tensor_tensor(gate[:, f % 2], bank[2 + f % 2][:], 1.0 / WSCALE, gate[:, f % 2],
                                                           ALU.mult, ALU.mult).then_inc(g_done, 1)
                            if f > 0:
                                low(i - 1, f - 1)
                        low(g * FT + FT - 1, FT - 1)
                        dve.wait_ge(x_loaded, g * 16 + 16)
                        for t in range(TT):
                            dve.wait_ge(o_ready, g * TT + t + 1)
                            nc.vector.scalar_tensor_tensor(x_tiles[:, t], bank[4 + t][:], 1.0 / WSCALE, x_tiles[:, t],
                                                           ALU.mult, ALU.add).then_inc(o_done, 1)

                    group(0)
                    with dve.Fori(1, B) as g:
                        group(g)

                @block.tensor
                def _(pe):
                    def group(i, k):
                        g = i * 2 + k
                        pe.wait_ge(xT_loaded[k], i * 16 + 16)

                        def xt(h, c):
                            return xT[k][:, h, c]

                        def hidden(out_bank, w, f):
                            fs = slice(f * P, f * P + P)
                            for c in range(KT):
                                nc.tensor.matmul(out_bank, w[:, 0, c, fs], xt(0, c), start=(c == 0), stop=False)
                                nc.tensor.matmul(out_bank, w[:, 0, c, fs], xt(1, c), start=False, stop=False)
                                last = nc.tensor.matmul(out_bank, w[:, 1, c, fs], xt(0, c), start=False, stop=(c == KT - 1))
                            last.then_inc(h_ready, 1)

                        for f in range(FT):
                            n = g * FT + f
                            wait(pe, silu_done, n - 1)
                            hidden(bank[f % 2][:], w1, f)
                            wait(pe, g_done, n - 1)
                            hidden(bank[2 + f % 2][:], w3, f)
                        wait(pe, o_done, g * TT)
                        for f in range(FT):
                            pe.wait_ge(g_low, g * FT + f + 1)
                            for t in range(TT):
                                ts = slice(t * P, t * P + P)
                                nc.tensor.matmul(bank[4 + t][:], gT[:, 0, f, ts], w2[:, 0, f], start=(f == 0), stop=False)
                                nc.tensor.matmul(bank[4 + t][:], gT[:, 0, f, ts], w2[:, 1, f], start=False, stop=False)
                                last = nc.tensor.matmul(bank[4 + t][:], gT[:, 1, f, ts], w2[:, 0, f], start=False, stop=(f == FT - 1))
                                if f == FT - 1:
                                    last.then_inc(o_ready, 1)

                    group(0, 0)
                    group(0, 1)
                    with pe.Fori(1, B // 2) as i:
                        group(i, 0)
                        group(i, 1)

        build_routed(nc, sem, keep, experts, tile_expert, bank, matrix, out, xn_dram, slot_dram, w1, w3, w2, gT)


AHEAD = 6
RING = 8


def build_routed(nc, sem, keep, experts, tile_expert, bank, matrix, out, xn_dram, slot_dram, w1, w3, w2, gT):
    with ExitStack() as scope:
        def view(t, lead, dt, *shape):
            flat = t[:].rearrange("p a b c -> p (a b c)").bitcast(dt)
            return flat

        f1, f3, f2, fg = (view(t, None, F32) for t in (w1, w3, w2, gT))
        raw = [f1[:, 0:2048], f1[:, 2048:4096], f3[:, 0:2048]]
        xg = [fg[:, k * C:k * C + C] for k in range(RING)]
        h_sb = [f2[:, k * C:k * C + C] for k in range(2)]
        y_sb = [f2[:, (2 + k) * C:(3 + k) * C] for k in range(2)]
        h16 = w2[:].rearrange("p a b c -> p (a b c)")
        xT = [h16[:, 4096 + k * 1024:4096 + k * 1024 + 1024].rearrange("p (h c t) -> p h c t", h=2, c=KT) for k in range(4)]
        h16b = w3[:].rearrange("p a b c -> p (a b c)")
        hT = [h16b[:, 4096 + k * 1024:4096 + k * 1024 + 1024].rearrange("p (h c t) -> p h c t", h=2, c=KT) for k in range(2)]
        ident = scope.enter_context(nc.sbuf_tensor("r_ident", [P, P], F32))
        rows = scope.enter_context(nc.sbuf_tensor("rows", [P, RING, 2], mybir.dt.int32))
        made, raw_high, raw_low = sem("r_made"), sem("raw_high"), sem("raw_low")
        raw_loaded = [sem(f"raw_loaded{n}") for n in range(3)]
        rows_loaded = [sem(f"rows_loaded{k}") for k in range(RING)]
        gathered, added = [sem(f"gathered{k}") for k in range(RING)], sem("added")
        xT_ready, xT_high, xT_low = sem("r_xT_ready"), sem("r_xT_high"), sem("r_xT_low")
        h_ready, gelu_done = sem("r_h_ready"), sem("gelu_done")
        hT_ready, hT_high, hT_low = sem("hT_ready"), sem("hT_high"), sem("hT_low")
        y_ready, y_done = sem("r_y_ready"), sem("r_y_done")
        pool_waits = sem("r_pool_waits")
        late = [X_SLOT, RAW_SLOT, XT_SLOT + 1]
        Q = SLOT_TILES
        I32 = mybir.dt.int32
        slot_v = slot_dram.rearrange("(q p) c -> q p c", p=P)

        def turns_all(eng, body):
            for k in range(8):
                body(0, k)
            with eng.Fori(1, Q // 8 - 1) as i:
                for k in range(8):
                    body(i, k)
            for k in range(8):
                body(Q // 8 - 1, k)

        with nc.Block() as block:
            @block.sync
            def _(sp):
                for n, m in enumerate(late):
                    sp.dma_start(raw[n].rearrange("p (a c) -> p a c", a=KT), matrix(m).rearrange("(a p) c -> p a c", p=P)
                                 ).then_inc(raw_loaded[n], 16)

                def body(i, k):
                    q = i * 8 + k
                    wait(sp, added, q * 16 - 7 * 16)
                    src = slot_v[q] if isinstance(q, int) else slot_v[bass.ds(q, 1)].rearrange("o p c -> (o p) c")
                    sp.dma_start(rows[:, k], src).then_inc(rows_loaded[k], 16)
                turns_all(sp, body)

            @block.gpsimd
            def _(pool):
                nc.gpsimd.memset(ident[:], 0.0).then_inc(made, 1)
                pool.wait_ge(made, 1)
                nc.gpsimd.affine_select(out=ident[:], in_=ident[:], compare_op=ALU.not_equal, fill=1.0, base=0,
                                        pattern=[[-1, P]], channel_multiplier=1).then_inc(made, 1)

                def gather(i, k):
                    i, k = i + k // 8, k % 8
                    q = i * 8 + k
                    wait(pool, xT_ready, q - RING + 1)
                    wait_apart(pool, rows_loaded[k], i * 16 + 16, pool_waits)
                    nc.gpsimd.indirect_dma_start(xg[k], None, xn_dram,
                                                 bass.IndirectOffsetOnAxis(ap=rows[:, k, 0:1].bitcast(mybir.dt.uint32), axis=0)
                                                 ).then_inc(gathered[k], 16)

                def add(i, k):
                    q = i * 8 + k
                    wait(pool, added, q * 16)
                    wait_apart(pool, y_done, q + 1, pool_waits)
                    nc.gpsimd.indirect_dma_start(out, bass.IndirectOffsetOnAxis(ap=rows[:, k, 0:1].bitcast(mybir.dt.uint32), axis=0),
                                                 y_sb[k % 2], None, compute_op=ALU.add).then_inc(added, 16)

                for k in range(AHEAD):
                    gather(0, k)

                def body(i, k):
                    if not (isinstance(i, int) and i * 8 + k + AHEAD >= Q):
                        gather(i, k + AHEAD)
                    add(i, k)
                turns_all(pool, body)
                pool.wait_ge(added, 16 * Q)

            @block.scalar
            def _(act):
                for n, m in enumerate(late):
                    act.wait_ge(raw_loaded[n], 16)
                    nc.scalar.activation(experts[:, m, 0], raw[n].rearrange("p (a c) -> p a c", a=KT), ACT.Copy,
                                         scale=WSCALE).then_inc(raw_high, 1)

                def x_high(i, k):
                    i, k = i + k // 8, k % 8
                    q = i * 8 + k
                    act.wait_ge(xT_ready, q + 1)
                    wait(act, h_ready, q - 3)
                    nc.scalar.activation(xT[k % 4][:, 0], bank[k % 2][:].rearrange("p (c t) -> p c t", c=KT), ACT.Copy).then_inc(xT_high, 1)

                def h_high(i, k):
                    i, k = i + k // 8, k % 8
                    q = i * 8 + k
                    act.wait_ge(hT_ready, q + 1)
                    wait(act, y_ready, q - 1)
                    nc.scalar.activation(hT[k % 2][:, 0], bank[4 + k % 2][:].rearrange("p (c t) -> p c t", c=KT), ACT.Copy).then_inc(hT_high, 1)

                def gelu(i, k):
                    i, k = i + k // 8, k % 8
                    q = i * 8 + k
                    act.wait_ge(h_ready, q + 1)
                    wait(act, hT_ready, q - 1)
                    nc.scalar.activation(h_sb[k % 2], bank[2 + k % 2][:], ACT.Gelu, scale=1.0 / WSCALE).then_inc(gelu_done, 1)

                x_high(0, 0)
                x_high(0, 1)

                def ordered(i, k):
                    if not (isinstance(i, int) and i * 8 + k == 0):
                        h_high(i, k - 1)
                    if not (isinstance(i, int) and i * 8 + k + 2 >= Q):
                        x_high(i, k + 2)
                    gelu(i, k)
                turns_all(act, ordered)
                h_high(0, Q - 1)

            @block.vector
            def _(dve):
                for n, m in enumerate(late):
                    dve.wait_ge(raw_high, n + 1)
                    nc.vector.scalar_tensor_tensor(experts[:, m, 1], raw[n].rearrange("p (a c) -> p a c", a=KT), WSCALE,
                                                   experts[:, m, 0], ALU.mult, ALU.subtract).then_inc(raw_low, 1)

                def x_low(i, k):
                    i, k = i + k // 8, k % 8
                    q = i * 8 + k
                    dve.wait_ge(xT_high, q + 1)
                    nc.vector.tensor_tensor(xT[k % 4][:, 1], bank[k % 2][:].rearrange("p (c t) -> p c t", c=KT), xT[k % 4][:, 0],
                                            ALU.subtract).then_inc(xT_low, 1)

                def h_low(i, k):
                    i, k = i + k // 8, k % 8
                    q = i * 8 + k
                    dve.wait_ge(hT_high, q + 1)
                    nc.vector.tensor_tensor(hT[k % 2][:, 1], bank[4 + k % 2][:].rearrange("p (c t) -> p c t", c=KT), hT[k % 2][:, 0],
                                            ALU.subtract).then_inc(hT_low, 1)

                def y_out(i, k):
                    i, k = i + k // 8, k % 8
                    q = i * 8 + k
                    dve.wait_ge(y_ready, q + 1)
                    wait(dve, added, q * 16 - 16)
                    nc.vector.tensor_scalar(y_sb[k % 2], bank[6 + k % 2][:], rows[:, k, 1:2].bitcast(F32), 1.0 / WSCALE,
                                            ALU.mult, ALU.mult).then_inc(y_done, 1)

                x_low(0, 0)
                x_low(0, 1)

                def ordered(i, k):
                    if not (isinstance(i, int) and i * 8 + k == 0):
                        h_low(i, k - 1)
                    if not (isinstance(i, int) and i * 8 + k + 2 >= Q):
                        x_low(i, k + 2)
                    if not (isinstance(i, int) and i * 8 + k < 2):
                        y_out(i, k - 2)
                turns_all(dve, ordered)
                y_out(0, Q - 2)
                h_low(0, Q - 1)
                y_out(0, Q - 1)

            @block.tensor
            def _(pe):
                def x_transposes(i, k):
                    i, k = i + k // 8, k % 8
                    q = i * 8 + k
                    pe.wait_ge(gathered[k], i * 16 + 16)
                    wait(pe, xT_low, q - 1)
                    for c in range(KT):
                        last = nc.tensor.transpose(bank[k % 2][:, c * P:c * P + P], xg[k][:, c * P:c * P + P], ident[:])
                    last.then_inc(xT_ready, 1)

                def h_transposes(i, k):
                    i, k = i + k // 8, k % 8
                    q = i * 8 + k
                    pe.wait_ge(gelu_done, q + 1)
                    wait(pe, hT_low, q - 1)
                    for c in range(KT):
                        last = nc.tensor.transpose(bank[4 + k % 2][:, c * P:c * P + P], h_sb[k % 2][:, c * P:c * P + P], ident[:])
                    last.then_inc(hT_ready, 1)

                def expert_of(q):
                    return pe.value_load(tile_expert[0:1, bass.ds(q, 1)], min_val=0, max_val=NE - 1)

                def expert_product(e, bank_, lhs, second):
                    def w(h, c):
                        return experts[:, bass.ds(e * 2 + second, 1), h, c].rearrange("p o n -> p (o n)")
                    for c in range(KT):
                        nc.tensor.matmul(bank_[:], lhs[:, 0, c], w(0, c), start=(c == 0), stop=False)
                        nc.tensor.matmul(bank_[:], lhs[:, 0, c], w(1, c), start=False, stop=False)
                        last = nc.tensor.matmul(bank_[:], lhs[:, 1, c], w(0, c), start=False, stop=(c == KT - 1))
                    return last

                def hidden(i, k):
                    i, k = i + k // 8, k % 8
                    q = i * 8 + k
                    e = expert_of(q)
                    wait(pe, gelu_done, q - 1)
                    pe.wait_ge(xT_low, q + 1)
                    expert_product(e, bank[2 + k % 2], xT[k % 4], 0).then_inc(h_ready, 1)

                def result(i, k):
                    i, k = i + k // 8, k % 8
                    q = i * 8 + k
                    e = expert_of(q)
                    wait(pe, y_done, q - 1)
                    pe.wait_ge(hT_low, q + 1)
                    expert_product(e, bank[6 + k % 2], hT[k % 2], 1).then_inc(y_ready, 1)

                pe.wait_ge(made, 2)
                pe.wait_ge(raw_low, len(late))
                x_transposes(0, 0)
                x_transposes(0, 1)

                def ordered(i, k):
                    hidden(i, k)
                    if not (isinstance(i, int) and i * 8 + k == 0):
                        h_transposes(i, k - 1)
                    if not (isinstance(i, int) and i * 8 + k + 2 >= Q):
                        x_transposes(i, k + 2)
                    if not (isinstance(i, int) and i * 8 + k < 2):
                        result(i, k - 2)
                turns_all(pe, ordered)
                result(0, Q - 2)
                h_transposes(0, Q - 1)
                result(0, Q - 1)


def shape_constants():
    import numpy as np
    return np.concatenate([np.arange(NE), P * np.arange(TILES), np.arange(SLOT_TILES)]).astype(np.float32)[None]


def build_program(nc, out, in_x, in_ctx, in_basisT, in_core, in_coreT, in_head_res, in_wvT, in_bv, in_woT, in_bo, in_xwqT,
                  in_xbq, in_xwkT, in_xbk, in_xwvT, in_xbv, in_xwoT, in_xbo, in_rwT, in_r_bias, in_sw1, in_sw3, in_sw2,
                  in_ew1, in_ew2, in_constants):
    with ExitStack() as ctx:
        def sem(name):
            return ctx.enter_context(nc.semaphore(name))

        x2 = nc.dram_tensor("x2", (N, C), F32, kind="Internal").ap()
        xn = nc.dram_tensor("xn3", (N + P, C), F32, kind="Internal").ap()
        xT = nc.dram_tensor("xn3_transposed", (B, P, 2 * KT * T), F16, kind="Internal").ap()
        logits = ctx.enter_context(nc.sbuf_tensor("logits", [P, TILES, NE], F32))
        slots = nc.dram_tensor("slot_table", (SLOT_TILES * P, 2), mybir.dt.int32, kind="Internal").ap()
        build_attention(nc, sem, in_x, in_ctx, (in_basisT, in_core, in_coreT, in_head_res, in_wvT, in_bv, in_woT, in_bo,
                                                in_xwqT, in_xbq, in_xwkT, in_xbk, in_xwvT, in_xbv, in_xwoT, in_xbo),
                        in_rwT, logits, x2, xn, xT)
        build_ffn(nc, sem, logits, x2, out, in_r_bias, in_sw1, in_sw3, in_sw2, in_ew1, in_ew2, in_constants, xn, xT, slots)


def kernel(**inputs):
    import numpy as _np
    import concourse.bacc as _bacc
    from concourse import mybir as _mybir
    from concourse.bass_utils import run_bass_kernel_spmd as _run

    nc = _bacc.Bacc("TRN2", target_bir_lowering=False, num_devices=1)
    i = {k: _np.asarray(v) for k, v in inputs.items()}
    columns = lambda v: v.reshape(NG, P).T
    arrays = {
        "x": i["x"], "ctx": i["ctx_1024"], "basisT": i["L0_attn_basis_w"].T, "core": i["L0_attn_core"],
        "coreT": i["L0_attn_core"].T, "head_res": i["L0_attn_head_residual"], "wvT": i["L0_attn_v_w"].T,
        "bv": i["L0_attn_v_b"], "woT": i["L0_attn_o_w"].T, "bo": i["L0_attn_o_b"], "xwqT": i["L0_xattn_Wq"].T,
        "xbq": columns(i["L0_xattn_bq"]), "xwkT": i["L0_xattn_Wk"].T, "xbk": columns(i["L0_xattn_bk"]),
        "xwvT": i["L0_xattn_Wv"].T, "xbv": i["L0_xattn_bv"], "xwoT": i["L0_xattn_Wo"].T, "xbo": i["L0_xattn_bo"],
        "rwT": i["L0_ffn_router_w"].T, "r_bias": i["L0_ffn_router_bias"], "sw1": i["L0_ffn_sw1"],
        "sw3": i["L0_ffn_sw3"], "sw2": i["L0_ffn_sw2"], "ew1": i["L0_ffn_ew1"], "ew2": i["L0_ffn_ew2"],
        "constants": shape_constants(),
    }
    arrays = {"in_" + k: _np.ascontiguousarray(v) for k, v in arrays.items()}
    args = {k: nc.dram_tensor(k, v.shape, _mybir.dt.from_np(v.dtype), kind="ExternalInput").ap() for k, v in arrays.items()}
    out = nc.dram_tensor("out_0", (N + P, C), F32, kind="ExternalOutput").ap()
    build_program(nc, out, **args)
    r = _run(nc, [arrays], core_ids=[0])
    return r.results[0]["out_0"][:N].reshape(B, T, C)
```

```python
from contextlib import ExitStack

import concourse.bass as bass
from concourse import mybir

ALU = mybir.AluOpType
ACT = mybir.ActivationFunctionType
F32 = mybir.dt.float32
F16 = mybir.dt.float16
AX_X = mybir.AxisListType.X

P = 128
B, T, C = 8, 512, 512
TT = T // P
KT = C // P
H, R, HD = 16, 64, 32
S = 77
HG = P // HD
NG = H // HG
VW = HD + 1
WSCALE = 32.0
MSCALE = 64.0
BIG = 60000.0
EPS = 1e-5
XSCALE = float(HD) ** -0.5 / (WSCALE * WSCALE)
NE = 8
STEPS = 2 * TT


def wait(eng, s, value):
    if not isinstance(value, int) or value > 0:
        eng.wait_ge(s, value)


def wait_apart(eng, s, value, passed):
    eng.wait_ge(s, value)
    eng.sem_inc(passed, 1)


UNSPLIT = ("k", "o", "cs", "cy", "xo", "logits")


REST_STEPS = {
    "yT": (2, 2, 3, 3),
    "o": (5, 5, 6, 9),
    "ctxT": (8,),
    "k": (9,),
    "cv": (10,),
    "x2T": (12, 12, 12, 14),
    "q": (16, 17, 18, 19),
    "cpT": (24, 25, 26, 27, 30, 30, 32, 33, 36, 36, 38, 40, 42, 42, 44, 45),
    "cy": (26, 29, 32, 35, 38, 41, 44, 48),
    "cs": (20, 20, 21, 22, 23, 25, 27, 28, 31, 31, 33, 33, 37, 37, 39, 40),
    "y2T": (50, 51, 51, 51),
    "xo": (52, 52, 53, 54),
    "x3T": (59, 59, 60, 60),
    "logits": (62,)}
AHEAD_STEPS = {
    "x1T": (14, 18, 19, 20),
    "latent": (23,),
    "v": (28, 34, 40, 47),
    "left": (61,)}


def by_step(steps_of):
    return sorted(((step, (name, i)) for name, steps in steps_of.items() for i, step in enumerate(steps)), key=lambda j: j[0])


REST, AHEAD_JOBS = by_step(REST_STEPS), by_step(AHEAD_STEPS)
START_JOBS = [("x1T", c) for c in range(KT)] + [("latent", 0), ("v", 0), ("left", 0), ("v", 1), ("v", 2), ("v", 3)]
K_LOW_STEP, XN2_STEP, XN3_STEP = 11, 11, 58
LN1_STEPS = (7, 8, 9, 10)


def build_attention(nc, sem, x, ctx_in, weights, rwT, logits, x2_dram, xn_dram, xT_dram):
    basisT, core, coreT, head_res, wvT, bv, woT, bo, xwqT, xbq, xwkT, xbk, xwvT, xbv, xwoT, xbo = weights
    with ExitStack() as keep:
        def sb(name, shape, dt):
            return keep.enter_context(nc.sbuf_tensor(name, shape, dt))

        w_names = ["wv", "wo", "xwq", "xwk", "xwv", "xwo"]
        w_loaded = {n: sem("loaded_" + n) for n in w_names}
        x_loaded = sem("x_loaded")
        x_in = sb("x_in", [P, TT, C], F32)
        y = sb("y", [P, TT, C], F32)
        c_probs = sb("c_probs", [P, 2, H, S], F32)
        raw_bias = c_probs[:].rearrange("p a h s -> p (a h s)")[:, 0:2 * C].rearrange("p (a c) -> p a c", a=2)
        bias_loaded, bias_scaled = sem("bias_loaded"), sem("bias_scaled")
        W = {n: sb(n, [P, 2, KT, C], F16) for n in w_names}
        w_basis = sb("w_basis", [P, 2, KT, P], F16)
        head_mat = sb("head_mat", [P, H, P], F16)
        ident = sb("ident", [P, P], F32)
        big_ident = sb("big_ident", [P, P], F16)
        causal = sb("causal", [P, P], F16)
        value_bias = sb("value_bias", [P, 2, C], F16)
        first_rows = sb("first_rows", [P, P], F16)
        ob_row = sb("ob_row", [P, C], F32)
        xob_row = sb("xob_row", [P, C], F32)
        q_bias = sb("q_bias", [P, NG], F32)
        k_bias = sb("k_bias", [P, NG], F32)
        neg_half = sb("neg_half", [P, TT], F32)
        router = sb("router", [P, 2, KT, NE], F16)

        with ExitStack() as prep:
            def tmp(name, shape, dt):
                return prep.enter_context(nc.sbuf_tensor(name, shape, dt))

            raw_basis = tmp("raw_basis", [P, KT, R], F32)
            raw_router = tmp("raw_router", [P, KT, NE], F32)
            raw_heads = tmp("raw_heads", [P, H, R], F32)
            raw_core = tmp("raw_core", [P, 2, R], F32)
            head_sum = tmp("head_sum", [P, R], F32)
            core_sum = tmp("core_sum", [P, R], F32)
            shared = tmp("shared", [P, R], F32)
            small_loaded = sem("small_loaded")
            w_high, w_low = sem("w_high"), sem("w_low")
            pool_made, head_step, head_high = sem("pool_made"), sem("head_step"), sem("head_high")
            with nc.Block() as block:
                @block.sync
                def _(sp):
                    for half in (0, R):
                        sp.dma_start(raw_heads[half:half + R], head_res.rearrange("h r s -> r h s")).then_inc(small_loaded, 16)
                        sp.dma_start(raw_core[half:half + R, 0, :], core).then_inc(small_loaded, 16)
                        sp.dma_start(raw_core[half:half + R, 1, :], coreT).then_inc(small_loaded, 16)
                    sp.dma_start(raw_basis[:], basisT.rearrange("(a p) n -> p a n", p=P)).then_inc(small_loaded, 16)
                    sp.dma_start(raw_router[:], rwT.rearrange("(a p) n -> p a n", p=P)).then_inc(small_loaded, 16)
                    sp.dma_start(x_in[:], x[0].rearrange("(a p) c -> p a c", p=P)).then_inc(x_loaded, 16)
                    sp.dma_start(y[:], wvT.rearrange("(a p) n -> p a n", p=P)).then_inc(w_loaded["wv"], 16)
                    for dst, src in ((raw_bias[:, 0], bv), (ob_row[:], bo), (raw_bias[:, 1], xbv), (xob_row[:], xbo)):
                        sp.dma_start(dst, src.rearrange("(a n) -> a n", a=1).broadcast_to([P, C])).then_inc(bias_loaded, 16)
                    for dst, src in ((q_bias, xbq), (k_bias, xbk)):
                        sp.dma_start(dst[:], src).then_inc(bias_loaded, 16)

                @block.gpsimd
                def _(pool):
                    nc.gpsimd.memset(neg_half[:], -0.5).then_inc(pool_made, 1)
                    nc.gpsimd.memset(ident[:], 0.0).then_inc(pool_made, 1)
                    nc.gpsimd.memset(big_ident[:], 0.0).then_inc(pool_made, 1)
                    nc.gpsimd.memset(causal[:], 0.0).then_inc(pool_made, 1)
                    nc.gpsimd.memset(first_rows[:], 0.0).then_inc(pool_made, 1)
                    pool.wait_ge(pool_made, 5)
                    for row in (0, R):
                        nc.gpsimd.memset(first_rows[row:row + 1], 1.0).then_inc(pool_made, 1)
                    pool.wait_ge(pool_made, 7)
                    for t, value in ((ident, 1.0), (big_ident, BIG)):
                        nc.gpsimd.affine_select(out=t[:], in_=t[:], compare_op=ALU.not_equal, fill=value, base=0,
                                                pattern=[[-1, P]], channel_multiplier=1).then_inc(pool_made, 1)
                    nc.gpsimd.affine_select(out=causal[:], in_=causal[:], compare_op=ALU.is_ge, fill=-BIG, base=0,
                                            pattern=[[-1, P]], channel_multiplier=1).then_inc(pool_made, 1)

                @block.scalar
                def _(act):
                    act.wait_ge(small_loaded, 16 * 8)
                    for half in range(2):
                        nc.scalar.activation(w_basis[:, 0, :, half * R:half * R + R], raw_basis[:], ACT.Copy,
                                             scale=WSCALE).then_inc(w_high, 1)
                    nc.scalar.activation(router[:, 0], raw_router[:], ACT.Copy, scale=WSCALE).then_inc(w_high, 1)
                    act.wait_ge(head_step, 6)
                    nc.scalar.activation(head_mat[:, :, 0:R], raw_heads[:], ACT.Copy, scale=MSCALE).then_inc(head_high, 1)

                @block.vector
                def _(dve):
                    dve.wait_ge(small_loaded, 16 * 8)
                    nc.vector.tensor_reduce(head_sum[:], raw_heads[:].rearrange("p h s -> p s h"), AX_X,
                                            ALU.add).then_inc(head_step, 1)
                    nc.vector.tensor_tensor(core_sum[:], raw_core[:, 0], raw_core[:, 1], ALU.add).then_inc(head_step, 1)
                    dve.wait_ge(head_step, 2)
                    nc.vector.tensor_scalar(core_sum[:], core_sum[:], 0.5 / H, None, ALU.mult).then_inc(head_step, 1)
                    nc.vector.tensor_scalar(head_sum[:], head_sum[:], 1.0 / H, None, ALU.mult).then_inc(head_step, 1)
                    dve.wait_ge(head_step, 4)
                    nc.vector.tensor_tensor(shared[:], core_sum[:], head_sum[:], ALU.subtract).then_inc(head_step, 1)
                    dve.wait_ge(head_step, 5)
                    nc.vector.tensor_tensor(raw_heads[:], raw_heads[:],
                                            shared[:].unsqueeze(1).broadcast_to([P, H, R]), ALU.add).then_inc(head_step, 1)
                    for half in range(2):
                        dve.wait_ge(w_high, half + 1)
                        cols = slice(half * R, half * R + R)
                        nc.vector.scalar_tensor_tensor(w_basis[:, 1, :, cols], raw_basis[:], WSCALE,
                                                       w_basis[:, 0, :, cols], ALU.mult, ALU.subtract).then_inc(w_low, 1)
                    dve.wait_ge(w_high, 3)
                    nc.vector.scalar_tensor_tensor(router[:, 1], raw_router[:], WSCALE, router[:, 0],
                                                   ALU.mult, ALU.subtract).then_inc(w_low, 1)
                    dve.wait_ge(head_step, 6)
                    dve.wait_ge(head_high, 1)
                    nc.vector.scalar_tensor_tensor(head_mat[R:P, :, 0:R], raw_heads[R:P], MSCALE,
                                                   head_mat[R:P, :, 0:R], ALU.mult, ALU.subtract).then_inc(head_step, 1)
                    dve.wait_ge(head_step, 7)
                    nc.vector.tensor_copy(head_mat[:, :, R:P], head_mat[:, :, 0:R]).then_inc(head_step, 1)

        x_res = sb("x_res", [P, TT, C], F32)
        xn = sb("xn", [P, TT, C], F32)
        ctx_sb = sb("ctx_sb", [S, C], F32)
        stats = sb("stats", [P, 3, TT, 6], F32)
        moments = sb("moments", [P, 3, TT, 2], F32)
        rstd = sb("rstd", [P, 3, TT], F32)
        shift = sb("shift", [P, 3, TT], F32)
        x1T = sb("x1T", [P, 2, KT, T], F16)
        xT = sb("xT", [P, 2, KT, T], F16)
        latents = sb("latents", [P, 2, 2, T], F16)
        values_of = sb("values_of", [P, 2, 2, TT, H, VW], F16)
        left = sb("left", [P, 2, T], F16)
        neg_max = sb("neg_max", [P, STEPS], F32)
        probs = sb("probs", [P, TT, T], F32)
        probsT = sb("probsT", [P, 4, 2, T], F16)
        sums = sb("sums", [P, 2, TT], F32)
        yT = sb("yT", [P, 2, KT, T], F16)
        qT = sb("qT", [P, 2, NG, T], F16)
        ctxT = sb("ctxT", [P, 2, KT, S], F16)
        k_sum = sb("k_sum", [P, NG, S], F32)
        k_diag = sb("k_diag", [P, 2, NG, HG * S], F16)
        c_values = sb("c_values", [S, 2, H, VW], F16)
        c_max = sb("c_max", [P, 2, H], F32)
        c_probsT = sb("c_probsT", [S, NG, 2, HG * P], F16)
        c_sums = sb("c_sums", [P, 2, H], F32)
        score_bank = [keep.enter_context(nc.psum_tensor(f"score_bank{i}", [P, 512], F32)) for i in range(2)]
        probsT_bank = [keep.enter_context(nc.psum_tensor(f"probsT_bank{i}", [P, 512], F32)) for i in range(2)]
        y_bank = keep.enter_context(nc.psum_tensor("y_bank", [P, 512], F32))
        job_bank = [keep.enter_context(nc.psum_tensor(f"job_bank{i}", [P, 512], F32)) for i in range(3)]

        res_loaded, ctx_loaded = sem("res_loaded"), sem("ctx_loaded")
        later_high, later_low = sem("later_high"), sem("later_low")
        later_scaled = sem("later_scaled")
        wv_high, wv_low = sem("wv_high"), sem("wv_low")
        x2_stored, xn_stored, xT_stored = sem("x2_stored"), sem("xn_stored"), sem("xT_stored")
        ln_stats, ln_moments, ln_pool, ln_scale, ln_done = (
            [sem(f"{name}{n + 1}") for n in range(3)] for name in ("ln_stats", "ln_moments", "ln_pool", "ln_scale", "ln_done"))
        stores_passed = sem("stores_passed")
        ones_set = sem("ones_set")
        dve_waits, pool_waits = sem("dve_waits"), sem("pool_waits")
        scores_ready, max_done, exp_done = sem("scores_ready"), sem("max_done"), sem("exp_done")
        pT_ready, pT_high, pT_low = sem("pT_ready"), sem("pT_high"), sem("pT_low")
        y_ready, sums_done, y_normed = sem("y_ready"), sem("sums_done"), sem("y_normed")
        job_ready, job_high, job_done = sem("job_ready"), sem("job_high"), sem("job_done")
        res_biased, x1_biased = sem("res_biased"), sem("x1_biased")
        k_high, k_low = sem("k_high"), sem("k_low")
        c_max_done, c_exp_done, c_sums_done = sem("c_max_done"), sem("c_exp_done"), sem("c_sums_done")

        later_raw = {"wo": x_res[:], "xwq": xn[:]}
        for name, buffer in (("xwk", xT), ("xwv", yT), ("xwo", qT)):
            later_raw[name] = buffer[:].rearrange("p h c t -> p (h c t)").bitcast(F32).rearrange("p (a c) -> p a c", a=KT)
        LATER_STEPS = {8 * k + 10: name for k, name in enumerate(later_raw)}

        x_v = x.rearrange("b (a p) c -> b p a c", p=P)
        x2_v = x2_dram.rearrange("(b a p) c -> b p a c", p=P, a=TT)
        xn_v = xn_dram[0:B * T].rearrange("(b a p) c -> b p a c", p=P, a=TT)

        def of_batch(v, b, names):
            return v[b] if isinstance(b, int) else v[bass.ds(b, 1)].rearrange(f"o {names} -> (o {names.split()[0]}) " + " ".join(names.split()[1:]))

        def low(out, in_, scale, high):
            return nc.vector.scalar_tensor_tensor(out, in_, scale, high, ALU.mult, ALU.subtract)

        def jobs_of(heads, rest, ahead):
            steps = {k: [] for k in range(H * TT)}
            if rest:
                for k, job in REST:
                    steps[k].append(job)
            if ahead:
                for k, job in AHEAD_JOBS:
                    steps[k].append(job)
            if heads:
                for h in range(1, H):
                    k = min((TT * h - 3, TT * h - 4, TT * h - 5, TT * h - 2), key=lambda k: len(steps[k]) // 2 if k >= 0 else 9)
                    steps[k].append(("left", h))
            assert all(len(v) <= 3 for v in steps.values())
            return steps

        class Turn:
            def __init__(self, b, parity, heads, rest, ahead, jobs_before, high_before):
                self.b, self.heads, self.rest, self.ahead = b, heads, rest, ahead
                self.latent, self.values = latents[:, parity], values_of[:, parity]
                self.next_latent, self.next_values = latents[:, 1 - parity], values_of[:, 1 - parity]
                self.steps = jobs_of(heads, rest, ahead)
                self.order = [j for k in sorted(self.steps) for j in self.steps[k]]
                self.high_order = [j for j in self.order if j[0] not in UNSPLIT]
                self.jobs, self.highs = jobs_before, high_before
                self.g = b * (H * TT)

            def number(self, job):
                return self.order.index(job)

            def done(self, job):
                return self.jobs + self.number(job) + 1

            def high(self, job):
                return self.highs + self.high_order.index(job) + 1

            def bank(self, job):
                return job_bank[self.number(job) % 3]

            def bank_free(self, job):
                n = self.number(job)
                return self.jobs + (n - 2 if n >= 3 else 0)

        def turns(eng, body):
            n_first, h_first = count_jobs(jobs_of(True, False, True))
            n_full, h_full = count_jobs(jobs_of(True, True, True))
            n_last, h_last = count_jobs(jobs_of(True, True, False))
            first = len(START_JOBS)
            body(Turn(0, 0, True, False, True, first, first))
            with eng.Fori(0, (B - 2) // 2) as i:
                for k in range(2):
                    done = i * 2 + k
                    body(Turn(done + 1, 1 - k, True, True, True, done * n_full + (first + n_first), done * h_full + (first + h_first)))
            n, h = first + n_first + (B - 2) * n_full, first + h_first + (B - 2) * h_full
            body(Turn(B - 1, (B - 1) % 2, True, True, False, n, h))
            body(Turn(B, B % 2, False, True, False, n + n_last, h + h_last))

        def count_jobs(jobs):
            order = [j for v in jobs.values() for j in v]
            return len(order), sum(j[0] not in UNSPLIT for j in order)

        class Start:
            order = high_order = START_JOBS
            next_latent, next_values = latents[:, 0], values_of[:, 0]
            jobs = highs = 0
            b = -1
            number, done, high, bank, bank_free = Turn.number, Turn.done, Turn.high, Turn.bank, Turn.bank_free

        start = Start()

        with nc.Block() as block:
            @block.sync
            def _(sp):
                def load_x(b, names="p a c"):
                    sp.dma_start(x_in[:], of_batch(x_v, b, "p a c")).then_inc(x_loaded, 16)

                def load_later(names):
                    for name in names:
                        src = {"wo": woT, "xwq": xwqT, "xwk": xwkT, "xwv": xwvT, "xwo": xwoT}[name]
                        sp.dma_start(later_raw[name], src.rearrange("(a p) n -> p a n", p=P)).then_inc(w_loaded[name], 16)

                load_later(["wo"])
                sp.sem_inc(stores_passed, 1)

                def body(t):
                    b = t.b
                    if t.ahead:
                        sp.wait_ge(job_ready, t.jobs if t.rest else start.done(("x1T", KT - 1)))
                        load_x(b + 1)
                    if not t.rest:
                        load_later(["xwq", "xwk", "xwv", "xwo"])
                        sp.wait_ge(later_low, len(later_raw))
                    if t.rest:
                        sp.dma_start(x_res[:], of_batch(x_v, b - 1, "p a c")).then_inc(res_loaded, 16)
                        sp.wait_ge(job_ready, t.jobs)
                        sp.dma_start(ctx_sb[:], of_batch(ctx_in, b - 1, "s c")).then_inc(ctx_loaded, 16)
                        sp.wait_ge(job_done, t.done(("xo", TT - 1)))
                        sp.dma_start(of_batch(x2_v, b - 1, "p a c"), x_res[:]).then_inc(x2_stored, 16)
                        sp.wait_ge(ln_done[2], b * TT)
                        sp.dma_start(of_batch(xn_v, b - 1, "p a c"), xn[:]).then_inc(xn_stored, 16)
                        sp.wait_ge(job_done, t.done(("x3T", KT - 1)))
                        sp.dma_start(of_batch(xT_dram, b - 1, "p n"), xT[:].rearrange("p h c t -> p (h c t)")).then_inc(xT_stored, 16)
                        for s in (x2_stored, xn_stored, xT_stored):
                            sp.wait_ge(s, b * 16)
                        sp.sem_inc(stores_passed, 1)

                turns(sp, body)

            @block.gpsimd
            def _(pool):
                def scale_of(n, i):
                    wait_apart(pool, ln_moments[n], i * TT + TT, pool_waits)
                    nc.gpsimd.tensor_scalar(rstd[:, n], moments[:, n, :, 1], 1.0, EPS, ALU.mult, ALU.add).then_inc(ln_pool[n], 1)
                    pool.wait_ge(ln_pool[n], i * 3 + 1)
                    nc.gpsimd.tensor_tensor(rstd[:, n], rstd[:, n], neg_half[:], ALU.pow).then_inc(ln_pool[n], 1)
                    pool.wait_ge(ln_pool[n], i * 3 + 2)
                    nc.gpsimd.tensor_tensor(shift[:, n], moments[:, n, :, 0], rstd[:, n], ALU.mult).then_inc(ln_pool[n], 1)
                    wait_apart(pool, ln_pool[n], i * 3 + 3, pool_waits)
                    nc.gpsimd.tensor_scalar(shift[:, n], shift[:, n], -1.0, 0.0, ALU.mult, ALU.add).then_inc(ln_scale[n], 1)

                def normalise_input(i):
                    wait_apart(pool, ln_scale[0], i + 1, pool_waits)
                    for tile in range(TT):
                        nc.gpsimd.tensor_scalar(x_in[:, tile], x_in[:, tile], rstd[:, 0, tile:tile + 1], shift[:, 0, tile:tile + 1],
                                                ALU.mult, ALU.add).then_inc(ln_done[0], 1)

                scale_of(0, 0)
                normalise_input(0)
                pool.wait_ge(bias_loaded, 16 * 6)
                for t in (q_bias, k_bias):
                    nc.gpsimd.tensor_scalar(t[:], t[:], WSCALE, None, ALU.mult).then_inc(bias_scaled, 1)
                nc.gpsimd.tensor_scalar(raw_bias, raw_bias, WSCALE, 0.0, ALU.mult, ALU.add).then_inc(bias_scaled, 1)
                pool.wait_ge(bias_scaled, 3)
                nc.gpsimd.tensor_copy(value_bias[:], raw_bias).then_inc(bias_scaled, 1)
                pool.wait_ge(bias_scaled, 4)
                nc.gpsimd.tensor_tensor(value_bias[R:P], raw_bias[R:P], value_bias[R:P], ALU.subtract).then_inc(bias_scaled, 1)
                pool.wait_ge(bias_scaled, 5)
                for parity in range(2):
                    nc.gpsimd.memset(values_of[:, parity, 0, :, :, HD:VW], WSCALE).then_inc(ones_set, 1)
                nc.gpsimd.memset(c_values[:, 0, :, HD:VW], WSCALE).then_inc(ones_set, 1)
                nc.gpsimd.memset(k_diag[:], 0.0).then_inc(ones_set, 1)

                def body(t):
                    b = t.b
                    if t.rest:
                        pool.wait_ge(res_loaded, b * 16)
                        for tile in range(TT):
                            nc.gpsimd.tensor_tensor(x_res[:, tile], x_res[:, tile], ob_row[:], ALU.add).then_inc(res_biased, 1)
                        scale_of(1, b - 1)
                    if t.ahead:
                        scale_of(0, b + 1)
                        normalise_input(b + 1)
                    if not t.rest:
                        for n, (name, raw) in enumerate(later_raw.items()):
                            pool.wait_ge(later_high, n + 1)
                            nc.gpsimd.tensor_scalar(raw, raw, WSCALE, 0.0, ALU.mult, ALU.add).then_inc(later_scaled, 1)
                            pool.wait_ge(later_scaled, n + 1)
                            nc.gpsimd.tensor_tensor(W[name][:, 1], raw, W[name][:, 0], ALU.subtract).then_inc(later_low, 1)
                    if t.rest:
                        pool.wait_ge(ln_done[1], b * TT)
                        for tile in range(TT):
                            nc.gpsimd.tensor_tensor(x_res[:, tile], x_res[:, tile], xob_row[:], ALU.add).then_inc(x1_biased, 1)
                        scale_of(2, b - 1)

                turns(pool, body)

            @block.scalar
            def _(act):
                def copy_high(out, in_, scale=1.0):
                    return nc.scalar.activation(out, in_, ACT.Copy, scale=scale)

                def job(t, name, i):
                    if name in UNSPLIT:
                        return
                    act.wait_ge(job_ready, t.done((name, i)))
                    src = t.bank((name, i))
                    if name == "latent":
                        ins = copy_high(t.next_latent[:, 0], src[:], 0.25 / WSCALE)
                    elif name == "v":
                        ins = copy_high(t.next_values[:, 0, i, :, 0:HD], src[:].rearrange("p (h d) -> p h d", h=H))
                    elif name == "left":
                        ins = copy_high(left[:, i % 2], src[:], 0.5 / 16)
                    elif name == "x1T":
                        ins = copy_high(x1T[:, 0, i], src[:])
                    elif name == "x2T":
                        if i == 0:
                            act.wait_ge(stores_passed, t.b)
                        ins = copy_high(xT[:, 0, i], src[:])
                    elif name == "x3T":
                        ins = copy_high(xT[:, 0, i], src[:])
                    elif name in ("yT", "y2T"):
                        ins = copy_high(yT[:, 0, i], src[:])
                    elif name == "ctxT":
                        ins = copy_high(ctxT[:, 0], src[:, 0:KT * S].rearrange("p (c s) -> p c s", c=KT))
                    elif name == "cv":
                        ins = copy_high(c_values[:, 0, :, 0:HD], src[0:S].rearrange("p (h d) -> p h d", h=H))
                    elif name == "q":
                        ins = nc.scalar.activation(qT[:, 0, i], src[:], ACT.Identity, bias=q_bias[:, i:i + 1], scale=1.0)
                    elif name == "cpT":
                        ins = copy_high(c_probsT[:, i % NG, 0], src[0:S])
                    ins.then_inc(job_high, 1)

                def normalise(t, n):
                    act.wait_ge(ln_scale[n], t.b)
                    for tile in range(TT):
                        nc.scalar.activation(xn[:, tile], x_res[:, tile], ACT.Identity, bias=shift[:, n, tile:tile + 1],
                                             scale=rstd[:, n, tile:tile + 1]).then_inc(ln_done[n], 1)

                def after_job(t, name, i):
                    if name == "k":
                        act.wait_ge(job_done, t.done((name, i)))
                        for j in range(HG):
                            rows = slice(j * HD, j * HD + HD)
                            copy_high(k_diag[rows, 0, :, j * S:j * S + S], k_sum[rows]).then_inc(k_high, 1)
                    if name == "cs" and i % NG == NG - 1:
                        act.wait_ge(job_done, t.done((name, i)))
                        tile = i // NG
                        nc.scalar.activation(c_probs[:, tile % 2], c_probs[:, tile % 2], ACT.Exp, scale=XSCALE).then_inc(c_exp_done, 1)

                def probs_high(t, j):
                    n = (j % TT + 1) * P
                    act.wait_ge(pT_ready, t.g + j + 1)
                    if j >= 4:
                        act.wait_ge(y_ready, t.g + j - 3)
                    copy_high(probsT[:, j % 4, 0, 0:n], probsT_bank[j % 2][:, 0:n]).then_inc(pT_high, 1)

                def exp_tile(t, k):
                    n = (k % TT + 1) * P
                    act.wait_ge(max_done, t.g + k + 1)
                    nc.scalar.activation(probs[:, k % TT, 0:n], score_bank[k % 2][:, 0:n], ACT.Exp,
                                         bias=neg_max[:, k % STEPS:k % STEPS + 1], scale=1.0).then_inc(exp_done, 1)

                def body(t):
                    for k in range(H * TT + 2):
                        for j in t.steps.get(k - 2, []):
                            after_job(t, *j)
                        for j in t.steps.get(k - 1, []):
                            job(t, *j)
                        if t.heads and 1 <= k <= H * TT:
                            exp_tile(t, k - 1)
                        if t.heads and k >= 2:
                            probs_high(t, k - 2)
                        if not t.rest and k in LATER_STEPS:
                            name = LATER_STEPS[k]
                            act.wait_ge(w_loaded[name], 16)
                            nc.scalar.activation(W[name][:, 0], later_raw[name], ACT.Copy, scale=WSCALE).then_inc(later_high, 1)
                        if t.rest and k == XN2_STEP:
                            act.wait_ge(stores_passed, t.b)
                            normalise(t, 1)
                        if t.rest and k == XN3_STEP:
                            normalise(t, 2)

                act.wait_ge(w_loaded["wv"], 16)
                nc.scalar.activation(W["wv"][:, 0], y[:], ACT.Copy, scale=WSCALE).then_inc(wv_high, 1)
                for j in START_JOBS:
                    job(start, *j)
                act.wait_ge(bias_scaled, 5)
                act.wait_ge(ones_set, 4)
                turns(act, body)

            @block.vector
            def _(dve):
                def moments_of(n, i, tile, src):
                    nc.vector.bn_stats(stats[:, n, tile], src[:, tile]).then_inc(ln_stats[n], 1)
                    for done in ([tile - 1] if tile > 0 else []) + ([tile] if tile == TT - 1 else []):
                        wait_apart(dve, ln_stats[n], i * TT + done + 1, dve_waits)
                        nc.vector.bn_aggr(moments[:, n, done], stats[:, n, done]).then_inc(ln_moments[n], 1)

                def cross_scores(src, i):
                    return src[:, 0:HG * S].rearrange("p (h s) -> p h s", h=HG), c_max[:, i // NG % 2, i % NG * HG:i % NG * HG + HG]

                def cross_heads(src, i):
                    return src[:, 0:8 * VW].rearrange("p (h d) -> p h d", h=8), c_sums[:, i // 2 % 2, i % 2 * 8:i % 2 * 8 + 8]

                def first_half(t, name, i):
                    if name == "cs":
                        dve.wait_ge(job_ready, t.done((name, i)))
                        scores, top = cross_scores(t.bank((name, i)), i)
                        nc.vector.tensor_reduce(top, scores, AX_X, ALU.max).then_inc(c_max_done, 1)
                    if name == "cy":
                        dve.wait_ge(job_ready, t.done((name, i)))
                        heads, total = cross_heads(t.bank((name, i)), i)
                        nc.vector.reciprocal(total, heads[:, :, HD]).then_inc(c_sums_done, 1)

                def job(t, name, i):
                    src = t.bank((name, i))
                    if name not in UNSPLIT:
                        dve.wait_ge(job_high, t.high((name, i)))
                    elif name not in ("cs", "cy"):
                        dve.wait_ge(job_ready, t.done((name, i)))
                    if name == "latent":
                        ins = low(t.next_latent[:, 1], src[:], 0.25 / WSCALE, t.next_latent[:, 0])
                    elif name == "v":
                        ins = low(t.next_values[:, 1, i, :, 0:HD], src[:].rearrange("p (h d) -> p h d", h=H), 1.0,
                                  t.next_values[:, 0, i, :, 0:HD])
                    elif name == "left":
                        ins = low(left[R:P, i % 2], src[R:P], 0.5 / 16, left[R:P, i % 2])
                    elif name == "x1T":
                        ins = low(x1T[:, 1, i], src[:], 1.0, x1T[:, 0, i])
                    elif name in ("x2T", "x3T"):
                        ins = low(xT[:, 1, i], src[:], 1.0, xT[:, 0, i])
                    elif name in ("yT", "y2T"):
                        ins = low(yT[:, 1, i], src[:], 1.0, yT[:, 0, i])
                    elif name == "ctxT":
                        ins = low(ctxT[:, 1], src[:, 0:KT * S].rearrange("p (c s) -> p c s", c=KT), 1.0, ctxT[:, 0])
                    elif name == "k":
                        ins = nc.vector.tensor_tensor(k_sum[:], src[:, 0:NG * S].rearrange("p (c s) -> p c s", c=NG),
                                                      k_bias[:].unsqueeze(2).broadcast_to([P, NG, S]), ALU.add)
                    elif name == "cv":
                        ins = low(c_values[:, 1, :, 0:HD], src[0:S].rearrange("p (h d) -> p h d", h=H), 1.0, c_values[:, 0, :, 0:HD])
                    elif name == "o":
                        dve.wait_ge(res_biased, (t.b - 1) * TT + i + 1)
                        ins = nc.vector.scalar_tensor_tensor(x_res[:, i], src[:], 1.0 / WSCALE, x_res[:, i], ALU.mult, ALU.add)
                    elif name == "q":
                        ins = nc.vector.scalar_tensor_tensor(qT[:, 1, i], src[:], q_bias[:, i:i + 1], qT[:, 0, i], ALU.add, ALU.subtract)
                    elif name == "cs":
                        tile, m = i // NG, i % NG
                        scores, top = cross_scores(src, i)
                        dve.wait_ge(c_max_done, (t.b - 1) * (TT * NG) + i + 1)
                        ins = nc.vector.tensor_tensor(c_probs[:, tile % 2, m * HG:m * HG + HG], scores,
                                                      top.unsqueeze(2).broadcast_to([P, HG, S]), ALU.subtract)
                    elif name == "cpT":
                        ins = low(c_probsT[:, i % NG, 1], src[0:S], 1.0, c_probsT[:, i % NG, 0])
                    elif name == "cy":
                        tile, half = i // 2, i % 2
                        heads, total = cross_heads(src, i)
                        dve.wait_ge(c_sums_done, (t.b - 1) * (2 * TT) + i + 1)
                        ins = nc.vector.tensor_tensor(
                            xn[:, tile, half * 256:half * 256 + 256].rearrange("p (h d) -> p h d", h=8), heads[:, :, 0:HD],
                            total.unsqueeze(2).broadcast_to([P, 8, HD]), ALU.mult)
                    elif name == "xo":
                        dve.wait_ge(x1_biased, (t.b - 1) * TT + i + 1)
                        ins = nc.vector.scalar_tensor_tensor(x_res[:, i], src[:], 1.0 / WSCALE, x_res[:, i], ALU.mult, ALU.add)
                    elif name == "logits":
                        at = (t.b - 1) * TT
                        dst = logits[:, at:at + TT] if isinstance(t.b, int) else logits[:, bass.ds(at, TT)]
                        ins = nc.vector.tensor_scalar(dst, src[:, 0:TT * NE].rearrange("p (t e) -> p t e", t=TT), 1.0 / WSCALE, None,
                                                      ALU.mult)
                    ins.then_inc(job_done, 1)
                    if name == "k":
                        wait_apart(dve, job_done, t.done((name, i)), dve_waits)

                def between(t, k):
                    for name, i in t.steps.get(k - 1, []):
                        if name in ("o", "xo"):
                            wait_apart(dve, job_done, t.done((name, i)), dve_waits)
                            moments_of(1 if name == "o" else 2, t.b - 1, i, x_res)
                    if t.rest and k == K_LOW_STEP:
                        for j in range(HG):
                            dve.wait_ge(k_high, (t.b - 1) * HG + j + 1)
                            rows = slice(j * HD, j * HD + HD)
                            nc.vector.tensor_tensor(k_diag[rows, 1, :, j * S:j * S + S], k_sum[rows],
                                                    k_diag[rows, 0, :, j * S:j * S + S], ALU.subtract).then_inc(k_low, 1)
                    if t.ahead and k in LN1_STEPS:
                        dve.wait_ge(x_loaded, (t.b + 1) * 16 + 16)
                        moments_of(0, t.b + 1, LN1_STEPS.index(k), x_in)

                def max_tile(t, k):
                    n = (k % TT + 1) * P
                    dve.wait_ge(scores_ready, t.g + k + 1)
                    nc.vector.tensor_reduce(neg_max[:, k % STEPS:k % STEPS + 1], score_bank[k % 2][:, 0:n], AX_X, ALU.max,
                                            negate=True).then_inc(max_done, 1)

                def probs_low(t, j):
                    n = (j % TT + 1) * P
                    dve.wait_ge(pT_high, t.g + j + 1)
                    nc.vector.tensor_tensor(probsT[:, j % 4, 1, 0:n], probsT_bank[j % 2][:, 0:n], probsT[:, j % 4, 0, 0:n],
                                            ALU.subtract).then_inc(pT_low, 1)

                def head_sums(t, h):
                    i = t.b * H + h
                    dve.wait_ge(y_ready, (i + 1) * TT)
                    src = y_bank[:, 0:TT * VW].rearrange("p (t d) -> p t d", t=TT)
                    nc.vector.reciprocal(sums[:, h % 2], src[:, :, HD]).then_inc(sums_done, 1)

                def head_out(t, h):
                    src = y_bank[:, 0:TT * VW].rearrange("p (t d) -> p t d", t=TT)
                    dve.wait_ge(sums_done, t.b * H + h + 1)
                    nc.vector.tensor_tensor(y[:, :, h * HD:h * HD + HD], src[:, :, 0:HD],
                                            sums[:, h % 2].unsqueeze(2).broadcast_to([P, TT, HD]), ALU.mult).then_inc(y_normed, 1)

                def body(t):
                    for k in range(H * TT + 5):
                        jobs = t.steps.get(k - 1, [])
                        whole = next((n for n, j in enumerate(jobs) if j[0] in ("cs", "cy")), len(jobs))
                        for j in jobs[:whole]:
                            job(t, *j)
                        for j in jobs[whole:]:
                            first_half(t, *j)
                        if t.heads and k % TT == 0 and k >= 8:
                            head_sums(t, k // TT - 2)
                        if t.heads and k < H * TT:
                            max_tile(t, k)
                        for j in jobs[whole:]:
                            job(t, *j)
                        if t.heads and k % TT == 0 and k >= 8:
                            head_out(t, k // TT - 2)
                        if t.heads and 2 <= k < H * TT + 2:
                            probs_low(t, k - 2)
                        between(t, k)

                for tile in range(TT):
                    dve.wait_ge(x_loaded, 16)
                    moments_of(0, 0, tile, x_in)
                dve.wait_ge(wv_high, 1)
                nc.vector.scalar_tensor_tensor(W["wv"][:, 1], y[:], WSCALE, W["wv"][:, 0], ALU.mult, ALU.subtract).then_inc(wv_low, 1)
                for j in START_JOBS:
                    job(start, *j)
                dve.wait_ge(bias_scaled, 5)
                turns(dve, body)

            @block.tensor
            def _(pe):
                def product(out, left_high, left_low, right_high, right_low, n=KT, more=False):
                    for c in range(n):
                        nc.tensor.matmul(out, left_high(c), right_high(c), start=(c == 0), stop=False)
                        nc.tensor.matmul(out, left_high(c), right_low(c), start=False, stop=False)
                        last = nc.tensor.matmul(out, left_low(c), right_high(c), start=False, stop=(c == n - 1 and not more))
                    return last

                def rows_times(out, src, tile, w, more=False):
                    ts = slice(tile * P, tile * P + P)
                    return product(out, lambda c: src[:, 0, c, ts], lambda c: src[:, 1, c, ts], lambda c: W[w][:, 0, c], lambda c: W[w][:, 1, c],
                                   more=more)

                def columns_times(out, w, m, right, n=None):
                    ms = slice(m * P, m * P + P)
                    return product(out, lambda c: W[w][:, 0, c, ms], lambda c: W[w][:, 1, c, ms], lambda c: right[:, 0, c], lambda c: right[:, 1, c])

                def transposes(out, src, c):
                    for tile in range(TT):
                        last = nc.tensor.transpose(out[:, tile * P:tile * P + P], src[:, tile, c * P:c * P + P], ident[:])
                    return last

                def job(t, name, i):
                    out = t.bank((name, i))
                    b = t.b
                    wait(pe, job_done, t.bank_free((name, i)))
                    if name == "x1T":
                        pe.wait_ge(ln_done[0], (b + 1) * TT + TT)
                        ins = transposes(out, x_in, i)
                    elif name == "latent":
                        pe.wait_ge(job_done, t.done(("x1T", KT - 1)))
                        ins = product(out[:], lambda c: w_basis[:, 0, c], lambda c: w_basis[:, 1, c],
                                      lambda c: x1T[:, 0, c], lambda c: x1T[:, 1, c])
                    elif name == "v":
                        rows_times(out[:], x1T, i, "wv", more=True)
                        ins = nc.tensor.matmul(out[:], first_rows[:], value_bias[:, 0], start=False, stop=True)
                    elif name == "left":
                        if i == 0:
                            pe.wait_ge(job_done, t.done(("latent", 0)))
                        of_head = t.next_latent if i == 0 else t.latent
                        nc.tensor.matmul(out[:], head_mat[:, i, :], of_head[:, 0], start=True, stop=False)
                        ins = nc.tensor.matmul(out[:], head_mat[:, i, :], of_head[:, 1], start=False, stop=True)
                    elif name == "yT":
                        pe.wait_ge(y_normed, b * H)
                        ins = transposes(out, y, i)
                    elif name == "o":
                        pe.wait_ge(job_done, t.done(("yT", KT - 1)))
                        ins = rows_times(out[:], yT, i, "wo")
                    elif name == "ctxT":
                        pe.wait_ge(ctx_loaded, b * 16)
                        for c in range(KT):
                            ins = nc.tensor.transpose(out[:, c * S:c * S + S], ctx_sb[:, c * P:c * P + P], ident[0:S, 0:S])
                    elif name == "k":
                        pe.wait_ge(job_done, t.done(("ctxT", 0)))
                        for m in range(NG):
                            ins = columns_times(out[:, m * S:m * S + S], "xwk", m, ctxT)
                    elif name == "cv":
                        product(out[0:S], lambda c: ctxT[:, 0, c], lambda c: ctxT[:, 1, c],
                                lambda c: W["xwv"][:, 0, c], lambda c: W["xwv"][:, 1, c], more=True)
                        ins = nc.tensor.matmul(out[0:S], first_rows[:, 0:S], value_bias[:, 1], start=False, stop=True)
                    elif name in ("x2T", "x3T"):
                        pe.wait_ge(ln_done[1 if name == "x2T" else 2], b * TT)
                        ins = transposes(out, xn, i)
                    elif name == "q":
                        pe.wait_ge(job_done, t.done(("x2T", KT - 1)))
                        ins = columns_times(out[:], "xwq", i, xT)
                    elif name == "cs":
                        tile, m = i // NG, i % NG
                        if i == 0:
                            pe.wait_ge(job_done, t.done(("q", NG - 1)))
                            pe.wait_ge(k_low, b * HG)
                        ts = slice(tile * P, tile * P + P)
                        ins = product(out[:, 0:HG * S], lambda c: qT[:, 0, m, ts], lambda c: qT[:, 1, m, ts],
                                      lambda c: k_diag[:, 0, m], lambda c: k_diag[:, 1, m], n=1)
                    elif name == "cpT":
                        tile, m = i // NG, i % NG
                        pe.wait_ge(c_exp_done, (b - 1) * TT + tile + 1)
                        for h in range(HG):
                            ins = nc.tensor.transpose(out[0:S, h * P:h * P + P], c_probs[:, tile % 2, m * HG + h], ident[:])
                    elif name == "cy":
                        tile, half = i // 2, i % 2
                        pe.wait_ge(job_done, t.done(("cpT", tile * NG + half * 2 + 1)))
                        for n in range(8):
                            m, h = half * 2 + n // HG, n % HG
                            o = out[:, n * VW:n * VW + VW]
                            ph = c_probsT[:, m, 0, h * P:h * P + P]
                            pl = c_probsT[:, m, 1, h * P:h * P + P]
                            hh = m * HG + h
                            nc.tensor.matmul(o, ph, c_values[:, 0, hh, :], start=True, stop=False)
                            nc.tensor.matmul(o[:, 0:HD], ph, c_values[:, 1, hh, 0:HD], start=False, stop=False)
                            ins = nc.tensor.matmul(o, pl, c_values[:, 0, hh, :], start=False, stop=True)
                    elif name == "y2T":
                        pe.wait_ge(job_done, t.done(("cy", 2 * TT - 1)))
                        ins = transposes(out, xn, i)
                    elif name == "xo":
                        pe.wait_ge(job_done, t.done(("y2T", KT - 1)))
                        ins = rows_times(out[:], yT, i, "xwo")
                    elif name == "logits":
                        pe.wait_ge(job_done, t.done(("x3T", KT - 1)))
                        for tile in range(TT):
                            ts = slice(tile * P, tile * P + P)
                            ins = product(out[:, tile * NE:tile * NE + NE], lambda c: xT[:, 0, c, ts], lambda c: xT[:, 1, c, ts],
                                          lambda c: router[:, 0, c], lambda c: router[:, 1, c])
                    ins.then_inc(job_ready, 1)

                def score_tile(t, k):
                    tile, h = k % TT, k // TT
                    n = (tile + 1) * P
                    if tile == 0 and h > 0:
                        pe.wait_ge(job_done, t.done(("left", h)))
                    wait(pe, exp_done, t.g + (k - 1 if k >= 2 else 0))
                    lhs = left[:, h % 2, tile * P:tile * P + P]
                    out = score_bank[k % 2]
                    nc.tensor.matmul(out[:, 0:n], lhs, t.latent[:, 0, 0:n], start=True, stop=False)
                    nc.tensor.matmul(out[:, 0:n], lhs, t.latent[:, 1, 0:n], start=False, stop=False)
                    nc.tensor.matmul(out[:, n - P:n], big_ident[:], causal[:], start=False, stop=True).then_inc(scores_ready, 1)

                def transpose_tile(t, j):
                    tile = j % TT
                    pe.wait_ge(exp_done, t.g + j + 1)
                    wait(pe, pT_low, t.g + (j - 1 if j >= 2 else 0))
                    for u in range(tile + 1):
                        last = nc.tensor.transpose(probsT_bank[j % 2][:, u * P:u * P + P], probs[:, tile, u * P:u * P + P], ident[:])
                    last.then_inc(pT_ready, 1)

                def values_tile(t, j):
                    tile, h = j % TT, j // TT
                    pe.wait_ge(pT_low, t.g + j + 1)
                    if tile == 0:
                        wait(pe, y_normed, t.b * H + h)
                    out = y_bank[:, tile * VW:(tile + 1) * VW]
                    for u in range(tile + 1):
                        ph = probsT[:, j % 4, 0, u * P:u * P + P]
                        pl = probsT[:, j % 4, 1, u * P:u * P + P]
                        nc.tensor.matmul(out, ph, t.values[:, 0, u, h, :], start=(u == 0), stop=False)
                        nc.tensor.matmul(out[:, 0:HD], ph, t.values[:, 1, u, h, 0:HD], start=False, stop=False)
                        last = nc.tensor.matmul(out, pl, t.values[:, 0, u, h, :], start=False, stop=(u == tile))
                    last.then_inc(y_ready, 1)

                def body(t):
                    if t.heads:
                        pe.wait_ge(job_done, t.jobs)
                    for k in range(H * TT + 4):
                        if t.heads and k < H * TT:
                            score_tile(t, k)
                        if t.heads and 2 <= k < H * TT + 2:
                            transpose_tile(t, k - 2)
                        for j in t.steps.get(k, []):
                            job(t, *j)
                        if t.heads and k >= 4 and k % TT != 0:
                            if k % TT == 1:
                                values_tile(t, k - 5)
                            values_tile(t, k - 4)
                    if not t.rest:
                        pe.wait_ge(later_low, len(later_raw))

                for j in START_JOBS:
                    if j == ("v", 0):
                        pe.wait_ge(wv_low, 1)
                        pe.wait_ge(bias_scaled, 5)
                    job(start, *j)
                pe.wait_ge(ones_set, 4)
                turns(pe, body)


NE, TOPK = 8, 2
F = 1024
FT = F // P
N = B * T
TILES = N // P
SLOT_TILES = -(-(TOPK * N // P + NE - 1) // 2) * 2
NM = 2 * NE
X_SLOT, RAW_SLOT = 12, 13
XT_SLOT = 14
W2_STEPS = (4, 6)
POOL_PIECES = (0, 1, 2)


def build_ffn(nc, sem, logits, x2_dram, out, r_bias, sw1, sw3, sw2, ew1, ew2, constants, xn_dram, xT_dram, slot_dram):
    with ExitStack() as keep:
        def sb(name, shape, dt):
            return keep.enter_context(nc.sbuf_tensor(name, shape, dt))

        experts = sb("experts", [P, NM, 2, KT, C], F16)
        slots = sb("slots", [P, TOPK, TILES, 1], mybir.dt.uint32)
        slot_rows = sb("slot_rows", [P, TOPK, TILES, 2], F32)
        tile_expert = sb("tile_expert", [P, SLOT_TILES], mybir.dt.int32)
        w1, w3 = sb("w1", [P, 2, KT, F], F16), sb("w3", [P, 2, KT, F], F16)
        w2 = sb("w2", [P, 2, FT, C], F16)

        def bytes_of(k):
            return experts[:, k].rearrange("p a b c -> p (a b c)").bitcast(F32)

        x_tiles = bytes_of(X_SLOT).rearrange("p (a c) -> p a c", a=TT)
        raw_tile = bytes_of(RAW_SLOT).rearrange("p (a c) -> p a c", a=KT)

        def matrix(e):
            return ew1[e // 2] if e % 2 == 0 else ew2[e // 2]

        bank = [keep.enter_context(nc.psum_tensor(f"ffn_bank{i}", [P, 512], F32)) for i in range(8)]
        x2_v = x2_dram.rearrange("(g a p) c -> g p a c", p=P, a=TT)
        out_v = out[0:N].rearrange("(g a p) c -> g p a c", p=P, a=TT)
        xT = [experts[:, XT_SLOT + k] for k in range(2)]
        xT_loaded, x_loaded = [sem("xT_loaded0"), sem("xT_loaded1")], sem("s_x_loaded")

        raw_sw = [bytes_of(4 + n) for n in range(6)]
        sw_loaded, sw_high, sw_low = [sem(f"sw_loaded{n}") for n in range(6)], sem("sw_high"), sem("sw_low")

        def piece(n):
            w, a = n // 2, n % 2
            return [(w1[:, h, 2 * a:2 * a + 2], w3[:, h, 2 * a:2 * a + 2], w2[:, h, 4 * a:4 * a + 4])[w] for h in range(2)]

        def raw_piece(n):
            return raw_sw[n].rearrange("p (a c) -> p a c", c=piece(n)[0].shape[2])

        def load_piece(eng, n):
            src = (sw1, sw3, sw2)[n // 2].rearrange("(h a p) n -> h p a n", p=P, h=2)[n % 2]
            eng.dma_start(raw_piece(n), src).then_inc(sw_loaded[n], 16)

        def piece_high(act, n):
            act.wait_ge(sw_loaded[n], 16)
            nc.scalar.activation(piece(n)[0], raw_piece(n), ACT.Copy, scale=WSCALE).then_inc(sw_high, 1)

        def piece_low(dve, n):
            dve.wait_ge(sw_high, n + 1)
            nc.vector.scalar_tensor_tensor(piece(n)[1], raw_piece(n), WSCALE, piece(n)[0], ALU.mult, ALU.subtract).then_inc(sw_low, 1)

        def load_xT(eng, g):
            eng.dma_start(xT[g % 2].rearrange("p a b c -> p (a b c)"), xT_dram[g]).then_inc(xT_loaded[g % 2], 16)

        with ExitStack() as inner:
            views = iter(range(4 * 8))
            W_ = TILES * NE

            def grid():
                k = next(views)
                return bytes_of(k // 8)[:, (k % 8) * W_:(k % 8 + 1) * W_].rearrange("p (t e) -> p t e", e=NE)

            def col(name, n=TILES, dt=F32):
                return inner.enter_context(nc.sbuf_tensor(name, [P, n], dt))

            zeros = bytes_of(10)[:, 0:C]
            sw_scaled = sem("sw_scaled")
            const_loaded, zero_set, zeros_stored = sem("const_loaded"), sem("zero_set"), sem("zeros_stored")
            consts = col("consts", constants.shape[1])
            bias_row = col("bias_row", NE)
            score, biased, first, second, rest, both = grid(), grid(), grid(), grid(), grid(), grid()
            cand, within, total, upto, slot, work = grid(), grid(), grid(), grid(), grid(), grid()
            m1, m2, i1, i2 = col("m1"), col("m2"), col("i1"), col("i2")
            s1, s2, den, safe, fine = col("s1"), col("s2"), col("den"), col("safe"), col("fine")
            g1, g2, sf = col("g1"), col("g2"), col("sf", TOPK * TILES)
            count, tiles_of, tiles_upto, base = col("count", NE), col("tiles_of", NE), col("tiles_upto", NE), col("base", NE)
            ones_col = col("ones_col", TILES)
            both16 = col("both16", W_, F16)
            below = inner.enter_context(nc.sbuf_tensor("below", [P, P], F16))
            all_ones = inner.enter_context(nc.sbuf_tensor("all_ones", [P, P], F16))
            many = bytes_of(3)[:, 0:SLOT_TILES * NE].rearrange("p (q e) -> p q e", e=NE)
            ef = col("ef", SLOT_TILES)
            token = col("token", TILES, mybir.dt.int32)
            pad_rows = inner.enter_context(nc.sbuf_tensor("pad_rows", [P, SLOT_TILES, 2], mybir.dt.int32))
            e_row = consts[:, 0:NE]
            steps_row = consts[:, NE:NE + TILES]
            q_row = consts[:, NE + TILES:NE + TILES + SLOT_TILES]
            sig, chain, made2, pos_ready = sem("sig"), sem("chain"), sem("made2"), sem("pos_ready")
            pads_done, both_done = sem("pads_done"), sem("both_done")

            def over_tiles(row):
                return row.unsqueeze(1).broadcast_to([P, TILES, NE])

            def over_experts(c):
                return c.unsqueeze(2).broadcast_to([P, TILES, NE])

            with nc.Block() as block:
                @block.scalar
                def _(act):
                    nc.scalar.activation(score, logits[:], ACT.Sigmoid).then_inc(sig, 1)
                    for n in range(4):
                        piece_high(act, n)

                @block.sync
                def _(sp):
                    sp.dma_start(consts[:], constants.broadcast_to([P, constants.shape[1]])).then_inc(const_loaded, 16)
                    sp.dma_start(bias_row[:], r_bias.rearrange("(a n) -> a n", a=1).broadcast_to([P, NE])).then_inc(const_loaded, 16)
                    load_piece(sp, 0)
                    sp.wait_ge(zero_set, 1)
                    sp.dma_start(xn_dram[N:N + P], zeros).then_inc(zeros_stored, 16)
                    sp.wait_ge(made2, 5)
                    sp.dma_start(slot_dram.rearrange("(q p) c -> p q c", p=P), pad_rows[:]).then_inc(pads_done, 16)
                    for n in range(1, 4):
                        load_piece(sp, n)
                    load_xT(sp, 0)
                    for n in range(4, 6):
                        load_piece(sp, n)
                    sp.dma_start(x_tiles, x2_v[0]).then_inc(x_loaded, 16)
                    load_xT(sp, 1)
                    sp.wait_ge(zeros_stored, 16)
                    sp.wait_ge(pads_done, 16)

                @block.gpsimd
                def _(pool):
                    nc.gpsimd.memset(zeros, 0.0).then_inc(zero_set, 1)
                    nc.gpsimd.memset(below[:], 1.0).then_inc(made2, 1)
                    nc.gpsimd.memset(all_ones[:], 1.0).then_inc(made2, 1)
                    nc.gpsimd.memset(pad_rows[:, :, 1], 0).then_inc(made2, 1)
                    nc.gpsimd.iota(pad_rows[:, :, 0], pattern=[[0, SLOT_TILES]], base=N, channel_multiplier=1).then_inc(made2, 1)
                    nc.gpsimd.iota(token[:], pattern=[[P, TILES]], base=0, channel_multiplier=1).then_inc(made2, 1)
                    pool.wait_ge(made2, 5)
                    nc.gpsimd.affine_select(out=below[:], in_=below[:], compare_op=ALU.is_gt, fill=0.0, base=0,
                                            pattern=[[1, P]], channel_multiplier=-1).then_inc(made2, 1)

                    def split_shared(n):
                        hi, lo = piece(n)
                        pool.wait_ge(sw_high, n + 1)
                        src = raw_piece(n)
                        nc.gpsimd.tensor_scalar(src, src, WSCALE, 0.0, ALU.mult, ALU.add).then_inc(sw_scaled, 1)
                        pool.wait_ge(sw_scaled, POOL_PIECES.index(n) + 1)
                        nc.gpsimd.tensor_tensor(lo, src, hi, ALU.subtract).then_inc(sw_low, 1)

                    for n in POOL_PIECES:
                        split_shared(n)

                @block.tensor
                def _(pe):
                    pe.wait_ge(both_done, 1)
                    pe.wait_ge(made2, 6)
                    nc.tensor.matmul(bank[0][:, 0:W_], below[:], both16[:], start=True, stop=True).then_inc(pos_ready, 1)
                    nc.tensor.matmul(bank[1][:, 0:W_], all_ones[:], both16[:], start=True, stop=True).then_inc(pos_ready, 1)

                @block.vector
                def _(dve):
                    steps = [0]

                    def then(ins):
                        steps[0] += 1
                        ins.then_inc(chain, 1)
                        dve.wait_ge(chain, steps[0])

                    V = nc.vector
                    dve.wait_ge(const_loaded, 32)
                    dve.wait_ge(sig, 1)
                    then(V.tensor_tensor(biased, score, over_tiles(bias_row[:]), ALU.add))

                    def best(src, top, index, mask):
                        then(V.tensor_reduce(top, src, AX_X, ALU.max))
                        then(V.tensor_tensor(cand, src, over_experts(top), ALU.is_lt))
                        then(V.scalar_tensor_tensor(cand, cand, float(NE), over_tiles(e_row), ALU.mult, ALU.add))
                        then(V.tensor_reduce(index, cand, AX_X, ALU.min))
                        then(V.tensor_tensor(mask, over_tiles(e_row), over_experts(index), ALU.is_equal))

                    best(biased, m1[:], i1[:], first)
                    then(V.scalar_tensor_tensor(rest, first, -1e30, biased, ALU.mult, ALU.add))
                    best(rest, m2[:], i2[:], second)
                    then(V.tensor_tensor(both, first, second, ALU.add))
                    V.tensor_copy(both16[:], both.rearrange("p t e -> p (t e)")).then_inc(both_done, 1)
                    for mask, s in ((first, s1), (second, s2)):
                        then(V.tensor_tensor(work, mask, score, ALU.mult))
                        then(V.tensor_reduce(s[:], work, AX_X, ALU.add))
                    then(V.tensor_tensor(den[:], s1[:], s2[:], ALU.add))
                    then(V.tensor_scalar(safe[:], den[:], 1e-9, None, ALU.add))
                    then(V.reciprocal(safe[:], safe[:]))
                    then(V.tensor_scalar(fine[:], den[:], 1e-9, None, ALU.is_gt))
                    dve.wait_ge(made2, 5)
                    for s, g, k in ((s1, g1, 0), (s2, g2, 1)):
                        then(V.tensor_tensor(g[:], s[:], safe[:], ALU.mult))
                        then(V.tensor_tensor(g[:], g[:], fine[:], ALU.mult))
                        then(V.tensor_scalar(s[:], fine[:], -0.5, 0.5, ALU.mult, ALU.add))
                        then(V.tensor_tensor(slot_rows[:, k, :, 1], g[:], s[:], ALU.add))
                        then(V.tensor_copy(slot_rows[:, k, :, 0].bitcast(mybir.dt.int32), token[:]))
                    dve.wait_ge(pos_ready, 2)
                    then(V.tensor_copy(total, bank[1][:, 0:W_].rearrange("p (t e) -> p t e", e=NE)))
                    then(V.memset(ones_col[:], 1.0))
                    for e in range(NE):
                        then(V.tensor_tensor_scan(upto[:, :, e], ones_col[:], total[:, :, e], 0.0, ALU.mult, ALU.add))
                    then(V.tensor_copy(count[:], upto[:, TILES - 1]))
                    cmp = work.rearrange("p t e -> p (t e)").rearrange("p (e k) -> p e k", e=NE)
                    then(V.tensor_tensor(cmp, count[:].unsqueeze(2).broadcast_to([P, NE, TILES]),
                                         steps_row.unsqueeze(1).broadcast_to([P, NE, TILES]), ALU.is_gt))
                    then(V.tensor_reduce(tiles_of[:], cmp, AX_X, ALU.add))
                    then(V.tensor_tensor_scan(tiles_upto[:], ones_col[:, 0:NE], tiles_of[:], 0.0, ALU.mult, ALU.add))
                    then(V.tensor_tensor(base[:], tiles_upto[:], tiles_of[:], ALU.subtract))
                    then(V.tensor_scalar(base[:], base[:], float(P), None, ALU.mult))
                    then(V.tensor_tensor(slot, upto, total, ALU.subtract))
                    then(V.tensor_tensor(slot, slot, over_tiles(base[:]), ALU.add))
                    then(V.tensor_tensor(slot, slot, bank[0][:, 0:W_].rearrange("p (t e) -> p t e", e=NE), ALU.add))
                    for k, mask in enumerate((first, second)):
                        then(V.tensor_tensor(work, mask, slot, ALU.mult))
                        then(V.tensor_reduce(sf[:, k * TILES:(k + 1) * TILES], work, AX_X, ALU.add))
                    then(V.tensor_copy(slots[:, :, :, 0], sf[:].rearrange("p (k t) -> p k t", k=TOPK)))
                    then(V.tensor_tensor(many, tiles_upto[:].unsqueeze(1).broadcast_to([P, SLOT_TILES, NE]),
                                         q_row.unsqueeze(2).broadcast_to([P, SLOT_TILES, NE]), ALU.is_le))
                    then(V.tensor_reduce(ef[:], many, AX_X, ALU.add))
                    then(V.tensor_scalar(ef[:], ef[:], float(NE - 1), None, ALU.min))
                    then(V.tensor_copy(tile_expert[:], ef[:]))
                    for n in range(len(POOL_PIECES), 4):
                        piece_low(dve, n)

        raw_loaded = [sem(f"raw_loaded{n}") for n in range(3)]
        rows = sb("rows", [P, RING, 2], mybir.dt.int32)
        rows_loaded = [sem(f"rows_loaded{k}") for k in range(RING)]
        gathered = [sem(f"gathered{k}") for k in range(RING)]
        gT = sb("gT", [P, 2, FT, T], F16)
        with ExitStack() as scope:
            gate = scope.enter_context(nc.sbuf_tensor("gate", [P, 2, T], F32))
            x_stored = sem("s_x_stored")
            h_ready, silu_done, g_done, g_high, g_low = sem("h_ready"), sem("silu_done"), sem("g_done"), sem("g_high"), sem("g_low")
            o_ready, o_done = sem("s_o_ready"), sem("s_o_done")
            rows_placed = sem("rows_placed")
            mat_loaded, mat_step, mat_done = sem("mat_loaded"), sem("mat_step"), sem("mat_done")
            early = list(range(X_SLOT)) + [XT_SLOT]
            late = [RAW_SLOT, XT_SLOT + 1]
            raw = late_raw(w1, w3)
            raw_high, raw_low = sem("raw_high"), sem("raw_low")

            with nc.Block() as block:
                @block.sync
                def _(sp):
                    for g in range(B):
                        if g + 2 < B:
                            sp.wait_ge(h_ready, (g + 1) * 2 * FT)
                            load_xT(sp, g + 2)
                        if g == B - 1:
                            sp.wait_ge(h_ready, B * 2 * FT)
                            sp.wait_ge(rows_placed, 16 * TOPK * TILES)
                            for k in range(RING):
                                sp.dma_start(rows[:, k], rows_of(slot_dram, k)).then_inc(rows_loaded[k], 16)
                            for n, m in enumerate(late + [X_SLOT]):
                                sp.dma_start(raw[n].rearrange("p (a c) -> p a c", a=KT), matrix(m).rearrange("(a p) c -> p a c", p=P)
                                             ).then_inc(raw_loaded[n], 16)
                        sp.wait_ge(o_done, g * TT + TT)
                        sp.dma_start(out_v[g], x_tiles).then_inc(x_stored, 16)
                        if g + 1 < B:
                            sp.wait_ge(x_stored, g * 16 + 16)
                            sp.dma_start(x_tiles, x2_v[g + 1]).then_inc(x_loaded, 16)
                    sp.wait_ge(x_stored, 16 * B)

                @block.gpsimd
                def _(pool):
                    for k in range(TOPK):
                        for t in range(TILES):
                            nc.gpsimd.indirect_dma_start(
                                slot_dram, bass.IndirectOffsetOnAxis(ap=slots[:, k, t], axis=0),
                                slot_rows[:, k, t].bitcast(mybir.dt.int32), None).then_inc(rows_placed, 16)
                    for n, m in enumerate(early):
                        if m == 8:
                            pool.wait_ge(sw_low, 6)
                        if m >= XT_SLOT:
                            pool.wait_ge(h_ready, (B - 1) * 2 * FT)
                        if n > 0:
                            pool.wait_ge(mat_done, n)
                        pool.dma_start(raw_tile, matrix(m).rearrange("(a p) c -> p a c", p=P)).then_inc(mat_loaded, 16)
                        pool.wait_ge(mat_loaded, 16 * n + 16)
                        nc.gpsimd.tensor_scalar(raw_tile, raw_tile, WSCALE, 0.0, ALU.mult, ALU.add).then_inc(mat_step, 1)
                        pool.wait_ge(mat_step, 2 * n + 1)
                        nc.gpsimd.tensor_copy(experts[:, m, 0], raw_tile).then_inc(mat_step, 1)
                        pool.wait_ge(mat_step, 2 * n + 2)
                        nc.gpsimd.tensor_tensor(experts[:, m, 1], raw_tile, experts[:, m, 0], ALU.subtract).then_inc(mat_done, 1)
                    pool.wait_ge(h_ready, B * 2 * FT)
                    for k, slot in enumerate(early_slots(w3)):
                        pool.wait_ge(rows_loaded[k], 16)
                        gather_tile(nc, slot, xn_dram, rows[:, k], gathered[k])

                @block.scalar
                def _(act):
                    def high(i, f):
                        act.wait_ge(g_done, i + 1)
                        nc.scalar.activation(gT[:, 0, f], gate[:, f % 2], ACT.Copy).then_inc(g_high, 1)

                    def group(g):
                        for f in range(FT):
                            i = g * FT + f
                            act.wait_ge(h_ready, i * 2 + 1)
                            wait(act, g_low, i - 1)
                            nc.scalar.activation(gate[:, f % 2], bank[f % 2][:], ACT.Silu, scale=1.0 / WSCALE).then_inc(silu_done, 1)
                            if f == 0:
                                wait(act, o_ready, g * TT)
                            else:
                                high(i - 1, f - 1)
                            if isinstance(g, int) and g == 0 and f in W2_STEPS:
                                piece_high(act, 4 + W2_STEPS.index(f))
                        high(g * FT + FT - 1, FT - 1)

                    group(0)
                    with act.Fori(1, B) as g:
                        group(g)
                    act.wait_ge(mat_done, len(early))
                    for n, m in enumerate(late):
                        act.wait_ge(raw_loaded[n], 16)
                        nc.scalar.activation(experts[:, m, 0], raw[n].rearrange("p (a c) -> p a c", a=KT), ACT.Copy,
                                             scale=WSCALE).then_inc(raw_high, 1)

                @block.vector
                def _(dve):
                    def low(i, f):
                        dve.wait_ge(g_high, i + 1)
                        nc.vector.tensor_tensor(gT[:, 1, f], gate[:, f % 2], gT[:, 0, f], ALU.subtract).then_inc(g_low, 1)

                    def group(g, last=False):
                        for f in range(FT):
                            i = g * FT + f
                            dve.wait_ge(silu_done, i + 1)
                            dve.wait_ge(h_ready, i * 2 + 2)
                            nc.vector.scalar_tensor_tensor(gate[:, f % 2], bank[2 + f % 2][:], 1.0 / WSCALE, gate[:, f % 2],
                                                           ALU.mult, ALU.mult).then_inc(g_done, 1)
                            if f > 0:
                                low(i - 1, f - 1)
                            if isinstance(g, int) and g == 0 and f in W2_STEPS:
                                piece_low(dve, 4 + W2_STEPS.index(f))
                        low(g * FT + FT - 1, FT - 1)
                        if last:
                            for n, m in enumerate(late):
                                dve.wait_ge(raw_high, n + 1)
                                nc.vector.scalar_tensor_tensor(experts[:, m, 1], raw[n].rearrange("p (a c) -> p a c", a=KT), WSCALE,
                                                               experts[:, m, 0], ALU.mult, ALU.subtract).then_inc(raw_low, 1)
                        dve.wait_ge(x_loaded, g * 16 + 16)
                        for t in range(TT):
                            dve.wait_ge(o_ready, g * TT + t + 1)
                            nc.vector.scalar_tensor_tensor(x_tiles[:, t], bank[4 + t][:], 1.0 / WSCALE, x_tiles[:, t],
                                                           ALU.mult, ALU.add).then_inc(o_done, 1)

                    group(0)
                    with dve.Fori(1, B - 1) as g:
                        group(g)
                    group(B - 1, last=True)

                @block.tensor
                def _(pe):
                    def group(i, k):
                        g = i * 2 + k
                        pe.wait_ge(xT_loaded[k], i * 16 + 16)

                        def xt(h, c):
                            return xT[k][:, h, c]

                        def hidden(out_bank, w, f):
                            fs = slice(f * P, f * P + P)
                            for c in range(KT):
                                nc.tensor.matmul(out_bank, w[:, 0, c, fs], xt(0, c), start=(c == 0), stop=False)
                                nc.tensor.matmul(out_bank, w[:, 0, c, fs], xt(1, c), start=False, stop=False)
                                last = nc.tensor.matmul(out_bank, w[:, 1, c, fs], xt(0, c), start=False, stop=(c == KT - 1))
                            last.then_inc(h_ready, 1)

                        for f in range(FT):
                            n = g * FT + f
                            wait(pe, silu_done, n - 1)
                            hidden(bank[f % 2][:], w1, f)
                            wait(pe, g_done, n - 1)
                            hidden(bank[2 + f % 2][:], w3, f)
                        if isinstance(g, int) and g == 0:
                            pe.wait_ge(sw_low, 6)
                        wait(pe, o_done, g * TT)
                        for f in range(FT):
                            pe.wait_ge(g_low, g * FT + f + 1)
                            for t in range(TT):
                                ts = slice(t * P, t * P + P)
                                nc.tensor.matmul(bank[4 + t][:], gT[:, 0, f, ts], w2[:, 0, f], start=(f == 0), stop=False)
                                nc.tensor.matmul(bank[4 + t][:], gT[:, 0, f, ts], w2[:, 1, f], start=False, stop=False)
                                last = nc.tensor.matmul(bank[4 + t][:], gT[:, 1, f, ts], w2[:, 0, f], start=False, stop=(f == FT - 1))
                                if f == FT - 1:
                                    last.then_inc(o_ready, 1)

                    group(0, 0)
                    group(0, 1)
                    with pe.Fori(1, B // 2) as i:
                        group(i, 0)
                        group(i, 1)

        build_routed(nc, sem, keep, raw_loaded, rows, rows_loaded, gathered, experts, tile_expert, bank, matrix, out, xn_dram, slot_dram, w1, w3, w2, gT)


AHEAD = 6
RING = 8


def late_raw(w1, w3):
    f1, f3 = (t[:].rearrange("p a b c -> p (a b c)").bitcast(F32) for t in (w1, w3))
    return [f1[:, 0:2048], f1[:, 2048:4096], f3[:, 0:2048]]


def early_slots(w3):
    f3 = w3[:].rearrange("p a b c -> p (a b c)").bitcast(F32)
    return [f3[:, (6 + k) * C:(7 + k) * C] for k in range(2)]


def rows_of(slot_dram, q):
    slot_v = slot_dram.rearrange("(q p) c -> q p c", p=P)
    return slot_v[q] if isinstance(q, int) else slot_v[bass.ds(q, 1)].rearrange("o p c -> (o p) c")


def gather_tile(nc, slot, xn_dram, rows_k, gathered_k):
    nc.gpsimd.indirect_dma_start(slot, None, xn_dram,
                                 bass.IndirectOffsetOnAxis(ap=rows_k[:, 0:1].bitcast(mybir.dt.uint32), axis=0)).then_inc(gathered_k, 16)


def build_routed(nc, sem, keep, raw_loaded, rows, rows_loaded, gathered, experts, tile_expert, bank, matrix, out, xn_dram, slot_dram, w1, w3, w2, gT):
    with ExitStack() as scope:
        f2, fg = (t[:].rearrange("p a b c -> p (a b c)").bitcast(F32) for t in (w2, gT))
        raw_x = late_raw(w1, w3)[2].rearrange("p (a c) -> p a c", a=KT)
        xg = early_slots(w3) + [fg[:, k * C:k * C + C] for k in range(len(early_slots(w3)), RING)]
        h_sb = [f2[:, k * C:k * C + C] for k in range(2)]
        y_sb = [f2[:, (2 + k) * C:(3 + k) * C] for k in range(2)]
        h16 = w2[:].rearrange("p a b c -> p (a b c)")
        xT = [h16[:, 4096 + k * 1024:4096 + k * 1024 + 1024].rearrange("p (h c t) -> p h c t", h=2, c=KT) for k in range(4)]
        h16b = w3[:].rearrange("p a b c -> p (a b c)")
        hT = [h16b[:, 4096 + k * 1024:4096 + k * 1024 + 1024].rearrange("p (h c t) -> p h c t", h=2, c=KT) for k in range(2)]
        ident = scope.enter_context(nc.sbuf_tensor("r_ident", [P, P], F32))
        made, x_slot_high, x_slot_low = sem("r_made"), sem("x_slot_high"), sem("x_slot_low")
        added = sem("added")
        xT_ready, xT_high, xT_low = sem("r_xT_ready"), sem("r_xT_high"), sem("r_xT_low")
        h_ready, gelu_done = sem("r_h_ready"), sem("gelu_done")
        hT_ready, hT_high, hT_low = sem("hT_ready"), sem("hT_high"), sem("hT_low")
        y_ready, y_done = sem("r_y_ready"), sem("r_y_done")
        pool_waits = sem("r_pool_waits")
        Q = SLOT_TILES

        def turns_all(eng, body):
            for k in range(8):
                body(0, k)
            with eng.Fori(1, Q // 8 - 1) as i:
                for k in range(8):
                    body(i, k)
            for k in range(8):
                body(Q // 8 - 1, k)

        with nc.Block() as block:
            @block.sync
            def _(sp):
                def load_rows(i, k):
                    sp.wait_ge(added, i * 128 + k * 16 - 7 * 16)
                    sp.dma_start(rows[:, k], rows_of(slot_dram, i * 8 + k)).then_inc(rows_loaded[k], 16)

                with sp.Fori(1, Q // 8) as i:
                    for k in range(8):
                        load_rows(i, k)

            @block.gpsimd
            def _(pool):
                nc.gpsimd.memset(ident[:], 0.0).then_inc(made, 1)
                pool.wait_ge(made, 1)
                nc.gpsimd.affine_select(out=ident[:], in_=ident[:], compare_op=ALU.not_equal, fill=1.0, base=0,
                                        pattern=[[-1, P]], channel_multiplier=1).then_inc(made, 1)

                def gather(i, k):
                    i, k = i + k // 8, k % 8
                    q = i * 8 + k
                    wait(pool, xT_ready, q - RING + 1)
                    wait_apart(pool, rows_loaded[k], i * 16 + 16, pool_waits)
                    gather_tile(nc, xg[k], xn_dram, rows[:, k], gathered[k])

                def add(i, k):
                    q = i * 8 + k
                    wait(pool, added, q * 16)
                    wait_apart(pool, y_done, q + 1, pool_waits)
                    nc.gpsimd.indirect_dma_start(out, bass.IndirectOffsetOnAxis(ap=rows[:, k, 0:1].bitcast(mybir.dt.uint32), axis=0),
                                                 y_sb[k % 2], None, compute_op=ALU.add).then_inc(added, 16)

                for k in range(2, AHEAD):
                    gather(0, k)

                def body(i, k):
                    if not (isinstance(i, int) and i * 8 + k + AHEAD >= Q):
                        gather(i, k + AHEAD)
                    add(i, k)
                turns_all(pool, body)
                pool.wait_ge(added, 16 * Q)

            @block.scalar
            def _(act):
                act.wait_ge(raw_loaded[2], 16)
                nc.scalar.activation(experts[:, X_SLOT, 0], raw_x, ACT.Copy, scale=WSCALE).then_inc(x_slot_high, 1)

                def x_high(i, k):
                    i, k = i + k // 8, k % 8
                    q = i * 8 + k
                    act.wait_ge(xT_ready, q + 1)
                    wait(act, h_ready, q - 3)
                    nc.scalar.activation(xT[k % 4][:, 0], bank[k % 2][:].rearrange("p (c t) -> p c t", c=KT), ACT.Copy).then_inc(xT_high, 1)

                def h_high(i, k):
                    i, k = i + k // 8, k % 8
                    q = i * 8 + k
                    act.wait_ge(hT_ready, q + 1)
                    wait(act, y_ready, q - 1)
                    nc.scalar.activation(hT[k % 2][:, 0], bank[4 + k % 2][:].rearrange("p (c t) -> p c t", c=KT), ACT.Copy).then_inc(hT_high, 1)

                def gelu(i, k):
                    i, k = i + k // 8, k % 8
                    q = i * 8 + k
                    act.wait_ge(h_ready, q + 1)
                    wait(act, hT_ready, q - 1)
                    nc.scalar.activation(h_sb[k % 2], bank[2 + k % 2][:], ACT.Gelu, scale=1.0 / WSCALE).then_inc(gelu_done, 1)

                x_high(0, 0)
                x_high(0, 1)

                def ordered(i, k):
                    if not (isinstance(i, int) and i * 8 + k == 0):
                        h_high(i, k - 1)
                    if not (isinstance(i, int) and i * 8 + k + 2 >= Q):
                        x_high(i, k + 2)
                    gelu(i, k)
                turns_all(act, ordered)
                h_high(0, Q - 1)

            @block.vector
            def _(dve):
                dve.wait_ge(x_slot_high, 1)
                nc.vector.scalar_tensor_tensor(experts[:, X_SLOT, 1], raw_x, WSCALE, experts[:, X_SLOT, 0],
                                               ALU.mult, ALU.subtract).then_inc(x_slot_low, 1)

                def x_low(i, k):
                    i, k = i + k // 8, k % 8
                    q = i * 8 + k
                    dve.wait_ge(xT_high, q + 1)
                    nc.vector.tensor_tensor(xT[k % 4][:, 1], bank[k % 2][:].rearrange("p (c t) -> p c t", c=KT), xT[k % 4][:, 0],
                                            ALU.subtract).then_inc(xT_low, 1)

                def h_low(i, k):
                    i, k = i + k // 8, k % 8
                    q = i * 8 + k
                    dve.wait_ge(hT_high, q + 1)
                    nc.vector.tensor_tensor(hT[k % 2][:, 1], bank[4 + k % 2][:].rearrange("p (c t) -> p c t", c=KT), hT[k % 2][:, 0],
                                            ALU.subtract).then_inc(hT_low, 1)

                def y_out(i, k):
                    i, k = i + k // 8, k % 8
                    q = i * 8 + k
                    dve.wait_ge(y_ready, q + 1)
                    wait(dve, added, q * 16 - 16)
                    nc.vector.tensor_scalar(y_sb[k % 2], bank[6 + k % 2][:], rows[:, k, 1:2].bitcast(F32), 1.0 / WSCALE,
                                            ALU.mult, ALU.mult).then_inc(y_done, 1)

                x_low(0, 0)
                x_low(0, 1)

                def ordered(i, k):
                    if not (isinstance(i, int) and i * 8 + k == 0):
                        h_low(i, k - 1)
                    if not (isinstance(i, int) and i * 8 + k + 2 >= Q):
                        x_low(i, k + 2)
                    if not (isinstance(i, int) and i * 8 + k < 2):
                        y_out(i, k - 2)
                turns_all(dve, ordered)
                y_out(0, Q - 2)
                h_low(0, Q - 1)
                y_out(0, Q - 1)

            @block.tensor
            def _(pe):
                def x_transposes(i, k):
                    i, k = i + k // 8, k % 8
                    q = i * 8 + k
                    pe.wait_ge(gathered[k], i * 16 + 16)
                    wait(pe, xT_low, q - 1)
                    for c in range(KT):
                        last = nc.tensor.transpose(bank[k % 2][:, c * P:c * P + P], xg[k][:, c * P:c * P + P], ident[:])
                    last.then_inc(xT_ready, 1)

                def h_transposes(i, k):
                    i, k = i + k // 8, k % 8
                    q = i * 8 + k
                    pe.wait_ge(gelu_done, q + 1)
                    wait(pe, hT_low, q - 1)
                    for c in range(KT):
                        last = nc.tensor.transpose(bank[4 + k % 2][:, c * P:c * P + P], h_sb[k % 2][:, c * P:c * P + P], ident[:])
                    last.then_inc(hT_ready, 1)

                def expert_of(q):
                    return pe.value_load(tile_expert[0:1, bass.ds(q, 1)], min_val=0, max_val=NE - 1)

                def expert_product(e, bank_, lhs, second):
                    def w(h, c):
                        return experts[:, bass.ds(e * 2 + second, 1), h, c].rearrange("p o n -> p (o n)")
                    for c in range(KT):
                        nc.tensor.matmul(bank_[:], lhs[:, 0, c], w(0, c), start=(c == 0), stop=False)
                        nc.tensor.matmul(bank_[:], lhs[:, 0, c], w(1, c), start=False, stop=False)
                        last = nc.tensor.matmul(bank_[:], lhs[:, 1, c], w(0, c), start=False, stop=(c == KT - 1))
                    return last

                def hidden(i, k):
                    i, k = i + k // 8, k % 8
                    q = i * 8 + k
                    e = expert_of(q)
                    wait(pe, gelu_done, q - 1)
                    pe.wait_ge(xT_low, q + 1)
                    expert_product(e, bank[2 + k % 2], xT[k % 4], 0).then_inc(h_ready, 1)

                def result(i, k):
                    i, k = i + k // 8, k % 8
                    q = i * 8 + k
                    e = expert_of(q)
                    wait(pe, y_done, q - 1)
                    pe.wait_ge(hT_low, q + 1)
                    expert_product(e, bank[6 + k % 2], hT[k % 2], 1).then_inc(y_ready, 1)

                pe.wait_ge(made, 2)
                x_transposes(0, 0)
                x_transposes(0, 1)
                pe.wait_ge(x_slot_low, 1)

                def ordered(i, k):
                    hidden(i, k)
                    if not (isinstance(i, int) and i * 8 + k == 0):
                        h_transposes(i, k - 1)
                    if not (isinstance(i, int) and i * 8 + k + 2 >= Q):
                        x_transposes(i, k + 2)
                    if not (isinstance(i, int) and i * 8 + k < 2):
                        result(i, k - 2)
                turns_all(pe, ordered)
                result(0, Q - 2)
                h_transposes(0, Q - 1)
                result(0, Q - 1)


def shape_constants():
    import numpy as np
    return np.concatenate([np.arange(NE), P * np.arange(TILES), np.arange(SLOT_TILES)]).astype(np.float32)[None]


def build_program(nc, out, in_x, in_ctx, in_basisT, in_core, in_coreT, in_head_res, in_wvT, in_bv, in_woT, in_bo, in_xwqT,
                  in_xbq, in_xwkT, in_xbk, in_xwvT, in_xbv, in_xwoT, in_xbo, in_rwT, in_r_bias, in_sw1, in_sw3, in_sw2,
                  in_ew1, in_ew2, in_constants):
    with ExitStack() as ctx:
        def sem(name):
            return ctx.enter_context(nc.semaphore(name))

        x2 = nc.dram_tensor("x2", (N, C), F32, kind="Internal").ap()
        xn = nc.dram_tensor("xn3", (N + P, C), F32, kind="Internal").ap()
        xT = nc.dram_tensor("xn3_transposed", (B, P, 2 * KT * T), F16, kind="Internal").ap()
        logits = ctx.enter_context(nc.sbuf_tensor("logits", [P, TILES, NE], F32))
        slots = nc.dram_tensor("slot_table", (SLOT_TILES * P, 2), mybir.dt.int32, kind="Internal").ap()
        build_attention(nc, sem, in_x, in_ctx, (in_basisT, in_core, in_coreT, in_head_res, in_wvT, in_bv, in_woT, in_bo,
                                                in_xwqT, in_xbq, in_xwkT, in_xbk, in_xwvT, in_xbv, in_xwoT, in_xbo),
                        in_rwT, logits, x2, xn, xT)
        build_ffn(nc, sem, logits, x2, out, in_r_bias, in_sw1, in_sw3, in_sw2, in_ew1, in_ew2, in_constants, xn, xT, slots)


def kernel(**inputs):
    import numpy as _np
    import concourse.bacc as _bacc
    from concourse import mybir as _mybir
    from concourse.bass_utils import run_bass_kernel_spmd as _run

    nc = _bacc.Bacc("TRN2", target_bir_lowering=False, num_devices=1)
    i = {k: _np.asarray(v) for k, v in inputs.items()}
    columns = lambda v: v.reshape(NG, P).T
    arrays = {
        "x": i["x"], "ctx": i["ctx_1024"], "basisT": i["L0_attn_basis_w"].T, "core": i["L0_attn_core"],
        "coreT": i["L0_attn_core"].T, "head_res": i["L0_attn_head_residual"], "wvT": i["L0_attn_v_w"].T,
        "bv": i["L0_attn_v_b"], "woT": i["L0_attn_o_w"].T, "bo": i["L0_attn_o_b"], "xwqT": i["L0_xattn_Wq"].T,
        "xbq": columns(i["L0_xattn_bq"]), "xwkT": i["L0_xattn_Wk"].T, "xbk": columns(i["L0_xattn_bk"]),
        "xwvT": i["L0_xattn_Wv"].T, "xbv": i["L0_xattn_bv"], "xwoT": i["L0_xattn_Wo"].T, "xbo": i["L0_xattn_bo"],
        "rwT": i["L0_ffn_router_w"].T, "r_bias": i["L0_ffn_router_bias"], "sw1": i["L0_ffn_sw1"],
        "sw3": i["L0_ffn_sw3"], "sw2": i["L0_ffn_sw2"], "ew1": i["L0_ffn_ew1"], "ew2": i["L0_ffn_ew2"],
        "constants": shape_constants(),
    }
    arrays = {"in_" + k: _np.ascontiguousarray(v) for k, v in arrays.items()}
    args = {k: nc.dram_tensor(k, v.shape, _mybir.dt.from_np(v.dtype), kind="ExternalInput").ap() for k, v in arrays.items()}
    out = nc.dram_tensor("out_0", (N + P, C), F32, kind="ExternalOutput").ap()
    build_program(nc, out, **args)
    r = _run(nc, [arrays], core_ids=[0])
    return r.results[0]["out_0"][:N].reshape(B, T, C)
```
